# Optimizing a Trainium2 kernel written in Bass

```python
import numpy as np
import jax
import jax.numpy as jnp

def _softmax(x, axis=-1):
    return jax.nn.softmax(x, axis=axis)

def _gelu(x):
    return jax.nn.gelu(x, approximate=True)

def _silu(x):
    return jax.nn.silu(x)

def _sigmoid(x):
    return jax.nn.sigmoid(x)

def _layernorm(x, axis=-1, eps=1e-05):
    m = jnp.mean(x, axis=axis, keepdims=True)
    v = jnp.var(x, axis=axis, keepdims=True)
    return (x - m) / jnp.sqrt(v + eps)

def _scatter_add(tgt, idx, src, axis=0):
    return tgt.at[idx].add(src)

def _segment_sum(src, seg, n):
    return jax.ops.segment_sum(src, seg, n)
kernel_name = 'mk_vit_tower_d1_tok_img768_r4_4915f4'

def setup_inputs(seed: int=0):
    np.random.seed(seed)
    _w = jnp.asarray

    def _rec_inputs():
        import jax
        import jax.numpy as jnp
        _rk = jax.random.key(seed)
        x = -0.000596345 + 1.00056 * jax.random.normal(jax.random.fold_in(_rk, 1), (4, 3, 64, 64), jnp.float32)
        return x
    x = _rec_inputs()

    def _L0_tok_setup():
        import jax, jax.numpy as jnp
        import numpy as np
        B = 16
        IMG = 64
        CH = 3
        EMBED = 64
        GP = 16
        PRE = [1, 2, 4]
        N_LEVELS = 3
        FUSED = EMBED * N_LEVELS

        def hilbert_flat_indices(n):
            t = np.arange(n * n, dtype=np.int64)
            x = np.zeros(n * n, dtype=np.int64)
            y = np.zeros(n * n, dtype=np.int64)
            s = 1
            while s < n:
                rx = 1 & t // 2
                ry = 1 & (t ^ rx)
                swap = ry == 0
                flip = swap & (rx == 1)
                x = np.where(flip, s - 1 - x, x)
                y = np.where(flip, s - 1 - y, y)
                x2 = np.where(swap, y, x)
                y2 = np.where(swap, x, y)
                x, y = (x2, y2)
                x = x + s * rx
                y = y + s * ry
                t = t // 4
                s *= 2
            return y * n + x

        def _level(x, idx, W, b, p, gp):
            Bsz, C, H, _ = x.shape
            h = H // p
            t = x.reshape(Bsz, C, h, p, h, p).transpose(0, 2, 4, 3, 5, 1).reshape(Bsz, h * h, p * p * C)
            t = t[:, idx]
            t = t.reshape(Bsz, h * h // gp, gp * p * p * C)
            return t @ W.T + b

        def _interp_linear(x, n_out):
            L = x.shape[1]
            pos = (jnp.arange(n_out, dtype=jnp.float32) + 0.5) * (L / n_out) - 0.5
            pos = jnp.clip(pos, 0.0, L - 1)
            i0 = jnp.floor(pos).astype(jnp.int32)
            i1 = jnp.minimum(i0 + 1, L - 1)
            w = (pos - i0).astype(x.dtype)
            return x[:, i0] * (1.0 - w)[None, :, None] + x[:, i1] * w[None, :, None]
        key = jax.random.key(seed)
        ks = jax.random.split(key, 9)
        inp = {'x': jax.random.normal(ks[0], (B, CH, IMG, IMG), jnp.float32)}
        for i, p in enumerate(PRE):
            din = CH * p * p * GP
            inp[f'W{i}'] = jax.random.normal(ks[1 + 2 * i], (EMBED, din), jnp.float32) * din ** (-0.5)
            inp[f'b{i}'] = jax.random.normal(ks[2 + 2 * i], (EMBED,), jnp.float32) * 0.02
        inp['Wf'] = jax.random.normal(ks[7], (FUSED, FUSED), jnp.float32) * FUSED ** (-0.5)
        inp['bf'] = jax.random.normal(ks[8], (FUSED,), jnp.float32) * 0.02
        for i, p in enumerate(PRE):
            inp[f'idx{i}'] = jnp.asarray(hilbert_flat_indices(IMG // p), jnp.int32)
        return inp
    _L0_tok_all = _L0_tok_setup()
    _L0_tok_in = {k: v for k, v in _L0_tok_all.items() if k in ('W0', 'b0', 'W1', 'b1', 'W2', 'b2', 'Wf', 'bf', 'idx0', 'idx1', 'idx2')}
    del _L0_tok_all

    def _L0_attn_setup():
        import jax, jax.numpy as jnp
        import numpy as np
        DIM = 192
        NUM_HEADS = 12
        DIM_HEAD = 64
        SCALE = 1.0 / DIM_HEAD ** 0.5
        key = jax.random.key(seed)
        k1, k2, k3 = jax.random.split(key, 3)
        x = jax.random.normal(k1, (8, 256, DIM), dtype=jnp.float32)
        W_qkv = jax.random.normal(k2, (3 * NUM_HEADS * DIM_HEAD, DIM), dtype=jnp.float32) * 0.02
        W_out = jax.random.normal(k3, (DIM, NUM_HEADS * DIM_HEAD), dtype=jnp.float32) * 0.02
        return {'x': x, 'W_qkv': W_qkv, 'W_out': W_out}
    _L0_attn_all = _L0_attn_setup()
    _L0_attn_in = {k: v for k, v in _L0_attn_all.items() if k in ('W_qkv', 'W_out')}
    del _L0_attn_all

    def _L0_ffn_setup():
        import math
        import jax, jax.numpy as jnp
        import numpy as np
        NUM_EXPERTS = 8
        TOP_K = 2
        CAPACITY_FACTOR = 1.25
        H = 192
        INNER = 768
        B, S = (2, 512)
        key = jax.random.key(seed)
        ks = jax.random.split(key, 9)
        scale = 0.02
        x = jax.random.normal(ks[0], (B, S, H), dtype=jnp.float32)
        Wr = jax.random.normal(ks[1], (H, NUM_EXPERTS), dtype=jnp.float32) * scale
        w1 = jax.random.normal(ks[2], (NUM_EXPERTS, H, INNER), dtype=jnp.float32) * scale
        w3 = jax.random.normal(ks[3], (NUM_EXPERTS, H, INNER), dtype=jnp.float32) * scale
        w2 = jax.random.normal(ks[4], (NUM_EXPERTS, INNER, H), dtype=jnp.float32) * scale
        s1 = jax.random.normal(ks[5], (H, INNER), dtype=jnp.float32) * scale
        s3 = jax.random.normal(ks[6], (H, INNER), dtype=jnp.float32) * scale
        s2 = jax.random.normal(ks[7], (INNER, H), dtype=jnp.float32) * scale
        return {'x': x, 'Wr': Wr, 'w1': w1, 'w3': w3, 'w2': w2, 's1': s1, 's3': s3, 's2': s2}
    _L0_ffn_all = _L0_ffn_setup()
    _L0_ffn_in = {k: v for k, v in _L0_ffn_all.items() if k in ('Wr', 'w1', 'w3', 'w2', 's1', 's3', 's2')}
    del _L0_ffn_all
    return {'x': x, 'L0_tok_W0': _L0_tok_in['W0'], 'L0_tok_b0': _L0_tok_in['b0'], 'L0_tok_W1': _L0_tok_in['W1'], 'L0_tok_b1': _L0_tok_in['b1'], 'L0_tok_W2': _L0_tok_in['W2'], 'L0_tok_b2': _L0_tok_in['b2'], 'L0_tok_Wf': _L0_tok_in['Wf'], 'L0_tok_bf': _L0_tok_in['bf'], 'L0_tok_idx0': _L0_tok_in['idx0'], 'L0_tok_idx1': _L0_tok_in['idx1'], 'L0_tok_idx2': _L0_tok_in['idx2'], 'L0_attn_W_qkv': _L0_attn_in['W_qkv'], 'L0_attn_W_out': _L0_attn_in['W_out'], 'L0_ffn_Wr': _L0_ffn_in['Wr'], 'L0_ffn_w1': _L0_ffn_in['w1'], 'L0_ffn_w3': _L0_ffn_in['w3'], 'L0_ffn_w2': _L0_ffn_in['w2'], 'L0_ffn_s1': _L0_ffn_in['s1'], 'L0_ffn_s3': _L0_ffn_in['s3'], 'L0_ffn_s2': _L0_ffn_in['s2']}

def reference(x, L0_tok_W0, L0_tok_b0, L0_tok_W1, L0_tok_b1, L0_tok_W2, L0_tok_b2, L0_tok_Wf, L0_tok_bf, L0_tok_idx0, L0_tok_idx1, L0_tok_idx2, L0_attn_W_qkv, L0_attn_W_out, L0_ffn_Wr, L0_ffn_w1, L0_ffn_w3, L0_ffn_w2, L0_ffn_s1, L0_ffn_s3, L0_ffn_s2):
    import jax
    import jax.numpy as jnp

    def _L0_tok_ref(x, W0, b0, W1, b1, W2, b2, Wf, bf, idx0, idx1, idx2):
        import jax, jax.numpy as jnp
        import numpy as np
        B = 16
        IMG = 64
        CH = 3
        EMBED = 64
        GP = 16
        PRE = [1, 2, 4]
        N_LEVELS = 3
        FUSED = EMBED * N_LEVELS

        def hilbert_flat_indices(n):
            t = np.arange(n * n, dtype=np.int64)
            x = np.zeros(n * n, dtype=np.int64)
            y = np.zeros(n * n, dtype=np.int64)
            s = 1
            while s < n:
                rx = 1 & t // 2
                ry = 1 & (t ^ rx)
                swap = ry == 0
                flip = swap & (rx == 1)
                x = np.where(flip, s - 1 - x, x)
                y = np.where(flip, s - 1 - y, y)
                x2 = np.where(swap, y, x)
                y2 = np.where(swap, x, y)
                x, y = (x2, y2)
                x = x + s * rx
                y = y + s * ry
                t = t // 4
                s *= 2
            return y * n + x

        def _level(x, idx, W, b, p, gp):
            Bsz, C, H, _ = x.shape
            h = H // p
            t = x.reshape(Bsz, C, h, p, h, p).transpose(0, 2, 4, 3, 5, 1).reshape(Bsz, h * h, p * p * C)
            t = t[:, idx]
            t = t.reshape(Bsz, h * h // gp, gp * p * p * C)
            return t @ W.T + b

        def _interp_linear(x, n_out):
            L = x.shape[1]
            pos = (jnp.arange(n_out, dtype=jnp.float32) + 0.5) * (L / n_out) - 0.5
            pos = jnp.clip(pos, 0.0, L - 1)
            i0 = jnp.floor(pos).astype(jnp.int32)
            i1 = jnp.minimum(i0 + 1, L - 1)
            w = (pos - i0).astype(x.dtype)
            return x[:, i0] * (1.0 - w)[None, :, None] + x[:, i1] * w[None, :, None]
        Ws = [(idx0, W0, b0, PRE[0]), (idx1, W1, b1, PRE[1]), (idx2, W2, b2, PRE[2])]
        outs = [_level(x, idx, W, b, p, GP) for idx, W, b, p in Ws]
        n_tokens = outs[0].shape[1]
        outs = [outs[0]] + [_interp_linear(o, n_tokens) for o in outs[1:]]
        y = jnp.concatenate(outs, axis=-1)
        return y @ Wf.T + bf

    def _L0_attn_ref(x, W_qkv, W_out):
        import jax, jax.numpy as jnp
        import numpy as np
        DIM = 192
        NUM_HEADS = 12
        DIM_HEAD = 64
        SCALE = 1.0 / DIM_HEAD ** 0.5
        B, T, _ = x.shape
        qkv = x @ W_qkv.T
        qkv = qkv.reshape(B, T, 3, NUM_HEADS, DIM_HEAD)
        q, k, v = (qkv[:, :, i].transpose(0, 2, 1, 3) for i in range(3))
        logits = jnp.einsum('bhtd,bhsd->bhts', q, k) / SCALE
        att = jax.nn.softmax(logits, axis=-1)
        o = jnp.einsum('bhts,bhsd->bhtd', att, v)
        cat = o.transpose(0, 2, 1, 3).reshape(B, T, NUM_HEADS * DIM_HEAD)
        return cat @ W_out.T

    def _L0_ffn_ref(x, Wr, w1, w3, w2, s1, s3, s2):
        import math
        import jax, jax.numpy as jnp
        import numpy as np
        NUM_EXPERTS = 8
        TOP_K = 2
        CAPACITY_FACTOR = 1.25
        H = 192
        INNER = 768
        B, S = (2, 512)
        b, s, h = x.shape
        n = b * s
        flat = x.reshape(n, h)
        logits = flat @ Wr
        probs = jax.nn.softmax(logits, axis=-1)
        topk_p, topk_i = jax.lax.top_k(probs, TOP_K)
        topk_p = topk_p / jnp.clip(topk_p.sum(-1, keepdims=True), 1e-09)
        capacity = max(1, math.ceil(n * TOP_K / NUM_EXPERTS * CAPACITY_FACTOR))
        onehot = topk_i[None, :, :] == jnp.arange(NUM_EXPERTS)[:, None, None]
        w_tok = jnp.sum(topk_p[None] * onehot, axis=-1)
        assigned = jnp.any(onehot, axis=-1)
        score = jnp.where(assigned, w_tok, -jnp.inf)
        order = jnp.argsort(-score, axis=1)[:, :capacity]
        score_sel = jnp.take_along_axis(score, order, axis=1)
        valid = jnp.isfinite(score_sel)
        weight_sel = jnp.where(valid, score_sel, 0.0)
        dispatch = flat[order]
        gate = jax.nn.silu(jnp.einsum('ech,ehi->eci', dispatch, w1))
        up = jnp.einsum('ech,ehi->eci', dispatch, w3)
        expert_out = jnp.einsum('eci,eih->ech', gate * up, w2)
        expert_out = expert_out * weight_sel[..., None]
        routed = jnp.zeros((n, h), dtype=flat.dtype)
        routed = routed.at[order.reshape(-1)].add(expert_out.reshape(-1, h))
        shared = jax.nn.silu(flat @ s1) * (flat @ s3) @ s2
        out = routed + shared
        return out.reshape(b, s, h)
    h = _L0_tok_ref(x, L0_tok_W0, L0_tok_b0, L0_tok_W1, L0_tok_b1, L0_tok_W2, L0_tok_b2, L0_tok_Wf, L0_tok_bf, L0_tok_idx0, L0_tok_idx1, L0_tok_idx2)
    h = h + _L0_attn_ref(_layernorm(h, axis=-1), L0_attn_W_qkv, L0_attn_W_out)
    h = h + _L0_ffn_ref(_layernorm(h, axis=-1), L0_ffn_Wr, L0_ffn_w1, L0_ffn_w3, L0_ffn_w2, L0_ffn_s1, L0_ffn_s3, L0_ffn_s2)
    return h

_drawn_inputs = setup_inputs


def setup_inputs(seed=0):
    import zlib

    import numpy as np

    out = dict(_drawn_inputs(seed))
    spreads = {}
    factors = {'L0_tok_b0': 4.319,
     'L0_tok_b1': 4.421,
     'L0_tok_b2': 3.955,
     'L0_ffn_Wr': 3.796,
     'L0_ffn_w1': 3.295,
     'L0_ffn_w3': 3.292,
     'L0_ffn_w2': 3.278,
     'L0_ffn_s1': 2.946,
     'L0_ffn_s3': 2.918,
     'L0_ffn_s2': 2.918}
    for name, (base, spread) in spreads.items():
        noise = np.random.default_rng([zlib.crc32(name.encode()), seed]).standard_normal(out[name].shape)
        drawn = base * np.exp(spread * noise) if base else spread * noise
        out[name] = jnp.asarray(drawn.astype(out[name].dtype))
    for name, factor in factors.items():
        out[name] = (out[name] * factor).astype(out[name].dtype)
    return out
```

```python
from contextlib import ExitStack

import numpy as np

import concourse.bass as bass
from concourse import mybir

ALU = mybir.AluOpType
ACT = mybir.ActivationFunctionType
AX = mybir.AxisListType
F32 = mybir.dt.float32
F32R = mybir.dt.float32r
I32 = mybir.dt.int32

P = 128
B = 4
CH = 3
GP = 16
EMB = 64
TOK = 256
N = B * TOK
NT = N // P
D = 192
KC = 2
KD = D // KC
HEADS = 12
DH = 64
INNER = HEADS * DH
PAIRS = HEADS // 2
LOGIT_GAIN = 8.0
EXPERTS = 8
FF = 768
FM = FF // P
CAP = 320
CT = (P, P, CAP - 2 * P)
SLOTS = EXPERTS * CAP
DROPPED = 8192.0
SHARED_CHUNK = 512
LN_EPS = 1e-5
W13 = 2 * KC * FF


def vit_tower(nc, ins, out):
    with ExitStack() as ctx:
        def sem(name):
            return ctx.enter_context(nc.semaphore(name))

        def sb(name, shape, dt=F32, where=ctx):
            return where.enter_context(nc.sbuf_tensor(name, shape, dt))

        slots_in = nc.dram_tensor("slots_in", [SLOTS, D], F32, kind="Internal").ap()
        slots_out = nc.dram_tensor("slots_out", [SLOTS, D], F32, kind="Internal").ap()

        bank = ctx.enter_context(nc.psum_tensor("bank", [P, 8, 512], F32))

        ident = sb("ident", [P, P])
        tri = sb("tri", [P, P])
        iota8 = sb("iota8", [P, NT, EXPERTS])
        h = sb("h", [P, NT, D])
        raw = sb("raw", [P, 2, W13])
        ws_hi = sb("ws_hi", [KD, W13], F32R)
        ws_lo = sb("ws_lo", [KD, W13], F32R)
        we_hi = sb("we_hi", [KD, 2, W13], F32R)
        we_lo = sb("we_lo", [KD, 2, W13], F32R)
        w2s = sb("w2s", [P, FM, D])
        w2e = sb("w2e", [P, 2, FM, D])
        zeros = sb("zeros", [P, 960])
        stats = sb("stats", [P, NT, 6])
        mv = sb("mv", [P, NT, 2])
        ve = sb("ve", [P, NT])
        lnv = sb("lnv", [P, NT])
        rstd = sb("rstd", [P, NT])
        nt1 = sb("nt1", [P, NT])
        stats2 = sb("stats2", [P, NT, 6])
        mv2 = sb("mv2", [P, NT, 2])

        early = ExitStack()
        wq_hi = sb("wq_hi", [KD, KC, 3 * INNER], F32R, early)
        wq_lo = sb("wq_lo", [KD, KC, 3 * INNER], F32R, early)
        wo = sb("wo", [P, PAIRS, D], F32, early)
        kz = sb("kz", [P, 2, 2, TOK], F32, early)
        negmax = sb("negmax", [P, 2, 2], F32, early)
        rowsum = sb("rowsum", [P, 2, 2], F32, early)
        rinv = sb("rinv", [P, 2, 2], F32, early)
        tok = ExitStack()
        idx0 = sb("idx0_s", [P, 2 * GP], I32, tok)
        idx1 = sb("idx1_s", [P, 8], I32, tok)
        idx2 = sb("idx2_s", [P, 2], I32, tok)
        g0 = sb("g0", [P, 2, GP, B * CH], F32, tok)
        g1 = sb("g1", [P, 8, B * 12], F32, tok)
        g2 = sb("g2", [P, 2, B * 48], F32, tok)
        s0 = sb("s0", [P, 2, B, GP * CH], F32, tok)
        s1g = sb("s1g", [P, B, 96], F32, tok)
        s2g = sb("s2g", [P, B, 96], F32, tok)
        w0t = sb("w0t", [GP * CH, EMB], F32, tok)
        w1t = sb("w1t", [96, 2, EMB], F32, tok)
        w2t = sb("w2t", [96, 8, EMB], F32, tok)
        i1m = sb("i1m", [P, 2, 2 * P], F32, tok)
        i2m = sb("i2m", [B * 16, 2, B * P], F32, tok)
        bcat = sb("bcat", [P, 2], F32, tok)
        wft = sb("wft", [P, 2, D], F32, tok)
        x0t = sb("x0t", [GP * CH, 2, B, P], F32, tok)
        x1t = sb("x1t", [96, 2, B, 64], F32, tok)
        x2t = sb("x2t", [96, 8, B, 16], F32, tok)
        o1s = sb("o1s", [P, 2, EMB], F32, tok)
        o2s = sb("o2s", [EMB, EMB], F32, tok)
        cat_a = sb("cat_a", [P, 2, B, P], F32, tok)
        cat_b = sb("cat_b", [EMB + 1, 2, B, P], F32, tok)
        tok.close()
        xn = sb("xn", [P, 2, D], F32, early)
        xt_hi = sb("xt_hi", [KD, KC, TOK], F32R, early)
        xt_lo = sb("xt_lo", [KD, KC, TOK], F32R, early)
        qt = sb("qt", [P, 2, TOK], F32, early)
        v = sb("v", [P, 2, INNER], F32, early)
        prob = sb("prob", [P, 2, 2, TOK], F32, early)
        prob_t = sb("prob_t", [P, 2, 2, TOK], F32, early)
        ot = sb("ot", [P, PAIRS, TOK], F32, early)
        early.close()

        late = ctx.enter_context(ExitStack())
        xn2 = sb("xn2", [P, NT, D], F32, late)
        x2_hi = sb("x2_hi", [KD, KC, N], F32R, late)
        x2_lo = sb("x2_lo", [KD, KC, N], F32R, late)
        wr_raw = sb("wr_raw", [KD, KC, EXPERTS], F32, late)
        wr_hi = sb("wr_hi", [KD, KC, EXPERTS], F32R, late)
        wr_lo = sb("wr_lo", [KD, KC, EXPERTS], F32R, late)
        hs = sb("hs", [P, FM, N], F32, late)
        gate = sb("gate", [P, 2, 512], F32, late)
        ga = sb("ga", [P, 2, NT, D], F32, late)
        rk = sb("rk", [P, 2, NT, 4], F32, late)
        slot = sb("slot", [P, 2, NT], I32, late)
        base = sb("base", [P, 2, NT], F32, late)
        wk = sb("wk", [P, 2, NT], F32, late)
        oh = sb("oh", [P, 2, NT, EXPERTS], F32, late)
        big = [sb(f"rt{i}", [P, NT, EXPERTS], F32, late) for i in range(6)]
        sml = [sb(f"rs{i}", [P, NT], F32, late) for i in range(8)]
        ranking = ExitStack()
        oh_t = sb("oh_t", [P, 2, N], F32R, ranking)
        sc_hi = sb("sc_hi", [P, N], F32R, ranking)
        sc_lo = sb("sc_lo", [P, N], F32R, ranking)
        cmp = sb("cmp", [P, N], F32, ranking)
        ranking.close()
        he = sb("he", [P, FM, CAP], F32, late)
        xd = sb("xd", [P, 2, 3, D], F32, late)
        xd_hi = sb("xd_hi", [KD, KC, CAP], F32R, late)
        xd_lo = sb("xd_lo", [KD, KC, CAP], F32R, late)
        ye = sb("ye", [P, 2, 3, D], F32, late)

        consts_in = sem("consts_in")
        idx_in = sem("idx_in")
        wqkv_in = sem("wqkv_in")
        wo_in = sem("wo_in")
        wr_in = sem("wr_in")
        w2s_in = sem("w2s_in")
        g2_in, g1_in = sem("g2_in"), sem("g1_in")
        g0_in = [sem("g0_in_half0"), sem("g0_in_half1")]
        raw_in = [sem("raw_in_0"), sem("raw_in_1")]
        w2e_in = [sem("w2e_in_0"), sem("w2e_in_1")]
        xd_in = [sem("xd_in_0"), sem("xd_in_1")]
        zeros_ready = sem("zeros_ready")
        slots_zeroed = sem("slots_zeroed")
        scattered = sem("scattered")
        ye_out = [sem("ye_out_0"), sem("ye_out_1")]
        gathered = [sem(f"gathered_{t}") for t in range(NT)]
        out_stored = sem("out_stored")
        grouped = sem("grouped")
        dve = sem("dve_step")
        act = sem("act_step")
        pe_tok = sem("pe_tok")
        tok_copied = sem("tok_copied")
        h_in = sem("h_in")
        ve_ready = sem("ve_ready")
        y0_ready = sem("y0_ready")
        wq_split = sem("wq_split")
        early_zeroed = sem("early_zeroed")
        xn_ready = sem("xn_ready")
        xt_done = sem("xt_done")
        xt_hi_ready = sem("xt_hi_ready")
        xt_lo_ready = sem("xt_lo_ready")
        proj_done = sem("proj_done")
        q_ready = sem("q_ready")
        k_ready = sem("k_ready")
        vproj_done = sem("vproj_done")
        v_ready = sem("v_ready")
        scores_done = sem("scores_done")
        max_ready = sem("max_ready")
        exp_done = sem("exp_done")
        norm_done = sem("norm_done")
        pt_done = sem("pt_done")
        pt_ready = sem("pt_ready")
        pv_done = sem("pv_done")
        o_ready = sem("o_ready")
        oproj_done = sem("oproj_done")
        resid_done = sem("resid_done")
        pool_hi = sem("pool_hi")
        split_go = sem("split_go")
        raw_split = sem("raw_split")
        xn2_ready = sem("xn2_ready")
        x2t_done = sem("x2t_done")
        x2_hi_ready = sem("x2_hi_ready")
        x2_lo_ready = sem("x2_lo_ready")
        wr_split = sem("wr_split")
        logits_done = sem("logits_done")
        lsh_ready = sem("lsh_ready")
        ex_ready = sem("ex_ready")
        topk_ready = sem("topk_ready")
        late_zeroed = sem("late_zeroed")
        sct_done = sem("sct_done")
        sct_copied = sem("sct_copied")
        sc_lo_ready = sem("sc_lo_ready")
        rank_rows = sem("rank_rows")
        rank_read = sem("rank_read")
        slot_ready = sem("slot_ready")
        gu_done = sem("gu_done")
        gate_ready = sem("gate_ready")
        hid_ready = sem("hid_ready")
        xdt_done = sem("xdt_done")
        xd_hi_ready = sem("xd_hi_ready")
        xd_lo_ready = sem("xd_lo_ready")
        ye_done = sem("ye_done")
        ye_copied = sem("ye_copied")
        ys_done = sem("ys_done")
        ys_read = sem("ys_read")
        tile_out = sem("tile_out")

        STEPS = ["t2", "t1", "o2", "o1", "i2_0", "i2_1", "i1_0", "t0_0", "a_0", "t0_1", "a_1", "h01", "h23", "h45", "h67"]
        STEP = {s: i + 1 for i, s in enumerate(STEPS)}

        NPRE = 4
        MSTEPS = [(c, m) for c in range(N // SHARED_CHUNK) for m in range(FM)]
        GROUPS = [(k, g) for k in range(2) for g in range(NT // 4)]

        block = ctx.enter_context(nc.Block())

        @block.sync
        def _(sp):
            for dst, src in ((idx2, "idx2"), (idx1, "idx1"), (idx0, "idx0")):
                sp.dma_start(dst[:], ins[src]).then_inc(idx_in, 16)
            raw_qkv = raw[0:KD].rearrange("p a c -> p (a c)")[:, 0:KC * 3 * INNER]
            for dst, src in ((ident, "ident"), (w2t, "w2t"), (w1t, "w1t"), (w0t, "w0t"), (i1m, "i1m"), (i2m, "i2m"),
                             (bcat, "bcat"), (wft, "wft"), (tri, "tri"), (iota8, "iota8")):
                sp.dma_start(dst[:], ins[src]).then_inc(consts_in, 16)
            sp.dma_start(raw_qkv, ins["wqkv"]).then_inc(wqkv_in, 16)
            sp.dma_start(wo[:], ins["wo"]).then_inc(wo_in, 16)
            sp.dma_start(w2s[:], ins["w2"][EXPERTS]).then_inc(w2s_in, 16)
            for e in range(2):
                sp.dma_start(w2e[:, e], ins["w2"][e]).then_inc(w2e_in[e], 16)
            sp.wait_ge(zeros_ready, 1)
            rows = slots_in.rearrange("(p r) d -> p (r d)", p=P)
            for q in range(4):
                sp.dma_start(rows[:, q * 960:(q + 1) * 960], zeros[:]).then_inc(slots_zeroed, 16)
            sp.wait_ge(wq_split, 2)
            sp.dma_start(raw[0:KD, 0], ins["w13"][EXPERTS]).then_inc(raw_in[0], 16)
            sp.dma_start(raw[0:KD, 1], ins["w13"][0]).then_inc(raw_in[1], 16)
            sp.wait_ge(raw_split, 1)
            sp.dma_start(raw[0:KD, 0], ins["w13"][1]).then_inc(raw_in[0], 16)
            sp.wait_ge(resid_done, NT)
            sp.dma_start(wr_raw[:], ins["wr"]).then_inc(wr_in, 16)
            sp.wait_ge(scattered, 16 * 2 * NT)

            def load_slots(e, par):
                full = slots_in[bass.ds(e * CAP, 2 * P), :].rearrange("(t p) d -> p t d", p=P)
                sp.dma_start(xd[:, par, 0:2, :], full).then_inc(xd_in[par], 16)
                sp.dma_start(xd[0:CT[2], par, 2, :], slots_in[bass.ds(e * CAP + 2 * P, CT[2]), :]).then_inc(xd_in[par], 16)

            def store_slots(e, par):
                sp.wait_ge(ye_copied, 3 * e + 3)
                full = slots_out[bass.ds(e * CAP, 2 * P), :].rearrange("(t p) d -> p t d", p=P)
                sp.dma_start(full, ye[:, par, 0:2, :]).then_inc(ye_out[par], 16)
                sp.dma_start(slots_out[bass.ds(e * CAP + 2 * P, CT[2]), :], ye[0:CT[2], par, 2, :]).then_inc(ye_out[par], 16)

            load_slots(0, 0)
            load_slots(1, 1)
            with sp.Fori(0, EXPERTS // 2 - 1) as ee:
                for par in range(2):
                    e = 2 * ee + par
                    sp.wait_ge(raw_split, e + 2)
                    sp.dma_start(raw[0:KD, 1 - par], ins["w13"][bass.ds(e + 2, 1)].rearrange("o k c -> (o k) c")).then_inc(raw_in[1 - par], 16)
                    sp.wait_ge(xdt_done, e + 1)
                    load_slots(e + 2, par)
                    store_slots(e, par)
                    sp.wait_ge(ye_done, 3 * e + 3)
                    sp.dma_start(w2e[:, par], ins["w2"][bass.ds(e + 2, 1)].rearrange("o p m d -> (o p) m d")).then_inc(w2e_in[par], 16)
            for par in range(2):
                store_slots(EXPERTS - 2 + par, par)
            for t in range(NT):
                sp.wait_ge(tile_out, t + 1)
                sp.dma_start(out[t], ga[:, 0, t, :]).then_inc(out_stored, 16)
            sp.wait_ge(out_stored, 16 * NT)

        @block.gpsimd
        def _(pool):
            nc.gpsimd.memset(zeros[:], 0.0).then_inc(zeros_ready, 1)
            pool.wait_ge(idx_in, 16 * 3)
            for j in range(2):
                nc.gpsimd.indirect_dma_start(out=g2[:, j, :], out_offset=None, in_=ins["x2"],
                                             in_offset=bass.IndirectOffsetOnAxis(ap=idx2[:, j:j + 1], axis=0)).then_inc(g2_in, 16)
            for j in range(8):
                nc.gpsimd.indirect_dma_start(out=g1[:, j, :], out_offset=None, in_=ins["x1"],
                                             in_offset=bass.IndirectOffsetOnAxis(ap=idx1[:, j:j + 1], axis=0)).then_inc(g1_in, 16)
            for half in range(2):
                for g in range(GP):
                    c = half * GP + g
                    nc.gpsimd.indirect_dma_start(out=g0[:, half, g, :], out_offset=None, in_=ins["x0"],
                                                 in_offset=bass.IndirectOffsetOnAxis(ap=idx0[:, c:c + 1], axis=0)).then_inc(g0_in[half], 16)

            def split(n, src, hi, lo):
                pool.wait_ge(raw_in[n % 2], 16 * (n // 2 + 1))
                nc.gpsimd.tensor_scalar(hi, src, 1.0, 0.0, ALU.mult, ALU.add).then_inc(pool_hi, 1)
                pool.wait_ge(pool_hi, n + 1)
                nc.gpsimd.tensor_tensor(lo, src, hi.bitcast(F32), ALU.subtract).then_inc(raw_split, 1)

            split(0, raw[0:KD, 0], ws_hi[:], ws_lo[:])
            split(1, raw[0:KD, 1], we_hi[:, 0], we_lo[:, 0])
            split(2, raw[0:KD, 0], we_hi[:, 1], we_lo[:, 1])
            pool.wait_ge(slots_zeroed, 16 * 4)
            for i, (k, g) in enumerate(GROUPS):
                pool.wait_ge(slot_ready, i + 1)
                for t in range(4 * g, 4 * g + 4):
                    nc.gpsimd.indirect_dma_start(out=slots_in, out_offset=bass.IndirectOffsetOnAxis(ap=slot[:, k, t:t + 1], axis=0),
                                                 in_=xn2[:, t, :], in_offset=None, bounds_check=SLOTS - 1,
                                                 oob_is_err=False).then_inc(scattered, 16)
            with pool.Fori(0, EXPERTS // 2 - 1) as ee:
                for par in range(2):
                    e = 2 * ee + par
                    pool.wait_ge(raw_in[1 - par], 16 * (ee + 2 + par))
                    pool.wait_ge(gu_done, len(MSTEPS) + FM * e + FM)
                    pool.sem_inc(split_go, 1)
                    nc.gpsimd.tensor_scalar(we_hi[:, par], raw[0:KD, 1 - par], 1.0, 0.0, ALU.mult, ALU.add).then_inc(pool_hi, 1)
                    pool.wait_ge(pool_hi, 3 + e + 1)
                    nc.gpsimd.tensor_tensor(we_lo[:, par], raw[0:KD, 1 - par], we_hi[:, par].bitcast(F32), ALU.subtract).then_inc(raw_split, 1)
            pool.wait_ge(ye_out[0], 32 * EXPERTS // 2)
            pool.wait_ge(ye_out[1], 32 * EXPERTS // 2)
            pool.wait_ge(late_zeroed, 3)
            for t in range(NT):
                for k in range(2):
                    nc.gpsimd.indirect_dma_start(out=ga[:, k, t, :], out_offset=None, in_=slots_out,
                                                 in_offset=bass.IndirectOffsetOnAxis(ap=slot[:, k, t:t + 1], axis=0),
                                                 bounds_check=SLOTS - 1, oob_is_err=False).then_inc(gathered[t], 16)

        @block.tensor
        def _(pe):
            mm = nc.tensor.matmul

            def mm3(dst, a_hi, a_lo, b_hi, b_lo, start, stop):
                mm(dst, a_lo, b_hi, start=start, stop=False)
                mm(dst, a_hi, b_lo, start=False, stop=False)
                return mm(dst, a_hi, b_hi, start=False, stop=stop)

            pe.wait_ge(consts_in, 16 * 10)
            pe.wait_ge(grouped, 1)
            for b in range(B):
                t = nc.tensor.transpose(bank[0:96, 0, b * P:(b + 1) * P], s2g[:, b], ident[:])
            t.then_inc(pe_tok, 1)
            pe.wait_ge(grouped, 2)
            for b in range(B):
                t = nc.tensor.transpose(bank[0:96, 1, b * P:(b + 1) * P], s1g[:, b], ident[:])
            t.then_inc(pe_tok, 1)
            pe.wait_ge(tok_copied, STEP["t2"])
            for g in range(8):
                t = mm(bank[0:EMB, 2, 0:EMB], x2t[:, g].rearrange("p b t -> p (b t)"), w2t[:, g], start=(g == 0), stop=(g == 7))
            t.then_inc(pe_tok, 1)
            pe.wait_ge(tok_copied, STEP["t1"])
            for q in range(2):
                for c in range(2):
                    t = mm(bank[:, 3, q * EMB:(q + 1) * EMB], x1t[:, c, 2 * q:2 * q + 2].rearrange("p b t -> p (b t)"), w1t[:, c],
                           start=(c == 0), stop=(c == 1))
            t.then_inc(pe_tok, 1)
            pe.wait_ge(tok_copied, STEP["o2"])
            for half in range(2):
                mm(bank[0:EMB, 6 + half, :], o2s[:], i2m[:, half], start=True, stop=True).then_inc(pe_tok, 1)
            pe.wait_ge(tok_copied, STEP["o1"])
            for half in range(2):
                for q in range(2):
                    t = mm(bank[EMB:P, 4 + half, q * TOK:(q + 1) * TOK], o1s[:, q], i1m[:, half],
                           start=True, stop=True)
            t.then_inc(pe_tok, 1)
            for half in range(2):
                pe.wait_ge(grouped, 3 + half)
                for b in range(B):
                    t = nc.tensor.transpose(bank[0:GP * CH, half, b * P:(b + 1) * P], s0[:, half, b], ident[:])
                t.then_inc(pe_tok, 1)
                pe.wait_ge(tok_copied, STEP[f"t0_{half}"])
                mm(bank[0:EMB, 4 + half, :], w0t[:], x0t[:, half].rearrange("p b t -> p (b t)"),
                   start=True, stop=True).then_inc(pe_tok, 1)
            pe.wait_ge(tok_copied, STEP["a_1"])
            for b in range(B):
                for half in range(2):
                    dst = bank[:, b, half * D:(half + 1) * D]
                    mm(dst, cat_a[:, half, b], wft[:, 0], start=True, stop=False)
                    t = mm(dst, cat_b[:, half, b], wft[0:EMB + 1, 1], start=False, stop=True)
                t.then_inc(pe_tok, 1)

            def turn_x(b):
                pe.wait_ge(xn_ready, b + 1)
                for c in range(KC):
                    for half in range(2):
                        t = nc.tensor.transpose(bank[0:KD, 6, c * TOK + half * P:c * TOK + (half + 1) * P],
                                                xn[:, half, c * KD:(c + 1) * KD], ident[:])
                t.then_inc(xt_done, 1)

            def project(col):
                for c in range(KC):
                    t = mm3(bank[:, 4, 0:TOK], wq_hi[:, c, col:col + P], wq_lo[:, c, col:col + P],
                            xt_hi[:, c], xt_lo[:, c], start=(c == 0), stop=(c == KC - 1))
                t.then_inc(proj_done, 1)

            def project_q(b, p, first=False):
                if not first:
                    pe.wait_ge(k_ready, PAIRS * b + p)
                if p == 0:
                    pe.wait_ge(xt_lo_ready, b + 1)
                project(p * P)

            def project_k(b, p):
                pe.wait_ge(q_ready, PAIRS * b + p + 1)
                project(INNER + p * P)

            def project_v(side, sh, bk):
                cols = slice(2 * INNER + side * (INNER // 2), 2 * INNER + (side + 1) * (INNER // 2))
                for c in range(KC):
                    t = mm3(bank[:, bk, 0:INNER // 2], xt_hi[:, c, sh * P:(sh + 1) * P], xt_lo[:, c, sh * P:(sh + 1) * P],
                            wq_hi[:, c, cols], wq_lo[:, c, cols], start=(c == 0), stop=(c == KC - 1))
                t.then_inc(vproj_done, 1)

            def scores(b, hd):
                u = HEADS * b + hd
                if hd % 2 == 0:
                    pe.wait_ge(q_ready, PAIRS * b + hd // 2 + 1)
                    pe.wait_ge(k_ready, PAIRS * b + hd // 2 + 1)
                if not (isinstance(b, int) and u < 2):
                    pe.wait_ge(exp_done, u - 1)
                for half in range(2):
                    t = mm(bank[:, hd % 2, half * TOK:(half + 1) * TOK], qt[:, hd // 2 % 2, half * P:(half + 1) * P],
                           kz[:, hd // 2 % 2, hd % 2], start=True, stop=True)
                t.then_inc(scores_done, 1)

            def turn_probs(b, hd):
                u = HEADS * b + hd
                pe.wait_ge(norm_done, u + 1)
                if hd:
                    pe.wait_ge(pt_ready, u - 1)
                for sh in range(2):
                    for half in range(2):
                        t = nc.tensor.transpose(bank[:, 2 + hd % 2, sh * TOK + half * P:sh * TOK + (half + 1) * P],
                                                prob[:, hd % 2, half, sh * P:(sh + 1) * P], ident[:])
                t.then_inc(pt_done, 1)

            def values(b, hd):
                u = HEADS * b + hd
                pe.wait_ge(pt_ready, u + 1)
                if hd == 0:
                    pe.wait_ge(v_ready, 4 * b + 2)
                if hd == HEADS // 2:
                    pe.wait_ge(v_ready, 4 * b + 4)
                if hd % 2 == 0:
                    pe.wait_ge(o_ready, PAIRS * b + hd // 2)
                rows = slice(hd % 2 * DH, (hd % 2 + 1) * DH)
                for sh in range(2):
                    t = mm(bank[rows, 5, 0:TOK], v[:, sh, hd * DH:(hd + 1) * DH], prob_t[:, hd % 2, sh],
                           start=(sh == 0), stop=(sh == 1))
                t.then_inc(pv_done, 1)

            def project_out(b, half, bk):
                pe.wait_ge(o_ready, PAIRS * b + PAIRS)
                for p in range(PAIRS):
                    t = mm(bank[:, bk, 0:D], ot[:, p, half * P:(half + 1) * P], wo[:, p], start=(p == 0), stop=(p == PAIRS - 1))
                t.then_inc(oproj_done, 1)

            pe.wait_ge(h_in, B)
            turn_x(0)
            pe.wait_ge(wq_split, 2)
            pe.wait_ge(early_zeroed, 1)
            project_q(0, 0, first=True)
            project_v(0, 0, 7)
            project_k(0, 0)
            pe.wait_ge(xt_lo_ready, 1)
            project_v(0, 1, 6)
            project_q(0, 1)
            pe.wait_ge(wo_in, 16)
            project_k(0, 1)
            scores(0, 0)

            def image(b, last):
                for hd in range(HEADS):
                    if hd < HEADS - 1:
                        scores(b, hd + 1)
                    elif not last:
                        scores(b + 1, 0)
                    if hd in (2, 4, 6, 8):
                        project_k(b, hd // 2 + 1)
                    if hd in (1, 3, 5, 7):
                        project_q(b, (hd + 3) // 2)
                    if hd == 1:
                        pe.wait_ge(resid_done, 2 * b)
                        pe.wait_ge(v_ready, 4 * b + 2)
                        project_v(1, 0, 6)
                    if hd == 2:
                        project_v(1, 1, 7)
                    if hd == 8 and not last:
                        pe.wait_ge(v_ready, 4 * b + 4)
                        turn_x(b + 1)
                    turn_probs(b, hd)
                    if hd > 0:
                        values(b, hd - 1)
                    if hd == 9 and not last:
                        project_q(b + 1, 0)
                        project_v(0, 0, 7)
                    if hd == 10 and not last:
                        project_k(b + 1, 0)
                        project_v(0, 1, 6)
                    if hd == 11 and not last:
                        project_q(b + 1, 1)
                values(b, HEADS - 1)
                if not last:
                    project_k(b + 1, 1)
                    pe.wait_ge(v_ready, 4 * b + 6)
                else:
                    pe.wait_ge(v_ready, 4 * b + 4)
                project_out(b, 0, 7)
                project_out(b, 1, 6)

            with pe.Fori(0, B - 1) as b:
                image(b, False)
            image(B - 1, True)

            for q in range(4):
                pe.wait_ge(xn2_ready, 2 * q + 2)
                for c in range(KC):
                    for i in range(2):
                        t = nc.tensor.transpose(bank[0:KD, q, c * TOK + i * P:c * TOK + (i + 1) * P],
                                                xn2[:, 2 * q + i, c * KD:(c + 1) * KD], ident[:])
                t.then_inc(x2t_done, 1)
            pe.wait_ge(wr_split, 2)
            pe.wait_ge(x2_lo_ready, 4)
            for t in range(NT):
                for c in range(KC):
                    x = mm3(bank[:, 0, t * EXPERTS:(t + 1) * EXPERTS], x2_hi[:, c, t * P:(t + 1) * P],
                            x2_lo[:, c, t * P:(t + 1) * P], wr_hi[:, c], wr_lo[:, c], start=(c == 0), stop=(c == KC - 1))
            x.then_inc(logits_done, 1)

            def hidden(n, w_hi, w_lo, m, x_hi, x_lo, cols, w):
                pair = 4 + 2 * (m % 2)
                if not (isinstance(n, int) and n < 2):
                    pe.wait_ge(hid_ready, n - 1)
                for half in range(2):
                    for c in range(KC):
                        at = (half * KC + c) * FF + m * P
                        t = mm3(bank[:, pair + half, 0:w], w_hi[:, at:at + P], w_lo[:, at:at + P],
                                x_hi[:, c, cols], x_lo[:, c, cols], start=(c == 0), stop=(c == KC - 1))
                t.then_inc(gu_done, 1)

            def shared_hidden(n):
                c, m = MSTEPS[n]
                hidden(n, ws_hi, ws_lo, m, x2_hi, x2_lo, slice(c * SHARED_CHUNK, (c + 1) * SHARED_CHUNK), SHARED_CHUNK)

            pe.wait_ge(raw_split, 1)
            for n in range(NPRE):
                shared_hidden(n)
            pe.wait_ge(topk_ready, 1)
            for src, b0, cnt in ((big[4], 0, 1), (oh[:, 0], 2, 2)):
                for t in range(NT):
                    x = nc.tensor.transpose(bank[0:EXPERTS, b0 + t // 4, t % 4 * P:(t % 4 + 1) * P], src[:, t, :], ident[:])
                x.then_inc(sct_done, 1)
            pe.wait_ge(sc_lo_ready, 1)
            for t in range(NT):
                x = nc.tensor.transpose(bank[0:EXPERTS, t // 4, t % 4 * P:(t % 4 + 1) * P], oh[:, 1, t, :], ident[:])
            x.then_inc(sct_done, 1)

            n = NPRE
            pe.wait_ge(late_zeroed, 3)
            for i in range(2 * NT):
                k, t = divmod(i, NT)
                b0 = 2 - 2 * (i % 2)
                if i < 2:
                    pe.wait_ge(sct_copied, 2 + i)
                else:
                    pe.wait_ge(rank_read, i - 1)
                for half in range(2):
                    dst = bank[:, b0 + half, :]
                    cols = slice(half * 512, (half + 1) * 512)
                    mm(dst, oh_t[:, k, t * P:(t + 1) * P], sc_lo[:, cols], start=True, stop=False)
                    x = mm(dst, oh_t[:, k, t * P:(t + 1) * P], sc_hi[:, cols], start=False, stop=True)
                x.then_inc(rank_rows, 1)
                if i % 2 == 1 and n < len(MSTEPS):
                    shared_hidden(n)
                    n += 1
            while n < len(MSTEPS):
                shared_hidden(n)
                n += 1

            def turn_slots(e, par, first=False):
                if first:
                    pe.wait_ge(rank_read, 2 * NT)
                else:
                    pe.wait_ge(xd_lo_ready, e)
                pe.wait_ge(xd_in[par], 32 * (e // 2 + 1) if isinstance(e, int) else 32 * (e_pair[0] + 1))
                for c in range(KC):
                    for s, rows in enumerate(CT):
                        t = nc.tensor.transpose(bank[0:KD, c, s * P:s * P + rows], xd[0:rows, par, s, c * KD:(c + 1) * KD],
                                                ident[0:rows, 0:rows])
                t.then_inc(xdt_done, 1)

            e_pair = [0]

            def expert(e, par, last):
                pe.wait_ge(xd_lo_ready, e + 1)
                pe.wait_ge(raw_split, e + 2)
                for m in range(FM):
                    hidden(len(MSTEPS) + FM * e + m, we_hi[:, par], we_lo[:, par], m, xd_hi, xd_lo, slice(0, CAP), CAP)
                if not last:
                    if par == 1:
                        e_pair[0] = e_pair[0] + 1
                    turn_slots(e + 1, 1 - par)
                pe.wait_ge(w2e_in[par], 16 * (e_pair_now[0] + 1))
                pe.wait_ge(hid_ready, len(MSTEPS) + FM * e + FM)
                for s, rows in enumerate(CT):
                    if not (isinstance(e, int) and 3 * e + s < 2):
                        pe.wait_ge(ye_copied, 3 * e + s - 1)
                    for m in range(FM):
                        t = mm(bank[0:rows, 2 + (3 * par + s) % 2, 0:D], he[:, m, s * P:s * P + rows], w2e[:, par, m],
                               start=(m == 0), stop=(m == FM - 1))
                    t.then_inc(ye_done, 1)

            turn_slots(0, 0, first=True)
            e_pair_now = [0]
            expert(0, 0, False)
            expert(1, 1, False)
            with pe.Fori(1, EXPERTS // 2 - 1) as ee:
                e_pair[0] = ee
                e_pair_now[0] = ee
                expert(2 * ee, 0, False)
                expert(2 * ee + 1, 1, False)
            e_pair[0] = e_pair_now[0] = EXPERTS // 2 - 1
            expert(EXPERTS - 2, 0, False)
            expert(EXPERTS - 1, 1, True)
            pe.wait_ge(w2s_in, 16)
            for t in range(NT):
                if t >= 4:
                    pe.wait_ge(ys_read, t - 3)
                elif t >= 2:
                    pe.wait_ge(ye_copied, 3 * EXPERTS)
                for m in range(FM):
                    x = mm(bank[:, t % 4, 0:D], hs[:, m, t * P:(t + 1) * P], w2s[:, m], start=(m == 0), stop=(m == FM - 1))
                x.then_inc(ys_done, 1)

        @block.scalar
        def _(sc):
            fn = nc.scalar.activation
            count = [0]

            def copied(step, *ops):
                sc.wait_ge(pe_tok, STEP[step])
                for x in ops:
                    last = x()
                last.then_inc(tok_copied, 1)

            sc.wait_ge(consts_in, 16 * 10)
            copied("t2", lambda: fn(x2t[:].rearrange("p g b t -> p b g t"), bank[0:96, 0, :].rearrange("p (b g t) -> p b g t", b=B, g=8), ACT.Copy))
            copied("t1", lambda: fn(x1t[:].rearrange("p c b t -> p b c t"), bank[0:96, 1, :].rearrange("p (b c t) -> p b c t", b=B, c=2), ACT.Copy))
            copied("o2", lambda: fn(o2s[:], bank[0:EMB, 2, 0:EMB], ACT.Copy))
            copied("o1", lambda: fn(o1s[:].rearrange("p q e -> p (q e)"), bank[:, 3, 0:2 * EMB], ACT.Copy))
            for half in range(2):
                copied(f"i2_{half}", lambda: fn(cat_b[0:EMB, half].rearrange("p b t -> p (b t)"), bank[0:EMB, 6 + half, :],
                                                ACT.Identity, bias=bcat[0:EMB, 1:2]))
            sc.wait_ge(pe_tok, STEP["i1_0"])
            nc.scalar.activation(lnv[:, 0:1], bcat[:, 0:1], ACT.Copy).then_inc(tok_copied, 1)
            for half in range(2):
                copied(f"t0_{half}", lambda: fn(x0t[:, half].rearrange("p b t -> p (b t)"), bank[0:GP * CH, half, :], ACT.Copy))
                copied(f"a_{half}", lambda: fn(cat_a[:, half].rearrange("p b t -> p (b t)"), bank[:, 4 + half, :],
                                               ACT.Identity, bias=bcat[:, 0:1]))
            for b in range(B):
                sc.wait_ge(pe_tok, STEP["h01"] + b)
                fn(h[:, 2 * b:2 * b + 2].rearrange("p t d -> p (t d)"), bank[:, b, 0:2 * D], ACT.Copy).then_inc(h_in, 1)

            def inv_std_start(n, ready, done):
                sc.wait_ge(ve_ready, ready)
                fn(lnv[:, 0:n], ve[:, 0:n], ACT.Ln).then_inc(act, 1)
                count[0] += 1
                sc.wait_ge(act, count[0])
                fn(rstd[:, 0:n], lnv[:, 0:n], ACT.Exp, scale=-0.5).then_inc(y0_ready, 1)

            inv_std_start(NT, 1, 1)

            def copy_x(b):
                sc.wait_ge(xt_done, b + 1)
                fn(xt_hi[:].rearrange("p c t -> p (c t)"), bank[0:KD, 6, :], ACT.Copy).then_inc(xt_hi_ready, 1)

            def copy_q(b, p):
                sc.wait_ge(proj_done, HEADS * b + 2 * p + 1)
                fn(qt[:, p % 2], bank[:, 4, 0:TOK], ACT.Copy, scale=LOGIT_GAIN).then_inc(q_ready, 1)

            def copy_v(n, side, sh, bk):
                sc.wait_ge(vproj_done, n)
                fn(v[:, sh, side * (INNER // 2):(side + 1) * (INNER // 2)], bank[:, bk, 0:INNER // 2], ACT.Copy).then_inc(v_ready, 1)

            def exps(b, hd):
                sc.wait_ge(max_ready, HEADS * b + hd + 1)
                if not (isinstance(b, int) and HEADS * b + hd < 2):
                    sc.wait_ge(pt_done, HEADS * b + hd - 1)
                for half in range(2):
                    last = fn(prob[:, hd % 2, half], bank[:, hd % 2, half * TOK:(half + 1) * TOK], ACT.Exp,
                              bias=negmax[:, hd % 2, half:half + 1], accum_out=rowsum[:, hd % 2, half:half + 1])
                last.then_inc(exp_done, 1)

            def copy_o(b, p):
                sc.wait_ge(pv_done, HEADS * b + 2 * p + 2)
                if p == 0:
                    sc.wait_ge(oproj_done, 2 * b)
                fn(ot[:, p], bank[:, 5, 0:TOK], ACT.Copy).then_inc(o_ready, 1)

            copy_x(0)
            copy_q(0, 0)
            copy_v(1, 0, 0, 7)
            copy_v(2, 0, 1, 6)
            copy_q(0, 1)
            exps(0, 0)

            def image(b, last):
                for hd in range(HEADS):
                    if hd in (1, 3, 5, 7):
                        copy_q(b, (hd + 3) // 2)
                    if hd < HEADS - 1:
                        exps(b, hd + 1)
                    elif not last:
                        exps(b + 1, 0)
                    if hd == 1:
                        copy_v(4 * b + 3, 1, 0, 6)
                    if hd == 2:
                        copy_v(4 * b + 4, 1, 1, 7)
                    if hd == 8 and not last:
                        sc.wait_ge(proj_done, HEADS * (b + 1))
                        copy_x(b + 1)
                    if hd >= 2 and hd % 2 == 0:
                        copy_o(b, hd // 2 - 1)
                    if hd == 9 and not last:
                        copy_q(b + 1, 0)
                        sc.wait_ge(pv_done, HEADS * b + HEADS // 2)
                        copy_v(4 * b + 5, 0, 0, 7)
                    if hd == 10 and not last:
                        copy_v(4 * b + 6, 0, 1, 6)
                    if hd == 11 and not last:
                        copy_q(b + 1, 1)
                copy_o(b, PAIRS - 1)

            with sc.Fori(0, B - 1) as b:
                image(b, False)
            image(B - 1, True)

            inv_std_start(NT, 2, 2)
            for q in range(4):
                sc.wait_ge(x2t_done, q + 1)
                fn(x2_hi[:, :, q * TOK:(q + 1) * TOK], bank[0:KD, q, :].rearrange("p (c t) -> p c t", c=KC), ACT.Copy).then_inc(x2_hi_ready, 1)
            sc.wait_ge(lsh_ready, 1)
            fn(big[1][:], big[0][:], ACT.Exp).then_inc(ex_ready, 1)

            def silu(n, m, w):
                sc.wait_ge(gu_done, n + 1)
                if not (isinstance(n, int) and n < 2):
                    sc.wait_ge(hid_ready, n - 1)
                fn(gate[:, m % 2, 0:w], bank[:, 4 + 2 * (m % 2), 0:w], ACT.Silu).then_inc(gate_ready, 1)

            for n in range(NPRE):
                silu(n, MSTEPS[n][1], SHARED_CHUNK)
            sc.wait_ge(late_zeroed, 3)
            sc.wait_ge(sct_done, 1)
            fn(sc_hi[0:EXPERTS], bank[0:EXPERTS, 0:2, :].rearrange("p a c -> p (a c)"), ACT.Copy).then_inc(sct_copied, 1)
            sc.wait_ge(sct_done, 2)
            fn(oh_t[0:EXPERTS, 0], bank[0:EXPERTS, 2:4, :].rearrange("p a c -> p (a c)"), ACT.Copy).then_inc(sct_copied, 1)
            sc.wait_ge(sct_done, 3)
            fn(oh_t[0:EXPERTS, 1], bank[0:EXPERTS, 0:2, :].rearrange("p a c -> p (a c)"), ACT.Copy).then_inc(sct_copied, 1)
            for n in range(NPRE, len(MSTEPS)):
                silu(n, MSTEPS[n][1], SHARED_CHUNK)

            def split_slots(e):
                sc.wait_ge(xdt_done, e + 1)
                fn(xd_hi[:], bank[0:KD, 0:KC, 0:CAP], ACT.Copy).then_inc(xd_hi_ready, 1)

            def copy_out(e, par):
                if not isinstance(e, int) or e >= 2:
                    sc.wait_ge(ye_out[par], 32 * (e_half[0]))
                for s, rows in enumerate(CT):
                    sc.wait_ge(ye_done, 3 * e + s + 1)
                    fn(ye[0:rows, par, s], bank[0:rows, 2 + (3 * par + s) % 2, 0:D], ACT.Copy).then_inc(ye_copied, 1)

            def expert(e, par, last):
                for m in range(FM):
                    silu(len(MSTEPS) + FM * e + m, m, CAP)
                if not last:
                    split_slots(e + 1)
                copy_out(e, par)

            split_slots(0)
            e_half = [0]
            expert(0, 0, False)
            expert(1, 1, False)
            with sc.Fori(1, EXPERTS // 2 - 1) as ee:
                e_half[0] = ee
                expert(2 * ee, 0, False)
                expert(2 * ee + 1, 1, False)
            e_half[0] = EXPERTS // 2 - 1
            expert(EXPERTS - 2, 0, False)
            expert(EXPERTS - 1, 1, True)

        @block.vector
        def _(vec):
            ts, tt, stt = nc.vector.tensor_scalar, nc.vector.tensor_tensor, nc.vector.scalar_tensor_tensor
            steps = [0]
            offset = [0]

            def step(x):
                x.then_inc(dve, 1)
                steps[0] += 1
                vec.wait_ge(dve, offset[0] + steps[0])

            nc.vector.memset(cat_b[EMB:EMB + 1].rearrange("p h b t -> p (h b t)"), 1.0)
            nc.vector.memset(kz[:].rearrange("p a b t -> p (a b t)"), 0.0).then_inc(early_zeroed, 1)
            raw_qkv = raw[0:KD].rearrange("p a c -> p (a c)")[:, 0:KC * 3 * INNER]
            flat_hi = wq_hi[:].rearrange("p c n -> p (c n)")
            vec.wait_ge(wqkv_in, 16)
            nc.vector.tensor_copy(flat_hi, raw_qkv).then_inc(wq_split, 1)
            vec.wait_ge(wq_split, 1)
            tt(wq_lo[:].rearrange("p c n -> p (c n)"), raw_qkv, flat_hi.bitcast(F32), ALU.subtract).then_inc(wq_split, 1)

            for gate_in, n_dma, dst, src, g in ((g2_in, 2, s2g[:], g2[:], 2), (g1_in, 8, s1g[:], g1[:], 8),
                                                (g0_in[0], GP, s0[:, 0], g0[:, 0], GP), (g0_in[1], GP, s0[:, 1], g0[:, 1], GP)):
                vec.wait_ge(gate_in, 16 * n_dma)
                form = src.rearrange("p g (b c) -> p b g c", b=B)
                nc.vector.tensor_copy(dst.rearrange("p b (g c) -> p b g c", g=g), form).then_inc(grouped, 1)

            def moments(t, st, m):
                step(nc.vector.bn_stats(st[:, t], h[:, t]))
                return nc.vector.bn_aggr(m[:, t], st[:, t])

            def inv_std(m, n_y0, sem_n):
                nc.vector.tensor_scalar(ve[:], m[:, :, 1], LN_EPS, None, ALU.add).then_inc(ve_ready, 1)
                vec.wait_ge(y0_ready, n_y0)
                step(tt(nt1[:], rstd[:], rstd[:], ALU.mult))
                step(tt(nt1[:], nt1[:], ve[:], ALU.mult))
                step(ts(nt1[:], nt1[:], -0.5, 1.5, ALU.mult, ALU.add))
                step(tt(rstd[:], rstd[:], nt1[:], ALU.mult))

            for b in range(B):
                vec.wait_ge(h_in, b + 1)
                for t in (2 * b, 2 * b + 1):
                    step(moments(t, stats, mv))
            inv_std(mv, 1, 1)

            def normalize(b):
                for half in range(2):
                    t = 2 * b + half
                    m = mv[:, bass.ds(t, 1), 0]
                    r = rstd[:, bass.ds(t, 1)]
                    x = ts(xn[:, half], h[:, bass.ds(t, 1)].rearrange("p o d -> p (o d)"), m, r, ALU.subtract, ALU.mult)
                x.then_inc(xn_ready, 1)

            def rest_x(b):
                vec.wait_ge(xt_hi_ready, b + 1)
                tt(xt_lo[:].rearrange("p c t -> p (c t)"), bank[0:KD, 6, :], xt_hi[:].rearrange("p c t -> p (c t)").bitcast(F32),
                   ALU.subtract).then_inc(xt_lo_ready, 1)

            def copy_k(b, p):
                vec.wait_ge(proj_done, HEADS * b + 2 * p + 2)
                nc.vector.tensor_copy(kz[0:DH, p % 2, 0], bank[0:DH, 4, 0:TOK])
                nc.vector.tensor_copy(kz[DH:P, p % 2, 1], bank[DH:P, 4, 0:TOK]).then_inc(k_ready, 1)

            def head_max(b, hd):
                vec.wait_ge(scores_done, HEADS * b + hd + 1)
                nc.vector.tensor_reduce(negmax[:, hd % 2], bank[:, hd % 2, :].rearrange("p (h s) -> p h s", h=2), AX.X, ALU.max,
                                        negate=True).then_inc(max_ready, 1)

            def head_norm(b, hd):
                vec.wait_ge(exp_done, HEADS * b + hd + 1)
                step(nc.vector.reciprocal(rinv[:, hd % 2], rowsum[:, hd % 2]))
                for half in range(2):
                    x = ts(prob[:, hd % 2, half], prob[:, hd % 2, half], rinv[:, hd % 2, half:half + 1], None, ALU.mult)
                x.then_inc(norm_done, 1)

            def copy_probs(b, hd):
                u = HEADS * b + hd
                vec.wait_ge(pt_done, u + 1)
                if hd:
                    vec.wait_ge(pv_done, u - 1)
                nc.vector.tensor_copy(prob_t[:, hd % 2].rearrange("p s t -> p (s t)"), bank[:, 2 + hd % 2, :]).then_inc(pt_ready, 1)

            normalize(0)
            rest_x(0)
            copy_k(0, 0)
            copy_k(0, 1)
            head_max(0, 0)
            head_norm(0, 0)

            def image(b, last):
                for hd in range(HEADS):
                    if hd in (2, 4, 6, 8):
                        copy_k(b, hd // 2 + 1)
                    if hd < HEADS - 1:
                        head_max(b, hd + 1)
                    elif not last:
                        head_max(b + 1, 0)
                    copy_probs(b, hd)
                    if hd < HEADS - 1:
                        head_norm(b, hd + 1)
                    elif not last:
                        head_norm(b + 1, 0)
                    if hd == 5 and not last:
                        vec.wait_ge(xt_done, b + 1)
                        normalize(b + 1)
                    if hd == 8 and not last:
                        rest_x(b + 1)
                    if hd == 10 and not last:
                        copy_k(b + 1, 0)
                    if hd == 6 and last:
                        for t in range(NT - 2):
                            step(nc.vector.bn_aggr(mv2[:, t], stats2[:, t]))
                if not last:
                    copy_k(b + 1, 1)
                for half in range(2):
                    vec.wait_ge(oproj_done, 2 * b + half + 1)
                    ht = h[:, bass.ds(2 * b + half, 1)].rearrange("p o d -> p (o d)")
                    st = stats2[:, bass.ds(2 * b + half, 1)].rearrange("p o d -> p (o d)")
                    tt(ht, bank[:, 7 - half, 0:D], ht, ALU.add).then_inc(resid_done, 1)
                    vec.wait_ge(resid_done, 2 * b + half + 1)
                    step(nc.vector.bn_stats(st, ht))

            before = steps[0]
            with vec.Fori(0, B - 1) as b:
                per_image = HEADS + 2
                offset[0] = per_image * b
                image(b, False)
            assert steps[0] - before == per_image
            offset[0] = per_image * (B - 2)
            image(B - 1, True)

            for t in (NT - 2, NT - 1):
                step(nc.vector.bn_aggr(mv2[:, t], stats2[:, t]))
            inv_std(mv2, 2, 2)
            for t in range(NT):
                ts(xn2[:, t], h[:, t], mv2[:, t, 0:1], rstd[:, t:t + 1], ALU.subtract, ALU.mult).then_inc(xn2_ready, 1)
            vec.wait_ge(wr_in, 16)
            nc.vector.tensor_copy(wr_hi[:], wr_raw[:]).then_inc(wr_split, 1)
            vec.wait_ge(wr_split, 1)
            tt(wr_lo[:], wr_raw[:], wr_hi[:].bitcast(F32), ALU.subtract).then_inc(wr_split, 1)
            for q in range(4):
                vec.wait_ge(x2_hi_ready, q + 1)
                cols = slice(q * TOK, (q + 1) * TOK)
                tt(x2_lo[:, :, cols], bank[0:KD, q, :].rearrange("p (c t) -> p c t", c=KC), x2_hi[:, :, cols].bitcast(F32),
                   ALU.subtract).then_inc(x2_lo_ready, 1)
            nc.vector.memset(oh_t[:].bitcast(F32), 0.0).then_inc(late_zeroed, 1)
            nc.vector.memset(sc_hi[:].bitcast(F32), 0.0).then_inc(late_zeroed, 1)
            nc.vector.memset(sc_lo[:].bitcast(F32), 0.0)
            step(nc.vector.memset(rk[:], 0.0))
            nc.vector.memset(ga[:].rearrange("p k t d -> p (k t d)"), 0.0).then_inc(late_zeroed, 1)

            def wide(x):
                return x.unsqueeze(2).to_broadcast([P, NT, EXPERTS])

            def mul_hidden(n, m, dst, w):
                vec.wait_ge(gate_ready, n + 1)
                tt(dst, gate[:, m % 2, 0:w], bank[:, 5 + 2 * (m % 2), 0:w], ALU.mult).then_inc(hid_ready, 1)

            done = [0]

            def shared_mul():
                n = done[0]
                if n < len(MSTEPS):
                    c, m = MSTEPS[n]
                    mul_hidden(n, m, hs[:, m, c * SHARED_CHUNK:(c + 1) * SHARED_CHUNK], SHARED_CHUNK)
                    done[0] += 1

            m1, s1, r1, i1, p1, p2, i2, tmp = [x[:] for x in sml]
            ls, pr, key, tmp8, score = big[0][:], big[2][:], big[3][:], big[5][:], big[4][:]
            vec.wait_ge(logits_done, 1)
            lg = bank[:, 0, 0:NT * EXPERTS].rearrange("p (t e) -> p t e", t=NT)
            step(nc.vector.tensor_reduce(m1, lg, AX.X, ALU.max))
            tt(ls, lg, wide(m1), ALU.subtract).then_inc(lsh_ready, 1)
            vec.wait_ge(ex_ready, 1)
            ex = big[1][:]
            step(nc.vector.tensor_reduce(s1, ex, AX.X, ALU.add))
            step(nc.vector.reciprocal(r1, s1))
            step(tt(pr, ex, wide(r1), ALU.mult))

            def choose(k, vals, top, idx):
                step(nc.vector.tensor_reduce(top, vals, AX.X, ALU.max))
                step(tt(key, vals, wide(top), ALU.is_lt))
                step(stt(key, key, float(EXPERTS), iota8[:], ALU.mult, ALU.add))
                step(nc.vector.tensor_reduce(idx, key, AX.X, ALU.min))
                step(tt(oh[:, k], iota8[:], wide(idx), ALU.is_equal))

            choose(0, pr, p1, i1)
            shared_mul()
            step(stt(pr, oh[:, 0], -2.0, pr, ALU.mult, ALU.add))
            choose(1, pr, p2, i2)
            shared_mul()
            step(tt(tmp, p1, p2, ALU.add))
            step(ts(tmp, tmp, 1e-9, None, ALU.max))
            step(nc.vector.reciprocal(r1, tmp))
            step(tt(wk[:, 0], p1, r1, ALU.mult))
            step(tt(wk[:, 1], p2, r1, ALU.mult))
            step(tt(score, oh[:, 0], wide(wk[:, 0]), ALU.mult))
            step(tt(key, oh[:, 1], wide(wk[:, 1]), ALU.mult))
            step(tt(score, score, key, ALU.add))
            step(tt(tmp8, oh[:, 0], oh[:, 1], ALU.add))
            stt(score, tmp8, -1.0, score, ALU.add, ALU.add).then_inc(topk_ready, 1)
            vec.wait_ge(topk_ready, 1)
            step(ts(base[:, 0], i1, float(CAP), None, ALU.mult))
            step(ts(base[:, 1], i2, float(CAP), None, ALU.mult))
            shared_mul()
            shared_mul()
            vec.wait_ge(sct_copied, 1)
            tt(sc_lo[0:EXPERTS], bank[0:EXPERTS, 0:2, :].rearrange("p a c -> p (a c)"), sc_hi[0:EXPERTS].bitcast(F32),
               ALU.subtract).then_inc(sc_lo_ready, 1)

            n_group = 0
            for i in range(2 * NT):
                k, t = divmod(i, NT)
                b0 = 2 - 2 * (i % 2)
                rows = bank[:, b0:b0 + 2, :].rearrange("p a c -> p (a c)")
                own = wk[:, k, t:t + 1]
                vec.wait_ge(rank_rows, i + 1)
                if i:
                    vec.wait_ge(rank_read, i)
                if t:
                    step(ts(cmp[:, 0:t * P], rows[:, 0:t * P], own, None, ALU.is_ge, ALU.add, rk[:, k, t, 0:1]))
                step(ts(cmp[:, t * P:N], rows[:, t * P:N], own, None, ALU.is_gt, ALU.add, rk[:, k, t, 1:2]))
                stt(cmp[:, t * P:(t + 1) * P], rows[:, t * P:(t + 1) * P], own, tri[:], ALU.is_equal, ALU.mult,
                    accum_out=rk[:, k, t, 2:3]).then_inc(rank_read, 1)
                if i % 2 == 1:
                    shared_mul()
                if t % 4 == 3:
                    g = slice(t - 3, t + 1)
                    r, s = s1[:, g], m1[:, g]
                    vec.wait_ge(rank_read, i + 1)
                    step(nc.vector.tensor_reduce(r, rk[:, k, g], AX.X, ALU.add))
                    step(ts(s, r, float(CAP), DROPPED, ALU.is_ge, ALU.mult))
                    step(tt(s, s, r, ALU.add))
                    tt(slot[:, k, g], s, base[:, k, g], ALU.add).then_inc(slot_ready, 1)
                    n_group += 1
                    vec.wait_ge(slot_ready, n_group)
            while done[0] < len(MSTEPS):
                shared_mul()

            def rest_slots(e):
                vec.wait_ge(xd_hi_ready, e + 1)
                tt(xd_lo[:], bank[0:KD, 0:KC, 0:CAP], xd_hi[:].bitcast(F32), ALU.subtract).then_inc(xd_lo_ready, 1)

            def expert(e, last):
                if not (isinstance(e, int) and e == 0):
                    vec.wait_ge(ye_done, 3 * e)
                for m in range(FM):
                    mul_hidden(len(MSTEPS) + FM * e + m, m, he[:, m], CAP)
                if not last:
                    rest_slots(e + 1)

            rest_slots(0)
            expert(0, False)
            expert(1, False)
            with vec.Fori(1, EXPERTS // 2 - 1) as ee:
                expert(2 * ee, False)
                expert(2 * ee + 1, False)
            expert(EXPERTS - 2, False)
            expert(EXPERTS - 1, True)

            for t in range(NT):
                vec.wait_ge(ys_done, t + 1)
                tt(h[:, t], bank[:, t % 4, 0:D], h[:, t], ALU.add).then_inc(ys_read, 1)
                vec.wait_ge(ys_read, t + 1)
                vec.wait_ge(gathered[t], 32)
                step(stt(ga[:, 0, t], ga[:, 0, t], wk[:, 0, t:t + 1], h[:, t], ALU.mult, ALU.add))
                stt(ga[:, 0, t], ga[:, 1, t], wk[:, 1, t:t + 1], ga[:, 0, t], ALU.mult, ALU.add).then_inc(tile_out, 1)


def _interp(n_in, n_out):
    pos = (np.arange(n_out, dtype=np.float32) + np.float32(0.5)) * np.float32(n_in / n_out) - np.float32(0.5)
    pos = np.clip(pos, 0.0, n_in - 1).astype(np.float32)
    i0 = np.floor(pos).astype(np.int64)
    i1 = np.minimum(i0 + 1, n_in - 1)
    w = (pos - i0).astype(np.float32)
    m = np.zeros((n_in, n_out), np.float32)
    m[i0, np.arange(n_out)] += np.float32(1.0) - w
    m[i1, np.arange(n_out)] += w
    return m


def _layout(x, W0, b0, W1, b1, W2, b2, Wf, bf, idx0, idx1, idx2, Wqkv, Wout, Wr, w1, w3, w2, s1, s3, s2):
    def patches(p):
        n = 64 // p
        return x.reshape(B, CH, n, p, n, p).transpose(2, 4, 0, 3, 5, 1).reshape(n * n, B * p * p * CH)

    a = {"x0": patches(1), "x1": patches(2), "x2": patches(4)}
    a["idx0"] = idx0.reshape(2, P, GP).transpose(1, 0, 2).reshape(P, 2 * GP)
    a["idx1"] = idx1.reshape(64, 2, 8).transpose(1, 0, 2).reshape(P, 8)
    a["idx2"] = idx2.reshape(16, 8, 2).transpose(1, 0, 2).reshape(P, 2)
    a["w0t"] = W0.T
    a["w1t"] = W1.T.reshape(2, 96, EMB).transpose(1, 0, 2)
    a["w2t"] = W2.T.reshape(8, 96, EMB).transpose(1, 0, 2)
    m1, m2 = _interp(64, TOK), _interp(16, TOK)
    i1 = np.zeros((2, 64, 2, 2, P), np.float32)
    for b in range(2):
        i1[b, :, :, b, :] = m1.reshape(64, 2, P)
    a["i1m"] = i1.reshape(P, 2, 2 * P)
    i2 = np.zeros((B, 16, 2, B, P), np.float32)
    for b in range(B):
        i2[b, :, :, b, :] = m2.reshape(16, 2, P)
    a["i2m"] = i2.reshape(B * 16, 2, B * P)
    bc = np.zeros((P, 2), np.float32)
    bc[0:EMB, 0], bc[EMB:, 0], bc[0:EMB, 1] = b0, b1, b2
    a["bcat"] = bc
    wf = np.zeros((P, 2, D), np.float32)
    wf[:, 0] = Wf.T[0:P]
    wf[0:EMB, 1] = Wf.T[P:D]
    wf[EMB, 1] = bf
    a["wft"] = wf
    a["ident"] = np.eye(P, dtype=np.float32)
    a["tri"] = np.tril(np.ones((P, P), np.float32), -1)
    a["iota8"] = np.broadcast_to(np.arange(EXPERTS, dtype=np.float32), (P, NT, EXPERTS))
    a["wqkv"] = Wqkv.T.reshape(KC, KD, 3 * INNER).transpose(1, 0, 2).reshape(KD, KC * 3 * INNER)
    a["wo"] = Wout.T.reshape(PAIRS, P, D).transpose(1, 0, 2)
    a["wr"] = Wr.reshape(KC, KD, EXPERTS).transpose(1, 0, 2)
    up = np.stack([np.concatenate([w1, s1[None]]), np.concatenate([w3, s3[None]])], 1)
    a["w13"] = up.reshape(EXPERTS + 1, 2, KC, KD, FF).transpose(0, 3, 1, 2, 4).reshape(EXPERTS + 1, KD, W13)
    down = np.concatenate([w2, s2[None]])
    a["w2"] = down.reshape(EXPERTS + 1, FM, P, D).transpose(0, 2, 1, 3)
    return {k: np.ascontiguousarray(v) for k, v in a.items()}


def kernel(x, L0_tok_W0, L0_tok_b0, L0_tok_W1, L0_tok_b1, L0_tok_W2, L0_tok_b2, L0_tok_Wf, L0_tok_bf,
           L0_tok_idx0, L0_tok_idx1, L0_tok_idx2, L0_attn_W_qkv, L0_attn_W_out, L0_ffn_Wr, L0_ffn_w1, L0_ffn_w3,
           L0_ffn_w2, L0_ffn_s1, L0_ffn_s3, L0_ffn_s2):
    import concourse.bacc as _bacc
    from concourse.bass_utils import run_bass_kernel_spmd as _run

    given = (x, L0_tok_W0, L0_tok_b0, L0_tok_W1, L0_tok_b1, L0_tok_W2, L0_tok_b2, L0_tok_Wf, L0_tok_bf,
             L0_tok_idx0, L0_tok_idx1, L0_tok_idx2, L0_attn_W_qkv, L0_attn_W_out, L0_ffn_Wr, L0_ffn_w1, L0_ffn_w3,
             L0_ffn_w2, L0_ffn_s1, L0_ffn_s3, L0_ffn_s2)
    arrays = _layout(*[np.asarray(g) for g in given])
    nc = _bacc.Bacc("TRN2", target_bir_lowering=False, num_devices=1)
    ins = {k: nc.dram_tensor(f"in_{k}", a.shape, mybir.dt.from_np(a.dtype), kind="ExternalInput").ap() for k, a in arrays.items()}
    out = nc.dram_tensor("out_tokens", (NT, P, D), F32, kind="ExternalOutput").ap()
    vit_tower(nc, ins, out)
    r = _run(nc, [{f"in_{k}": a for k, a in arrays.items()}], core_ids=[0])
    return r.results[0]["out_tokens"].reshape(B, TOK, D)
```

```python
from contextlib import ExitStack

import numpy as np

import concourse.bass as bass
from concourse import mybir

ALU = mybir.AluOpType
ACT = mybir.ActivationFunctionType
AX = mybir.AxisListType
F32 = mybir.dt.float32
F32R = mybir.dt.float32r
I32 = mybir.dt.int32

P = 128
B = 4
CH = 3
GP = 16
EMB = 64
N1, C1 = 1024, 12
N2, C2 = 256, 48
X12 = 8 * B * C1 + 2 * B * C2
TOK = 256
N = B * TOK
NT = N // P
D = 192
KC = 2
TAIL = D - P
DW = P + 2 * TAIL
PLANES = 3
HEADS = 12
DH = 64
INNER = HEADS * DH
PAIRS = HEADS // 2
LOGIT_GAIN = 8.0
EXPERTS = 8
FF = 768
FM = FF // P
CAP = 320
CT = (P, P, CAP - 2 * P)
SLOTS = EXPERTS * CAP
DROPPED = 8192.0
SHARED_CHUNK = 512
RSQRT_START = float(0x5F3759DF)
RW = DW + 2
INIT_ROWS = 5
TRASH = N
LN_EPS = 1e-5
W13 = 2 * FF


def vit_tower(nc, ins, out):
    with ExitStack() as ctx:
        def sem(name):
            return ctx.enter_context(nc.semaphore(name))

        def sb(name, shape, dt=F32, where=ctx):
            return where.enter_context(nc.sbuf_tensor(name, shape, dt))

        slots_in = nc.dram_tensor("slots_in", [SLOTS, RW], F32, kind="Internal").ap()

        bank = ctx.enter_context(nc.psum_tensor("bank", [P, 8, 512], F32))

        ident = sb("ident", [P, P])
        tri = sb("tri", [P, P])
        iota8 = sb("iota8", [P, NT, EXPERTS])
        h = sb("h", [P, NT, D])
        x2_lo = sb("x2_lo", [P, KC, N], F32R)
        raw = sb("raw", [P, 2, KC * W13])
        ws = sb("ws", [P, PLANES, W13], F32R)
        we = sb("we", [P, 2, PLANES, W13], F32R)
        w2s = sb("w2s", [P, FM, D])
        w2e = sb("w2e", [P, 2, FM, D])
        empty = sb("empty", [P, INIT_ROWS, RW])
        token_no = sb("token_no", [P, NT], I32)
        trash_no = sb("trash_no", [P, INIT_ROWS], I32)
        wr_raw = sb("wr_raw", [P, KC, EXPERTS])
        wr = sb("wr", [P, PLANES, EXPERTS], F32R)
        stats = sb("stats", [P, NT, 6])
        mv = sb("mv", [P, NT, 2])
        ve = sb("ve", [P, NT])
        hv = sb("hv", [P, NT])
        rstd = sb("rstd", [P, NT])
        nt1 = sb("nt1", [P, NT])
        stats2 = sb("stats2", [P, NT, 6])
        mv2 = sb("mv2", [P, NT, 2])

        early = ExitStack()
        wq = sb("wq", [P, PLANES, 3 * INNER], F32R, early)
        wo = sb("wo", [P, PAIRS, D], F32, early)
        kz = sb("kz", [P, 2, 2, TOK], F32, early)
        negmax = sb("negmax", [P, 2, 2], F32, early)
        rowsum = sb("rowsum", [P, 2, 2], F32, early)
        rinv = sb("rinv", [P, 2, 2], F32, early)
        tok = ExitStack()
        idx0 = sb("idx0_s", [P, 2 * GP], I32, tok)
        idx12 = sb("idx12_s", [P, N1 + N2], I32, tok)
        patch_no = sb("patch_no", [P, 8 + 2], F32, tok)
        x12 = sb("x12", [P, X12], F32, tok)
        x12_hi = sb("x12_hi", [P, X12], F32R, tok)
        x12_lo = sb("x12_lo", [P, X12], F32R, tok)
        x2p = sb("x2p", [2 * C2, 2, N2], F32, tok)
        x1p = sb("x1p", [B * C1, N1], F32, tok)
        g0 = sb("g0", [P, 2, GP, B * CH], F32, tok)
        s0 = sb("s0", [P, 2, B, GP * CH], F32, tok)
        s1g = sb("s1g", [P, B, 96], F32, tok)
        s2g = sb("s2g", [P, B, 96], F32, tok)
        w0t = sb("w0t", [GP * CH, EMB], F32, tok)
        w1t = sb("w1t", [96, 2, EMB], F32, tok)
        w2t = sb("w2t", [96, 8, EMB], F32, tok)
        i1m = sb("i1m", [P, 2, 2 * P], F32, tok)
        i2m = sb("i2m", [B * 16, 2, B * P], F32, tok)
        bcat = sb("bcat", [P, 2], F32, tok)
        wft = sb("wft", [P, 2, D], F32, tok)
        x0t = sb("x0t", [GP * CH, 2, B, P], F32, tok)
        x1t = sb("x1t", [96, 2, B, 64], F32, tok)
        x2t = sb("x2t", [96, 8, B, 16], F32, tok)
        o1s = sb("o1s", [P, 2, EMB], F32, tok)
        o2s = sb("o2s", [EMB, EMB], F32, tok)
        cat_a = sb("cat_a", [P, 2, B, P], F32, tok)
        cat_b = sb("cat_b", [EMB + 1, 2, B, P], F32, tok)
        tok.close()
        xn = sb("xn", [P, 2, DW], F32, early)
        xt_hi = sb("xt_hi", [P, KC, TOK], F32R, early)
        xt_lo = sb("xt_lo", [P, KC, TOK], F32R, early)
        qt = sb("qt", [P, 2, TOK], F32, early)
        v = sb("v", [P, 2, INNER], F32, early)
        prob = sb("prob", [P, 2, 2, TOK], F32, early)
        prob_t = sb("prob_t", [P, 2, 2, TOK], F32, early)
        ot = sb("ot", [P, PAIRS, TOK], F32, early)
        early.close()

        late = ctx.enter_context(ExitStack())
        xs = sb("xs", [P, 2, NT, RW], F32, late)
        x2_hi = sb("x2_hi", [P, KC, N], F32R, late)
        hs = sb("hs", [P, FM, N], F32, late)
        gate = sb("gate", [P, 2, 512], F32, late)
        rk = sb("rk", [P, 2, NT, 4], F32, late)
        slot = sb("slot", [P, 2, NT], I32, late)
        base = sb("base", [P, 2, NT], F32, late)
        oh = sb("oh", [P, 2, NT, EXPERTS], F32, late)
        big = [sb(f"rt{i}", [P, NT, EXPERTS], F32, late) for i in range(6)]
        sml = [sb(f"rs{i}", [P, NT], F32, late) for i in range(8)]
        ranking = ExitStack()
        oh_t = sb("oh_t", [P, 2, N], F32R, ranking)
        sc_hi = sb("sc_hi", [P, N], F32R, ranking)
        sc_lo = sb("sc_lo", [P, N], F32R, ranking)
        cmp = sb("cmp", [P, 2, N + P], F32, ranking)
        ranking.close()
        he = sb("he", [P, FM, CAP], F32, late)
        xd = sb("xd", [P, 2, 3, RW], F32, late)
        wn = sb("wn", [P, 2, 3, 2], F32, late)
        xd_hi = sb("xd_hi", [P, KC, CAP], F32R, late)
        xd_lo = sb("xd_lo", [P, KC, CAP], F32R, late)
        ye = sb("ye", [P, 2, 3, D], F32, late)

        consts_in = sem("consts_in")
        idx_in = sem("idx_in")
        wqkv_in = sem("wqkv_in")
        wo_in = sem("wo_in")
        wr_in = sem("wr_in")
        w2s_in = sem("w2s_in")
        idx12_in, x12_in = sem("idx12_in"), sem("x12_in")
        g0_in = [sem("g0_in_half0"), sem("g0_in_half1")]
        raw_in = [sem("raw_in_0"), sem("raw_in_1")]
        w2e_in = [sem("w2e_in_0"), sem("w2e_in_1")]
        xd_in = [sem("xd_in_0"), sem("xd_in_1")]
        empty_ready = sem("empty_ready")
        slots_empty = sem("slots_empty")
        scattered = sem("scattered")
        out_base = sem("out_base")
        added = [sem("added_0"), sem("added_1")]
        x12_split = sem("x12_split")
        picks = sem("picks")
        picked = sem("picked")
        picked_copied = sem("picked_copied")
        turned = sem("turned")
        grouped = sem("grouped")
        grouped_0 = sem("grouped_0")
        dve = sem("dve_step")
        pe_tok = sem("pe_tok")
        tok_copied = sem("tok_copied")
        fused = sem("fused")
        h_in = sem("h_in")
        wq_split = sem("wq_split")
        early_zeroed = sem("early_zeroed")
        xn_ready = sem("xn_ready")
        xt_done = sem("xt_done")
        xt_hi_ready = sem("xt_hi_ready")
        xt_lo_ready = sem("xt_lo_ready")
        proj_done = sem("proj_done")
        q_ready = sem("q_ready")
        k_ready = sem("k_ready")
        vproj_done = sem("vproj_done")
        v_ready = sem("v_ready")
        scores_done = sem("scores_done")
        max_ready = sem("max_ready")
        exp_done = sem("exp_done")
        norm_done = sem("norm_done")
        pt_done = sem("pt_done")
        pt_ready = sem("pt_ready")
        pv_done = sem("pv_done")
        o_ready = sem("o_ready")
        oproj_done = sem("oproj_done")
        resid_done = sem("resid_done")
        pool_hi = sem("pool_hi")
        pool_lo = sem("pool_lo")
        reg_waited = sem("reg_waited")
        raw_split = sem("raw_split")
        xn2_ready = sem("xn2_ready")
        xs1_ready = sem("xs1_ready")
        x2t_done = sem("x2t_done")
        x2_hi_ready = sem("x2_hi_ready")
        x2_lo_ready = sem("x2_lo_ready")
        wr_split = sem("wr_split")
        logits_done = sem("logits_done")
        lsh_ready = sem("lsh_ready")
        ex_ready = sem("ex_ready")
        topk_ready = sem("topk_ready")
        late_zeroed = sem("late_zeroed")
        sct_done = sem("sct_done")
        sct_copied = sem("sct_copied")
        sc_lo_ready = sem("sc_lo_ready")
        rank_rows = sem("rank_rows")
        rank_read = sem("rank_read")
        slot_ready = sem("slot_ready")
        gu_done = sem("gu_done")
        gate_ready = sem("gate_ready")
        hid_ready = sem("hid_ready")
        xdt_done = sem("xdt_done")
        xd_hi_ready = sem("xd_hi_ready")
        xd_lo_ready = sem("xd_lo_ready")
        ye_done = sem("ye_done")
        ye_copied = sem("ye_copied")
        ys_done = sem("ys_done")
        ys_read = sem("ys_read")

        onehot = we[:].rearrange("p a c n -> p (a c n)")

        STEPS = ["t2", "o2", "i2_0", "i2_1", "t1", "o1", "t0_0", "a_0", "t0_1", "a_1"]
        STEP = {s: i + 1 for i, s in enumerate(STEPS)}

        FUSED_AT = (((2, 0), (2, 1), (3, 0), (3, 1)), ((0, 0), (1, 0), (7, 0), (7, 1)))

        NPRE = 6
        X2_BANK = (6, 7, 6, 1)
        MSTEPS = [(c, m) for c in range(N // SHARED_CHUNK) for m in range(FM)]
        GROUPS = [(k, g) for k in range(2) for g in range(NT // 4)]

        block = ctx.enter_context(nc.Block())

        @block.sync
        def _(sp):
            sp.dma_start(idx0[:], ins["idx0"]).then_inc(idx_in, 16)
            sp.dma_start(idx12[:], ins["idx12"].broadcast_to((P, N1 + N2))).then_inc(idx12_in, 16)
            sp.dma_start(patch_no[:], ins["patch_no"]).then_inc(idx12_in, 16)
            sp.dma_start(x12[:], ins["x12"]).then_inc(x12_in, 16)
            raw_qkv = raw[:].rearrange("p a c -> p (a c)")[:, 0:KC * 3 * INNER]
            for dst, src in ((ident, "ident"), (w2t, "w2t"), (w1t, "w1t"), (w0t, "w0t"), (i1m, "i1m"), (i2m, "i2m"),
                             (bcat, "bcat"), (wft, "wft"), (tri, "tri"), (iota8, "iota8"), (token_no, "token_no"),
                             (trash_no, "trash_no")):
                sp.dma_start(dst[:], ins[src]).then_inc(consts_in, 16)
            sp.dma_start(wr_raw[:], ins["wr"]).then_inc(wr_in, 16)
            sp.dma_start(raw_qkv, ins["wqkv"]).then_inc(wqkv_in, 16)
            sp.dma_start(wo[:], ins["wo"]).then_inc(wo_in, 16)
            sp.wait_ge(g0_in[1], 16 * GP)
            sp.dma_start(w2s[:], ins["w2"][EXPERTS]).then_inc(w2s_in, 16)
            for e in range(2):
                sp.dma_start(w2e[:, e], ins["w2"][e]).then_inc(w2e_in[e], 16)
            sp.wait_ge(empty_ready, 2)
            rows = slots_in.rearrange("(q p r) d -> q p (r d)", p=P, r=INIT_ROWS)
            for q in range(SLOTS // (P * INIT_ROWS)):
                sp.dma_start(rows[q], empty[:].rearrange("p r d -> p (r d)")).then_inc(slots_empty, 16)
            sp.dma_start(out[TRASH:TRASH + CAP].rearrange("(p r) d -> p r d", r=INIT_ROWS),
                         empty[0:CAP // INIT_ROWS, :, 0:D]).then_inc(out_base, 16)
            sp.wait_ge(wq_split, 2)
            sp.dma_start(raw[:, 0], ins["w13"][EXPERTS]).then_inc(raw_in[0], 16)
            sp.dma_start(raw[:, 1], ins["w13"][0]).then_inc(raw_in[1], 16)
            sp.wait_ge(raw_split, 1)
            sp.dma_start(raw[:, 0], ins["w13"][1]).then_inc(raw_in[0], 16)
            sp.wait_ge(scattered, 16 * 2 * NT)

            def load_slots(e, par):
                full = slots_in[bass.ds(e * CAP, 2 * P), :].rearrange("(t p) d -> p t d", p=P)
                sp.dma_start(xd[:, par, 0:2, :], full).then_inc(xd_in[par], 16)
                sp.dma_start(xd[0:CT[2], par, 2, :], slots_in[bass.ds(e * CAP + 2 * P, CT[2]), :]).then_inc(xd_in[par], 16)

            def load_up(e, par):
                sp.wait_ge(raw_split, e + 2)
                sp.dma_start(raw[:, 1 - par], ins["w13"][bass.ds(e + 2, 1)].rearrange("o p c -> (o p) c")).then_inc(raw_in[1 - par], 16)

            def load_down(e, par):
                sp.wait_ge(ye_done, 3 * e + 3)
                sp.dma_start(w2e[:, par], ins["w2"][bass.ds(e + 2, 1)].rearrange("o p m d -> (o p) m d")).then_inc(w2e_in[par], 16)

            load_slots(0, 0)
            load_slots(1, 1)
            for t in range(NT):
                sp.wait_ge(ys_read, t + 1)
                sp.dma_start(out[t * P:(t + 1) * P], h[:, t]).then_inc(out_base, 16)
            load_up(0, 0)
            sp.wait_ge(xd_lo_ready, 1)
            load_slots(2, 0)
            load_up(1, 1)
            load_down(0, 0)
            sp.wait_ge(xd_lo_ready, 2)
            load_slots(3, 1)
            with sp.Fori(1, EXPERTS // 2 - 1) as ee:
                for par in range(2):
                    e = 2 * ee + par
                    load_up(e, par)
                    load_down(e - 1, 1 - par)
                    sp.wait_ge(xd_lo_ready, e + 1)
                    load_slots(e + 2, par)
            load_down(EXPERTS - 3, 1)

        @block.gpsimd
        def _(pool):
            nc.gpsimd.memset(empty[:], 0.0).then_inc(empty_ready, 1)
            pool.wait_ge(idx_in, 16)
            for half in range(2):
                for g in range(GP):
                    c = half * GP + g
                    nc.gpsimd.indirect_dma_start(out=g0[:, half, g, :], out_offset=None, in_=ins["x0"],
                                                 in_offset=bass.IndirectOffsetOnAxis(ap=idx0[:, c:c + 1], axis=0)).then_inc(g0_in[half], 16)

            def split(n, dst):
                src = raw[:, n % 2]
                pool.wait_ge(raw_in[n % 2], 16 * (n // 2 + 1))
                nc.gpsimd.tensor_scalar(dst[:, 0:2].rearrange("p c n -> p (c n)"), src, 1.0, 0.0, ALU.mult, ALU.add).then_inc(pool_hi, 1)
                pool.wait_ge(pool_hi, n + 1)
                nc.gpsimd.tensor_tensor(dst[:, 2], src[:, 0:W13], dst[:, 0].bitcast(F32), ALU.subtract).then_inc(pool_lo, 1)
                pool.wait_ge(pool_lo, n + 1)
                nc.gpsimd.tensor_tensor(dst[TAIL:P, 1], src[TAIL:P, W13:2 * W13], dst[TAIL:P, 1].bitcast(F32), ALU.subtract).then_inc(raw_split, 1)
                pool.wait_ge(raw_split, n + 1)

            pool.wait_ge(g0_in[0], 16 * GP)
            pool.wait_ge(g0_in[1], 16 * GP)
            split(0, ws[:])
            pool.wait_ge(picked, 3)
            split(1, we[:, 0])
            split(2, we[:, 1])
            pool.wait_ge(resid_done, NT)
            nc.gpsimd.memset(sc_hi[:].bitcast(F32), 0.0).then_inc(late_zeroed, 1)
            nc.gpsimd.memset(sc_lo[:].bitcast(F32), 0.0).then_inc(late_zeroed, 1)
            nc.gpsimd.memset(oh_t[:].bitcast(F32), 0.0).then_inc(late_zeroed, 1)
            pool.wait_ge(slots_empty, 16 * SLOTS // (P * INIT_ROWS))
            for i, (k, g) in enumerate(GROUPS):
                pool.wait_ge(slot_ready, i + 1)
                if k == 1 and g == 0:
                    pool.wait_ge(xs1_ready, 1)
                for t in range(4 * g, 4 * g + 4):
                    nc.gpsimd.indirect_dma_start(out=slots_in, out_offset=bass.IndirectOffsetOnAxis(ap=slot[:, k, t:t + 1], axis=0),
                                                 in_=xs[:, k, t, :], in_offset=None, bounds_check=SLOTS - 1,
                                                 oob_is_err=False).then_inc(scattered, 16)

            def add_rows(e, par, before=None):
                if before is not None:
                    pool.wait_ge(added[1 - par], before)
                for s, rows in enumerate(CT):
                    pool.wait_ge(ye_copied, 3 * e + s + 1)
                    pool.sem_inc(reg_waited, 1)
                    nc.gpsimd.indirect_dma_start(out=out, out_offset=bass.IndirectOffsetOnAxis(ap=wn[0:rows, par, s, 1:2].bitcast(I32), axis=0),
                                                 in_=ye[0:rows, par, s, :], in_offset=None,
                                                 compute_op=ALU.add).then_inc(added[par], 16)

            def next_hi(e, par, landed):
                pool.wait_ge(raw_in[1 - par], 16 * landed)
                pool.wait_ge(gu_done, len(MSTEPS) + FM * e + FM)
                pool.sem_inc(reg_waited, 1)
                nc.gpsimd.tensor_scalar(we[:, par, 0:2].rearrange("p c n -> p (c n)"), raw[:, 1 - par], 1.0, 0.0, ALU.mult, ALU.add).then_inc(pool_hi, 1)

            next_hi(0, 0, 2)
            pool.wait_ge(out_base, 16 * (NT + 1))
            add_rows(0, 0)
            next_hi(1, 1, 3)
            add_rows(1, 1, 48)
            with pool.Fori(1, EXPERTS // 2 - 1) as ee:
                next_hi(2 * ee, 0, ee + 2)
                add_rows(2 * ee, 0, 48 * ee)
                next_hi(2 * ee + 1, 1, ee + 3)
                add_rows(2 * ee + 1, 1, 48 * (ee + 1))
            add_rows(EXPERTS - 2, 0, 48 * (EXPERTS // 2 - 1))
            add_rows(EXPERTS - 1, 1, 48 * EXPERTS // 2)
            pool.wait_ge(added[1], 48 * EXPERTS // 2)

        @block.tensor
        def _(pe):
            mm = nc.tensor.matmul

            def product(dst, w, x_hi, x_lo):
                mm(dst, w[:, 2], x_hi[:, 0], start=True, stop=False)
                mm(dst, w[:, 0], x_lo[:, 0], start=False, stop=False)
                mm(dst, w[:, 1], x_lo[:, 1], start=False, stop=False)
                mm(dst, w[:, 1], x_hi[:, 1], start=False, stop=False)
                return mm(dst, w[:, 0], x_hi[:, 0], start=False, stop=True)

            def product_by_token(dst, x_hi, x_lo, w):
                mm(dst, x_hi[:, 0], w[:, 2], start=True, stop=False)
                mm(dst, x_lo[:, 0], w[:, 0], start=False, stop=False)
                mm(dst, x_lo[:, 1], w[:, 1], start=False, stop=False)
                mm(dst, x_hi[:, 1], w[:, 1], start=False, stop=False)
                return mm(dst, x_hi[:, 0], w[:, 0], start=False, stop=True)

            pe.wait_ge(x12_split, 2)
            pe.wait_ge(picks, 1)
            for q in range(2):
                for i, part in enumerate((x12_lo, x12_hi)):
                    for k in range(2):
                        at = 8 * B * C1 + (k * B + 2 * q) * C2
                        t = mm(bank[0:2 * C2, 6, q * N2:(q + 1) * N2], part[:, at:at + 2 * C2], onehot[:, 8 * N1 + k * N2:8 * N1 + (k + 1) * N2],
                               start=(i == 0 and k == 0), stop=(i == 1 and k == 1))
            t.then_inc(picked, 1)
            pe.wait_ge(consts_in, 16 * 12)
            pe.wait_ge(picked_copied, 1)
            for q in range(2):
                for j in range(2):
                    t = nc.tensor.transpose(bank[:, 7, (2 * q + j) * 2 * C2:(2 * q + j + 1) * 2 * C2], x2p[:, q, j * P:(j + 1) * P],
                                            ident[0:2 * C2, 0:2 * C2])
            t.then_inc(turned, 1)
            pe.wait_ge(grouped, 1)
            for b in range(B):
                t = nc.tensor.transpose(bank[0:96, 0, b * P:(b + 1) * P], s2g[:, b], ident[:])
            t.then_inc(pe_tok, 1)
            pe.wait_ge(tok_copied, STEP["t2"])
            for g in range(8):
                t = mm(bank[0:EMB, 2, 0:EMB], x2t[:, g].rearrange("p b t -> p (b t)"), w2t[:, g], start=(g == 0), stop=(g == 7))
            t.then_inc(pe_tok, 1)
            pe.wait_ge(tok_copied, STEP["o2"])
            for half in range(2):
                mm(bank[0:EMB, 6 + half, :], o2s[:], i2m[:, half], start=True, stop=True).then_inc(pe_tok, 1)
            pe.wait_ge(picks, 2)
            for half in range(2):
                for i, part in enumerate((x12_lo, x12_hi)):
                    for k in range(8):
                        t = mm(bank[0:B * C1, 4 + half, :], part[:, k * B * C1:(k + 1) * B * C1],
                               onehot[:, k * N1 + half * 512:k * N1 + (half + 1) * 512], start=(i == 0 and k == 0), stop=(i == 1 and k == 7))
                t.then_inc(picked, 1)
            for half in range(2):
                pe.wait_ge(picked_copied, 2 + half)
                for j in range(4 * half, 4 * half + 4):
                    t = nc.tensor.transpose(bank[:, 0, j * B * C1:(j + 1) * B * C1], x1p[:, j * P:(j + 1) * P], ident[0:B * C1, 0:B * C1])
            t.then_inc(turned, 1)
            pe.wait_ge(grouped, 2)
            for b in range(B):
                t = nc.tensor.transpose(bank[0:96, 1, b * P:(b + 1) * P], s1g[:, b], ident[:])
            t.then_inc(pe_tok, 1)
            pe.wait_ge(tok_copied, STEP["t1"])
            for q in range(2):
                for c in range(2):
                    t = mm(bank[:, 3, q * EMB:(q + 1) * EMB], x1t[:, c, 2 * q:2 * q + 2].rearrange("p b t -> p (b t)"), w1t[:, c],
                           start=(c == 0), stop=(c == 1))
            t.then_inc(pe_tok, 1)
            pe.wait_ge(tok_copied, STEP["o1"])
            for half in range(2):
                for q in range(2):
                    mm(bank[EMB:P, 4 + half, q * TOK:(q + 1) * TOK], o1s[:, q], i1m[:, half], start=True, stop=True)

            def turn_half(half):
                pe.wait_ge(grouped_0, half + 1)
                for b in range(B):
                    t = nc.tensor.transpose(bank[0:GP * CH, half, b * P:(b + 1) * P], s0[:, half, b], ident[:])
                t.then_inc(pe_tok, 1)

            def level_0(half):
                pe.wait_ge(tok_copied, STEP[f"t0_{half}"])
                mm(bank[0:EMB, 4 + half, :], w0t[:], x0t[:, half].rearrange("p b t -> p (b t)"),
                   start=True, stop=True).then_inc(pe_tok, 1)

            def fuse(half, b, done):
                at = FUSED_AT[half][b]
                dst = bank[:, at[0], at[1] * D:(at[1] + 1) * D]
                mm(dst, cat_a[:, half, b], wft[:, 0], start=True, stop=False)
                t = mm(dst, cat_b[:, half, b], wft[0:EMB + 1, 1], start=False, stop=True)
                if done:
                    t.then_inc(fused, 1)

            turn_half(0)
            level_0(0)
            pe.wait_ge(tok_copied, STEP["a_0"])
            fuse(0, 0, False)
            fuse(0, 1, True)
            turn_half(1)
            fuse(0, 2, False)
            fuse(0, 3, True)
            level_0(1)
            pe.wait_ge(tok_copied, STEP["a_1"])
            fuse(1, 0, True)
            fuse(1, 1, True)
            fuse(1, 2, False)
            fuse(1, 3, True)

            def turn_x(b):
                pe.wait_ge(xn_ready, b + 1)
                for c in range(KC):
                    for half in range(2):
                        t = nc.tensor.transpose(bank[:, 6, c * TOK + half * P:c * TOK + (half + 1) * P],
                                                xn[:, half, c * P:(c + 1) * P], ident[:])
                t.then_inc(xt_done, 1)

            def project(col):
                product(bank[:, 4, 0:TOK], wq[:, :, col:col + P], xt_hi, xt_lo).then_inc(proj_done, 1)

            def project_q(b, p, first=False):
                if not first:
                    pe.wait_ge(k_ready, PAIRS * b + p)
                if p == 0:
                    pe.wait_ge(xt_lo_ready, b + 1)
                project(p * P)

            def project_k(b, p):
                pe.wait_ge(q_ready, PAIRS * b + p + 1)
                project(INNER + p * P)

            def project_v(side, sh, bk):
                cols = slice(2 * INNER + side * (INNER // 2), 2 * INNER + (side + 1) * (INNER // 2))
                rows = slice(sh * P, (sh + 1) * P)
                product_by_token(bank[:, bk, 0:INNER // 2], xt_hi[:, :, rows], xt_lo[:, :, rows], wq[:, :, cols]).then_inc(vproj_done, 1)

            def scores(b, hd):
                u = HEADS * b + hd
                if hd % 2 == 0:
                    pe.wait_ge(q_ready, PAIRS * b + hd // 2 + 1)
                    pe.wait_ge(k_ready, PAIRS * b + hd // 2 + 1)
                if hd >= 2:
                    pe.wait_ge(exp_done, u - 1)
                for half in range(2):
                    t = mm(bank[:, hd % 2, half * TOK:(half + 1) * TOK], qt[:, hd // 2 % 2, half * P:(half + 1) * P],
                           kz[:, hd // 2 % 2, hd % 2], start=True, stop=True)
                t.then_inc(scores_done, 1)

            def turn_probs(b, hd):
                u = HEADS * b + hd
                pe.wait_ge(norm_done, u + 1)
                if hd >= 2:
                    pe.wait_ge(pt_ready, u - 1)
                for sh in range(2):
                    for half in range(2):
                        t = nc.tensor.transpose(bank[:, 2 + hd % 2, sh * TOK + half * P:sh * TOK + (half + 1) * P],
                                                prob[:, hd % 2, half, sh * P:(sh + 1) * P], ident[:])
                t.then_inc(pt_done, 1)

            def values(b, hd):
                u = HEADS * b + hd
                pe.wait_ge(pt_ready, u + 1)
                if hd == 0:
                    pe.wait_ge(v_ready, 4 * b + 2)
                if hd == HEADS // 2:
                    pe.wait_ge(v_ready, 4 * b + 4)
                if hd % 2 == 0 and hd:
                    pe.wait_ge(o_ready, PAIRS * b + hd // 2)
                rows = slice(hd % 2 * DH, (hd % 2 + 1) * DH)
                for sh in range(2):
                    t = mm(bank[rows, 5, 0:TOK], v[:, sh, hd * DH:(hd + 1) * DH], prob_t[:, hd % 2, sh],
                           start=(sh == 0), stop=(sh == 1))
                t.then_inc(pv_done, 1)

            def project_out(b, half, bk):
                pe.wait_ge(o_ready, PAIRS * b + PAIRS)
                for p in range(PAIRS):
                    t = mm(bank[:, bk, 0:D], ot[:, p, half * P:(half + 1) * P], wo[:, p], start=(p == 0), stop=(p == PAIRS - 1))
                t.then_inc(oproj_done, 1)

            turn_x(0)
            pe.wait_ge(wq_split, 2)
            pe.wait_ge(early_zeroed, 1)
            project_q(0, 0, first=True)
            pe.wait_ge(h_in, 5)
            project_v(0, 0, 7)
            project_k(0, 0)
            pe.wait_ge(xt_lo_ready, 1)
            project_v(0, 1, 6)
            project_q(0, 1)
            pe.wait_ge(wo_in, 16)
            project_k(0, 1)
            scores(0, 0)

            def image(b, last):
                for hd in range(HEADS):
                    if hd < HEADS - 1:
                        scores(b, hd + 1)
                    elif not last:
                        scores(b + 1, 0)
                    if hd < HEADS - 4:
                        (project_k if hd % 2 else project_q)(b, hd // 2 + 2)
                    elif not last:
                        (project_k if hd % 2 else project_q)(b + 1, hd // 2 - 4)
                    elif hd > HEADS - 4:
                        turn_x2(hd - (HEADS - 3))
                    if hd == 3:
                        project_v(1, 1, 7)
                    if hd == 7 and not last:
                        pe.wait_ge(v_ready, 4 * b + 4)
                        turn_x(b + 1)
                    turn_probs(b, hd)
                    if hd == 1:
                        pe.wait_ge(v_ready, 4 * b + 2)
                        project_v(1, 0, 6)
                    if hd > 0:
                        values(b, hd - 1)
                    if hd == 9 and not last:
                        project_v(0, 0, 7)
                    if hd == 10 and not last:
                        project_v(0, 1, 6)
                values(b, HEADS - 1)
                if not last:
                    pe.wait_ge(v_ready, 4 * b + 6)
                else:
                    pe.wait_ge(x2_lo_ready, 3)
                project_out(b, 0, 7)
                project_out(b, 1, 6)

            def turn_x2(q):
                pe.wait_ge(xn2_ready, 2 * q + 2)
                if q == 0:
                    pe.wait_ge(v_ready, 4 * B)
                if q == 2:
                    pe.wait_ge(x2_lo_ready, 1)
                for c in range(KC):
                    for i in range(2):
                        t = nc.tensor.transpose(bank[:, X2_BANK[q], c * TOK + i * P:c * TOK + (i + 1) * P],
                                                xs[:, 0, 2 * q + i, c * P:(c + 1) * P], ident[:])
                t.then_inc(x2t_done, 1)

            with pe.Fori(0, B - 1) as b:
                image(b, False)
            image(B - 1, True)

            def logits(tiles):
                for t in tiles:
                    rows = slice(t * P, (t + 1) * P)
                    x = product_by_token(bank[:, 0, t * EXPERTS:(t + 1) * EXPERTS], x2_hi[:, :, rows], x2_lo[:, :, rows], wr)
                return x


            def hidden(n, weights, m, x_hi, x_lo, cols, w):
                pair = 4 + 2 * (m % 2)
                if not (isinstance(n, int) and n < 2):
                    pe.wait_ge(hid_ready, n - 1)
                for half in range(2):
                    at = half * FF + m * P
                    t = product(bank[:, pair + half, 0:w], weights[:, :, at:at + P], x_hi[:, :, cols], x_lo[:, :, cols])
                t.then_inc(gu_done, 1)

            def shared_hidden(n):
                c, m = MSTEPS[n]
                hidden(n, ws, m, x2_hi, x2_lo, slice(c * SHARED_CHUNK, (c + 1) * SHARED_CHUNK), SHARED_CHUNK)

            pe.wait_ge(raw_split, 1)
            pe.wait_ge(wr_split, 2)
            pe.wait_ge(x2_lo_ready, 3)
            logits(range(NT - 2))
            shared_hidden(0)
            pe.wait_ge(resid_done, NT)
            shared_hidden(1)
            turn_x2(3)
            shared_hidden(2)
            pe.wait_ge(x2_lo_ready, 4)
            logits(range(NT - 2, NT)).then_inc(logits_done, 1)
            for n in range(3, NPRE):
                shared_hidden(n)
            pe.wait_ge(topk_ready, 1)
            for src, b0, cnt in ((big[4], 0, 1), (oh[:, 0], 2, 2)):
                for t in range(NT):
                    x = nc.tensor.transpose(bank[0:EXPERTS, b0 + t // 4, t % 4 * P:(t % 4 + 1) * P], src[:, t, :], ident[:])
                x.then_inc(sct_done, 1)
            pe.wait_ge(sc_lo_ready, 1)
            for t in range(NT):
                x = nc.tensor.transpose(bank[0:EXPERTS, t // 4, t % 4 * P:(t % 4 + 1) * P], oh[:, 1, t, :], ident[:])
            x.then_inc(sct_done, 1)

            n = NPRE
            pe.wait_ge(late_zeroed, 3)
            for i in range(2 * NT):
                k, t = divmod(i, NT)
                b0 = 2 - 2 * (i % 2)
                if i < 2:
                    pe.wait_ge(sct_copied, 2 + i)
                else:
                    pe.wait_ge(rank_read, i - 1)
                for half in range(2):
                    dst = bank[:, b0 + half, :]
                    cols = slice(half * 512, (half + 1) * 512)
                    mm(dst, oh_t[:, k, t * P:(t + 1) * P], sc_lo[:, cols], start=True, stop=False)
                    x = mm(dst, oh_t[:, k, t * P:(t + 1) * P], sc_hi[:, cols], start=False, stop=True)
                x.then_inc(rank_rows, 1)
                if i % 2 == 1 and n < len(MSTEPS):
                    shared_hidden(n)
                    n += 1
            while n < len(MSTEPS):
                shared_hidden(n)
                n += 1

            pe.wait_ge(w2s_in, 16)
            pe.wait_ge(hid_ready, len(MSTEPS))
            pe.wait_ge(rank_read, 2 * NT)
            for t in range(NT):
                if t >= 4:
                    pe.wait_ge(ys_read, t - 3)
                for m in range(FM):
                    x = mm(bank[:, t % 4, 0:D], hs[:, m, t * P:(t + 1) * P], w2s[:, m], start=(m == 0), stop=(m == FM - 1))
                x.then_inc(ys_done, 1)

            def turn_slots(e, par, first=False):
                if first:
                    pe.wait_ge(ys_read, NT)
                else:
                    pe.wait_ge(xd_lo_ready, e)
                pe.wait_ge(xd_in[par], 32 * (e // 2 + 1) if isinstance(e, int) else 32 * (e_pair[0] + 1))
                for c in range(KC):
                    for s, rows in enumerate(CT):
                        t = nc.tensor.transpose(bank[:, c, s * P:s * P + rows], xd[0:rows, par, s, c * P:(c + 1) * P],
                                                ident[0:rows, 0:rows])
                t.then_inc(xdt_done, 1)

            e_pair = [0]

            def expert(e, par, last):
                pe.wait_ge(xd_lo_ready, e + 1)
                pe.wait_ge(raw_split, e + 2)
                for m in range(FM):
                    hidden(len(MSTEPS) + FM * e + m, we[:, par], m, xd_hi, xd_lo, slice(0, CAP), CAP)
                if not last:
                    if par == 1:
                        e_pair[0] = e_pair[0] + 1
                    turn_slots(e + 1, 1 - par)
                pe.wait_ge(w2e_in[par], 16 * (e_pair_now[0] + 1))
                pe.wait_ge(hid_ready, len(MSTEPS) + FM * e + FM)
                for s, rows in enumerate(CT):
                    if not (isinstance(e, int) and 3 * e + s < 2):
                        pe.wait_ge(ye_copied, 3 * e + s - 1)
                    for m in range(FM):
                        t = mm(bank[0:rows, 2 + (3 * par + s) % 2, 0:D], he[:, m, s * P:s * P + rows], w2e[:, par, m],
                               start=(m == 0), stop=(m == FM - 1))
                    t.then_inc(ye_done, 1)

            turn_slots(0, 0, first=True)
            e_pair_now = [0]
            expert(0, 0, False)
            expert(1, 1, False)
            with pe.Fori(1, EXPERTS // 2 - 1) as ee:
                e_pair[0] = ee
                e_pair_now[0] = ee
                expert(2 * ee, 0, False)
                expert(2 * ee + 1, 1, False)
            e_pair[0] = e_pair_now[0] = EXPERTS // 2 - 1
            expert(EXPERTS - 2, 0, False)
            expert(EXPERTS - 1, 1, True)

        @block.scalar
        def _(sc):
            fn = nc.scalar.activation

            def copied(step, *ops):
                sc.wait_ge(pe_tok, STEP[step])
                for x in ops:
                    last = x()
                last.then_inc(tok_copied, 1)

            def grouped_rows(dst, src, g):
                return fn(dst.rearrange("p b (g c) -> p g b c", g=g), src.rearrange("p (g b c) -> p g b c", g=g, b=dst.shape[1]), ACT.Copy)

            sc.wait_ge(picked, 1)
            fn(x2p[:].rearrange("p q n -> p (q n)"), bank[0:2 * C2, 6, :], ACT.Copy).then_inc(picked_copied, 1)
            sc.wait_ge(turned, 1)
            for q in range(2):
                x = grouped_rows(s2g[:, 2 * q:2 * q + 2], bank[:, 7, q * 4 * C2:(q + 1) * 4 * C2], 2)
            x.then_inc(grouped, 1)
            copied("t2", lambda: fn(x2t[:].rearrange("p g b t -> p b g t"), bank[0:96, 0, :].rearrange("p (b g t) -> p b g t", b=B, g=8), ACT.Copy))
            copied("o2", lambda: fn(o2s[:], bank[0:EMB, 2, 0:EMB], ACT.Copy))
            sc.wait_ge(consts_in, 16 * 12)
            for half in range(2):
                copied(f"i2_{half}", lambda: fn(cat_b[0:EMB, half].rearrange("p b t -> p (b t)"), bank[0:EMB, 6 + half, :],
                                                ACT.Identity, bias=bcat[0:EMB, 1:2]))
            for half in range(2):
                sc.wait_ge(picked, 2 + half)
                fn(x1p[:, half * 512:(half + 1) * 512], bank[0:B * C1, 4 + half, :], ACT.Copy).then_inc(picked_copied, 1)
            sc.wait_ge(turned, 2)
            grouped_rows(s1g[:], bank[:, 0, 0:8 * B * C1], 8).then_inc(grouped, 1)
            copied("t1", lambda: fn(x1t[:].rearrange("p c b t -> p b c t"), bank[0:96, 1, :].rearrange("p (b c t) -> p b c t", b=B, c=2), ACT.Copy))
            copied("o1", lambda: fn(o1s[:].rearrange("p q e -> p (q e)"), bank[:, 3, 0:2 * EMB], ACT.Copy))

            def copy_half(half):
                copied(f"t0_{half}", lambda: fn(x0t[:, half].rearrange("p b t -> p (b t)"), bank[0:GP * CH, half, :], ACT.Copy))

            def copy_level_0(half):
                copied(f"a_{half}", lambda: fn(cat_a[:, half].rearrange("p b t -> p (b t)"), bank[:, 4 + half, :],
                                               ACT.Identity, bias=bcat[:, 0:1]))

            def copy_h(n, half, b, images):
                bk, place = FUSED_AT[half][b]
                sc.wait_ge(fused, n)
                fn(h[:].rearrange("p (b i) d -> p i b d", i=2)[:, half, b:b + images],
                   bank[:, bk, place * D:(place + images) * D].rearrange("p (b d) -> p b d", b=images), ACT.Copy).then_inc(h_in, 1)

            copy_half(0)
            copy_level_0(0)
            copy_h(1, 0, 0, 2)
            copy_half(1)
            copy_h(2, 0, 2, 2)
            copy_level_0(1)
            copy_h(3, 1, 0, 1)
            copy_h(4, 1, 1, 1)
            copy_h(5, 1, 2, 2)

            def copy_x(b):
                sc.wait_ge(xt_done, b + 1)
                fn(xt_hi[:].rearrange("p c t -> p (c t)"), bank[:, 6, :], ACT.Copy).then_inc(xt_hi_ready, 1)

            def copy_q(b, p):
                sc.wait_ge(proj_done, HEADS * b + 2 * p + 1)
                fn(qt[:, p % 2], bank[:, 4, 0:TOK], ACT.Copy, scale=LOGIT_GAIN).then_inc(q_ready, 1)

            def copy_v(n, side, sh, bk):
                sc.wait_ge(vproj_done, n)
                fn(v[:, sh, side * (INNER // 2):(side + 1) * (INNER // 2)], bank[:, bk, 0:INNER // 2], ACT.Copy).then_inc(v_ready, 1)

            def exps(b, hd):
                sc.wait_ge(max_ready, HEADS * b + hd + 1)
                for half in range(2):
                    last = fn(prob[:, hd % 2, half], bank[:, hd % 2, half * TOK:(half + 1) * TOK], ACT.Exp,
                              bias=negmax[:, hd % 2, half:half + 1], accum_out=rowsum[:, hd % 2, half:half + 1])
                last.then_inc(exp_done, 1)

            def copy_probs(b, hd):
                u = HEADS * b + hd
                sc.wait_ge(pt_done, u + 1)
                if hd >= 2:
                    sc.wait_ge(pv_done, u - 1)
                fn(prob_t[:, hd % 2].rearrange("p s t -> p (s t)"), bank[:, 2 + hd % 2, :], ACT.Copy).then_inc(pt_ready, 1)

            def copy_o(b, p):
                sc.wait_ge(pv_done, HEADS * b + 2 * p + 2)
                fn(ot[:, p], bank[:, 5, 0:TOK], ACT.Copy).then_inc(o_ready, 1)

            copy_x(0)
            copy_q(0, 0)
            copy_v(1, 0, 0, 7)
            copy_v(2, 0, 1, 6)
            copy_q(0, 1)
            exps(0, 0)

            def image(b, last):
                for hd in range(HEADS):
                    if hd < HEADS - 1:
                        exps(b, hd + 1)
                    elif not last:
                        exps(b + 1, 0)
                    if hd in (0, 2, 4, 6):
                        copy_q(b, hd // 2 + 2)
                    if hd in (8, 10) and not last:
                        copy_q(b + 1, hd // 2 - 4)
                    if hd > HEADS - 4 and last:
                        copy_x2(hd - (HEADS - 3))
                    if hd == 3:
                        copy_v(4 * b + 4, 1, 1, 7)
                    if hd == 7 and not last:
                        sc.wait_ge(proj_done, HEADS * (b + 1))
                        copy_x(b + 1)
                    copy_probs(b, hd)
                    if hd == 1:
                        copy_v(4 * b + 3, 1, 0, 6)
                    if hd >= 2 and hd % 2 == 0:
                        copy_o(b, hd // 2 - 1)
                    if hd == 9 and not last:
                        sc.wait_ge(pv_done, HEADS * b + HEADS // 2)
                        copy_v(4 * b + 5, 0, 0, 7)
                    if hd == 10 and not last:
                        copy_v(4 * b + 6, 0, 1, 6)
                copy_o(b, PAIRS - 1)

            def copy_x2(q):
                sc.wait_ge(x2t_done, q + 1)
                fn(x2_hi[:, :, q * TOK:(q + 1) * TOK], bank[:, X2_BANK[q], :].rearrange("p (c t) -> p c t", c=KC), ACT.Copy).then_inc(x2_hi_ready, 1)

            with sc.Fori(0, B - 1) as b:
                image(b, False)
            image(B - 1, True)

            def silu(n, m, w):
                sc.wait_ge(gu_done, n + 1)
                if not (isinstance(n, int) and n < 2):
                    sc.wait_ge(hid_ready, n - 1)
                fn(gate[:, m % 2, 0:w], bank[:, 4 + 2 * (m % 2), 0:w], ACT.Silu).then_inc(gate_ready, 1)

            for n in range(NPRE):
                silu(n, MSTEPS[n][1], SHARED_CHUNK)
                if n == 1:
                    copy_x2(3)
                    sc.wait_ge(xn2_ready, NT)
                    fn(xs[:, 1, :, 0:DW], xs[:, 0, :, 0:DW], ACT.Copy).then_inc(xs1_ready, 1)
                if n == 2:
                    sc.wait_ge(lsh_ready, 1)
                    fn(big[1][:], big[0][:], ACT.Exp).then_inc(ex_ready, 1)
            sc.wait_ge(late_zeroed, 3)
            sc.wait_ge(sct_done, 1)
            fn(sc_hi[0:EXPERTS], bank[0:EXPERTS, 0:2, :].rearrange("p a c -> p (a c)"), ACT.Copy).then_inc(sct_copied, 1)
            sc.wait_ge(sct_done, 2)
            fn(oh_t[0:EXPERTS, 0], bank[0:EXPERTS, 2:4, :].rearrange("p a c -> p (a c)"), ACT.Copy).then_inc(sct_copied, 1)
            sc.wait_ge(sct_done, 3)
            fn(oh_t[0:EXPERTS, 1], bank[0:EXPERTS, 0:2, :].rearrange("p a c -> p (a c)"), ACT.Copy).then_inc(sct_copied, 1)
            for n in range(NPRE, len(MSTEPS)):
                silu(n, MSTEPS[n][1], SHARED_CHUNK)

            def split_slots(e):
                sc.wait_ge(xdt_done, e + 1)
                fn(xd_hi[:], bank[:, 0:KC, 0:CAP], ACT.Copy).then_inc(xd_hi_ready, 1)

            def copy_out(e, par, stored=None):
                if stored is not None:
                    sc.wait_ge(added[par], stored)
                for s, rows in enumerate(CT):
                    sc.wait_ge(ye_done, 3 * e + s + 1)
                    fn(ye[0:rows, par, s], bank[0:rows, 2 + (3 * par + s) % 2, 0:D], ACT.Copy,
                       scale=wn[0:rows, par, s, 0:1]).then_inc(ye_copied, 1)

            def expert(e, par, last, stored=None):
                for m in range(FM):
                    silu(len(MSTEPS) + FM * e + m, m, CAP)
                if not last:
                    split_slots(e + 1)
                copy_out(e, par, stored)

            split_slots(0)
            expert(0, 0, False)
            expert(1, 1, False)
            with sc.Fori(1, EXPERTS // 2 - 1) as ee:
                expert(2 * ee, 0, False, 48 * ee)
                expert(2 * ee + 1, 1, False, 48 * ee)
            expert(EXPERTS - 2, 0, False, 48 * (EXPERTS // 2 - 1))
            expert(EXPERTS - 1, 1, True, 48 * (EXPERTS // 2 - 1))

        @block.vector
        def _(vec):
            ts, tt, stt = nc.vector.tensor_scalar, nc.vector.tensor_tensor, nc.vector.scalar_tensor_tensor
            steps = [0]
            offset = [0]

            def step(x):
                x.then_inc(dve, 1)
                steps[0] += 1
                vec.wait_ge(dve, offset[0] + steps[0])

            vec.wait_ge(x12_in, 16)
            nc.vector.tensor_copy(x12_hi[:], x12[:]).then_inc(x12_split, 1)
            vec.wait_ge(x12_split, 1)
            tt(x12_lo[:], x12[:], x12_hi[:].bitcast(F32), ALU.subtract).then_inc(x12_split, 1)
            vec.wait_ge(idx12_in, 32)
            for k in range(2):
                x = ts(onehot[:, N1 * 8 + k * N2:N1 * 8 + (k + 1) * N2], idx12[:, N1:], patch_no[:, 8 + k:9 + k], None, ALU.is_equal)
            x.then_inc(picks, 1)
            for k in range(8):
                x = ts(onehot[:, k * N1:(k + 1) * N1], idx12[:, 0:N1], patch_no[:, k:k + 1], None, ALU.is_equal)
            x.then_inc(picks, 1)

            nc.vector.memset(cat_b[EMB:EMB + 1].rearrange("p h b t -> p (h b t)"), 1.0)
            nc.vector.memset(kz[:].rearrange("p a b t -> p (a b t)"), 0.0).then_inc(early_zeroed, 1)
            def split_lo(src, dst, cols, signal):
                tt(dst[:, 2, cols], src[:, 0, cols], dst[:, 0, cols].bitcast(F32), ALU.subtract)
                tt(dst[TAIL:P, 1, cols], src[TAIL:P, 1, cols], dst[TAIL:P, 1, cols].bitcast(F32), ALU.subtract).then_inc(signal, 1)

            vec.wait_ge(wr_in, 16)
            nc.vector.tensor_copy(wr[:, 0:KC], wr_raw[:]).then_inc(wr_split, 1)
            vec.wait_ge(wr_split, 1)
            split_lo(wr_raw, wr, slice(0, EXPERTS), wr_split)
            vec.wait_ge(empty_ready, 1)
            vec.wait_ge(consts_in, 16 * 12)
            nc.vector.tensor_copy(empty[:, :, DW + 1].bitcast(I32), trash_no[:]).then_inc(empty_ready, 1)
            raw_qkv = raw[:].rearrange("p a c -> p (a c)")[:, 0:KC * 3 * INNER].rearrange("p (c n) -> p c n", c=KC)
            vec.wait_ge(wqkv_in, 16)
            nc.vector.tensor_copy(wq[:, 0:KC], raw_qkv).then_inc(wq_split, 1)
            vec.wait_ge(wq_split, 1)
            split_lo(raw_qkv, wq, slice(0, 3 * INNER), wq_split)

            def regroup(half):
                vec.wait_ge(g0_in[half], 16 * GP)
                nc.vector.tensor_copy(s0[:, half].rearrange("p b (g c) -> p b g c", g=GP),
                                      g0[:, half].rearrange("p g (b c) -> p b g c", b=B)).then_inc(grouped_0, 1)

            def inv_std_steps(m, a, n):
                cols = slice(a, a + n)
                var, y, t, half_v = ve[:, cols], rstd[:, cols], nt1[:, cols], hv[:, cols]
                yield ts(var, m[:, cols, 1], LN_EPS, None, ALU.add)
                yield ts(y.bitcast(I32), var.bitcast(I32), 1, None, ALU.arith_shift_right)
                yield ts(y.bitcast(I32), y.bitcast(I32), -1.0, RSQRT_START, ALU.mult, ALU.add)
                yield ts(half_v, var, -0.5, None, ALU.mult)
                for _ in range(3):
                    yield tt(t, y, y, ALU.mult)
                    yield tt(t, t, half_v, ALU.mult)
                    yield stt(y, t, 1.5, y, ALU.add, ALU.mult)

            def inv_std(m, a, n):
                for x in inv_std_steps(m, a, n):
                    step(x)

            def half_moments(half, images):
                for b in images:
                    c = half * B + b
                    step(nc.vector.bn_stats(stats[:, c], h[:, 2 * b + half]))
                    step(nc.vector.bn_aggr(mv[:, c], stats[:, c]))

            regroup(0)
            regroup(1)
            for q in range(2):
                vec.wait_ge(h_in, q + 1)
                half_moments(0, (2 * q, 2 * q + 1))
            inv_std(mv, 0, B)
            vec.wait_ge(h_in, 3)
            half_moments(1, (0,))
            inv_std(mv, B, 1)

            def normalize(b):
                for half in range(2):
                    t = 2 * b + half
                    m = mv[:, bass.ds(half * B + b, 1), 0]
                    r = rstd[:, bass.ds(half * B + b, 1)]
                    for to, cols in ((slice(0, D), slice(0, D)), (slice(D, DW), slice(P, D))):
                        x = ts(xn[:, half, to], h[:, bass.ds(t, 1), cols].rearrange("p o d -> p (o d)"), m, r, ALU.subtract, ALU.mult)
                x.then_inc(xn_ready, 1)

            def rest_x(b):
                vec.wait_ge(xt_hi_ready, b + 1)
                tt(xt_lo[:].rearrange("p c t -> p (c t)"), bank[:, 6, :], xt_hi[:].rearrange("p c t -> p (c t)").bitcast(F32),
                   ALU.subtract).then_inc(xt_lo_ready, 1)

            def copy_k(b, p):
                vec.wait_ge(proj_done, HEADS * b + 2 * p + 2)
                nc.vector.tensor_copy(kz[0:DH, p % 2, 0], bank[0:DH, 4, 0:TOK])
                nc.vector.tensor_copy(kz[DH:P, p % 2, 1], bank[DH:P, 4, 0:TOK]).then_inc(k_ready, 1)

            def head_max(b, hd):
                vec.wait_ge(scores_done, HEADS * b + hd + 1)
                nc.vector.tensor_reduce(negmax[:, hd % 2], bank[:, hd % 2, :].rearrange("p (h s) -> p h s", h=2), AX.X, ALU.max,
                                        negate=True).then_inc(max_ready, 1)

            def head_norm(b, hd):
                vec.wait_ge(exp_done, HEADS * b + hd + 1)
                step(nc.vector.reciprocal(rinv[:, hd % 2], rowsum[:, hd % 2]))
                for half in range(2):
                    x = ts(prob[:, hd % 2, half], prob[:, hd % 2, half], rinv[:, hd % 2, half:half + 1], None, ALU.mult)
                x.then_inc(norm_done, 1)

            normalize(0)
            rest_x(0)
            vec.wait_ge(h_in, 4)
            half_moments(1, (1,))
            copy_k(0, 0)
            vec.wait_ge(h_in, 5)
            half_moments(1, (2, 3))
            inv_std(mv, B + 1, B - 1)
            copy_k(0, 1)
            head_max(0, 0)
            head_norm(0, 0)

            def earlier_moments():
                for t in range(NT - 2):
                    yield nc.vector.bn_aggr(mv2[:, t], stats2[:, t])
                yield from inv_std_steps(mv2, 0, NT - 2)

            def image(b, last):
                moments = earlier_moments()
                for hd in range(HEADS):
                    if hd < HEADS - 1:
                        head_max(b, hd + 1)
                    elif not last:
                        head_max(b + 1, 0)
                    if hd in (1, 3, 5, 7):
                        copy_k(b, hd // 2 + 2)
                    if hd == 9 and not last:
                        copy_k(b + 1, 0)
                    if hd < HEADS - 1:
                        head_norm(b, hd + 1)
                    elif not last:
                        head_norm(b + 1, 0)
                        copy_k(b + 1, 1)
                    if hd == 5 and not last:
                        vec.wait_ge(xt_done, b + 1)
                        normalize(b + 1)
                    if hd == 7 and not last:
                        rest_x(b + 1)
                    if last:
                        for _, x in zip(range(3), moments):
                            step(x)
                    if hd == 8 and last:
                        vec.wait_ge(proj_done, HEADS * B)
                    if HEADS - 4 <= hd < HEADS - 1 and last:
                        for t in range(2):
                            normalize_2(2 * (hd - (HEADS - 4)) + t)
                    if hd > HEADS - 4 and last:
                        rest_x2(hd - (HEADS - 3))
                for half in range(2):
                    vec.wait_ge(oproj_done, 2 * b + half + 1)
                    ht = h[:, bass.ds(2 * b + half, 1)].rearrange("p o d -> p (o d)")
                    st = stats2[:, bass.ds(2 * b + half, 1)].rearrange("p o d -> p (o d)")
                    tt(ht, bank[:, 7 - half, 0:D], ht, ALU.add).then_inc(resid_done, 1)
                    vec.wait_ge(resid_done, 2 * b + half + 1)
                    step(nc.vector.bn_stats(st, ht))

            def normalize_2(t):
                ts(xs[:, 0, t, 0:D], h[:, t], mv2[:, t, 0:1], rstd[:, t:t + 1], ALU.subtract, ALU.mult)
                ts(xs[:, 0, t, D:DW], h[:, t, P:D], mv2[:, t, 0:1], rstd[:, t:t + 1], ALU.subtract, ALU.mult).then_inc(xn2_ready, 1)

            def rest_x2(q):
                vec.wait_ge(x2_hi_ready, q + 1)
                cols = slice(q * TOK, (q + 1) * TOK)
                tt(x2_lo[:, :, cols], bank[:, X2_BANK[q], :].rearrange("p (c t) -> p c t", c=KC), x2_hi[:, :, cols].bitcast(F32),
                   ALU.subtract).then_inc(x2_lo_ready, 1)

            before = steps[0]
            with vec.Fori(0, B - 1) as b:
                per_image = HEADS + 2
                offset[0] = per_image * b
                image(b, False)
            assert steps[0] - before == per_image
            offset[0] = per_image * (B - 2)
            image(B - 1, True)

            for t in (NT - 2, NT - 1):
                step(nc.vector.bn_aggr(mv2[:, t], stats2[:, t]))
            inv_std(mv2, NT - 2, 2)
            normalize_2(NT - 2)
            normalize_2(NT - 1)

            def wide(x):
                return x.unsqueeze(2).to_broadcast([P, NT, EXPERTS])

            def mul_hidden(n, m, dst, w):
                vec.wait_ge(gate_ready, n + 1)
                tt(dst, gate[:, m % 2, 0:w], bank[:, 5 + 2 * (m % 2), 0:w], ALU.mult).then_inc(hid_ready, 1)

            done = [0]

            def shared_mul():
                n = done[0]
                if n < len(MSTEPS):
                    c, m = MSTEPS[n]
                    mul_hidden(n, m, hs[:, m, c * SHARED_CHUNK:(c + 1) * SHARED_CHUNK], SHARED_CHUNK)
                    done[0] += 1

            shared_mul()
            shared_mul()
            rest_x2(3)
            nc.vector.tensor_copy(xs[:, 0, :, DW + 1].bitcast(I32), token_no[:])
            nc.vector.tensor_copy(xs[:, 1, :, DW + 1].bitcast(I32), token_no[:])
            step(nc.vector.memset(rk[:], 0.0))
            shared_mul()
            m1, s1, r1, i1, p1, p2, i2, tmp = [x[:] for x in sml]
            ls, pr, key, tmp8, score = big[0][:], big[2][:], big[3][:], big[5][:], big[4][:]
            vec.wait_ge(logits_done, 1)
            lg = bank[:, 0, 0:NT * EXPERTS].rearrange("p (t e) -> p t e", t=NT)
            step(nc.vector.tensor_reduce(m1, lg, AX.X, ALU.max))
            tt(ls, lg, wide(m1), ALU.subtract).then_inc(lsh_ready, 1)
            vec.wait_ge(ex_ready, 1)
            ex = big[1][:]
            step(nc.vector.tensor_reduce(s1, ex, AX.X, ALU.add))
            step(nc.vector.reciprocal(r1, s1))
            step(tt(pr, ex, wide(r1), ALU.mult))

            def choose(k, vals, top, idx):
                step(nc.vector.tensor_reduce(top, vals, AX.X, ALU.max))
                step(tt(key, vals, wide(top), ALU.is_lt))
                step(stt(key, key, float(EXPERTS), iota8[:], ALU.mult, ALU.add))
                step(nc.vector.tensor_reduce(idx, key, AX.X, ALU.min))
                step(tt(oh[:, k], iota8[:], wide(idx), ALU.is_equal))

            choose(0, pr, p1, i1)
            shared_mul()
            step(stt(pr, oh[:, 0], -2.0, pr, ALU.mult, ALU.add))
            choose(1, pr, p2, i2)
            shared_mul()
            step(tt(tmp, p1, p2, ALU.add))
            step(ts(tmp, tmp, 1e-9, None, ALU.max))
            step(nc.vector.reciprocal(r1, tmp))
            step(tt(xs[:, 0, :, DW], p1, r1, ALU.mult))
            step(tt(xs[:, 1, :, DW], p2, r1, ALU.mult))
            step(tt(score, oh[:, 0], wide(xs[:, 0, :, DW]), ALU.mult))
            step(tt(key, oh[:, 1], wide(xs[:, 1, :, DW]), ALU.mult))
            step(tt(score, score, key, ALU.add))
            step(tt(tmp8, oh[:, 0], oh[:, 1], ALU.add))
            stt(score, tmp8, -1.0, score, ALU.add, ALU.add).then_inc(topk_ready, 1)
            vec.wait_ge(topk_ready, 1)
            step(ts(base[:, 0], i1, float(CAP), None, ALU.mult))
            step(ts(base[:, 1], i2, float(CAP), None, ALU.mult))
            shared_mul()
            vec.wait_ge(late_zeroed, 3)
            vec.wait_ge(sct_copied, 1)
            tt(sc_lo[0:EXPERTS], bank[0:EXPERTS, 0:2, :].rearrange("p a c -> p (a c)"), sc_hi[0:EXPERTS].bitcast(F32),
               ALU.subtract).then_inc(sc_lo_ready, 1)

            n_group = 0
            for i in range(2 * NT):
                k, t = divmod(i, NT)
                b0 = 2 - 2 * (i % 2)
                rows = bank[:, b0:b0 + 2, :].rearrange("p a c -> p (a c)")
                own = xs[:, k, t, DW:DW + 1]
                vec.wait_ge(rank_rows, i + 1)
                if i > 1:
                    vec.wait_ge(rank_read, i - 1)
                junk = cmp[:, i % 2]
                if t:
                    ts(junk[:, 0:t * P], rows[:, 0:t * P], own, None, ALU.is_ge, ALU.add, rk[:, k, t, 0:1])
                ts(junk[:, t * P:N], rows[:, t * P:N], own, None, ALU.is_gt, ALU.add, rk[:, k, t, 1:2])
                stt(junk[:, N:N + P], rows[:, t * P:(t + 1) * P], own, tri[:], ALU.is_equal, ALU.mult,
                    accum_out=rk[:, k, t, 2:3]).then_inc(rank_read, 1)
                if i % 2 == 1:
                    shared_mul()
                if t % 4 == 3:
                    g = slice(t - 3, t + 1)
                    r, s = s1[:, g], m1[:, g]
                    vec.wait_ge(rank_read, i + 1)
                    step(nc.vector.tensor_reduce(r, rk[:, k, g], AX.X, ALU.add))
                    step(ts(s, r, float(CAP), DROPPED, ALU.is_ge, ALU.mult))
                    step(tt(s, s, r, ALU.add))
                    tt(slot[:, k, g], s, base[:, k, g], ALU.add).then_inc(slot_ready, 1)
                    n_group += 1
                    vec.wait_ge(slot_ready, n_group)
            while done[0] < len(MSTEPS):
                shared_mul()
            for t in range(NT):
                vec.wait_ge(ys_done, t + 1)
                tt(h[:, t], bank[:, t % 4, 0:D], h[:, t], ALU.add).then_inc(ys_read, 1)

            def rest_slots(e, par, added_before=None):
                vec.wait_ge(xd_hi_ready, e + 1)
                if added_before is not None:
                    vec.wait_ge(added[par], added_before)
                nc.vector.tensor_copy(wn[:, par, 0:2], xd[:, par, 0:2, DW:RW])
                nc.vector.tensor_copy(wn[0:CT[2], par, 2], xd[0:CT[2], par, 2, DW:RW])
                tt(xd_lo[:], bank[:, 0:KC, 0:CAP], xd_hi[:].bitcast(F32), ALU.subtract).then_inc(xd_lo_ready, 1)

            def next_lo(e, par, m):
                w = W13 // (FM // 2)
                cols = slice(m // 2 * w, (m // 2 + 1) * w)
                src, dst = raw[:, par].rearrange("p (c n) -> p c n", c=KC), we[:, 1 - par]
                if m == 0:
                    vec.wait_ge(pool_hi, e + 3)
                if m % 2 == 0:
                    tt(dst[:, 2, cols], src[:, 0, cols], dst[:, 0, cols].bitcast(F32), ALU.subtract)
                else:
                    x = tt(dst[TAIL:P, 1, cols], src[TAIL:P, 1, cols], dst[TAIL:P, 1, cols].bitcast(F32), ALU.subtract)
                    if m == FM - 1:
                        x.then_inc(raw_split, 1)

            def expert(e, par, added_before=None, splits=True):
                if not (isinstance(e, int) and e == 0):
                    vec.wait_ge(ye_done, 3 * e)
                for m in range(FM):
                    mul_hidden(len(MSTEPS) + FM * e + m, m, he[:, m], CAP)
                    if splits:
                        next_lo(e, par, m)
                if not (isinstance(e, int) and e == EXPERTS - 1):
                    rest_slots(e + 1, 1 - par, added_before)

            rest_slots(0, 0)
            expert(0, 0, splits=False)
            expert(1, 1, 48)
            with vec.Fori(1, EXPERTS // 2 - 1) as ee:
                expert(2 * ee, 0, 48 * ee)
                expert(2 * ee + 1, 1, 48 * (ee + 1))
            expert(EXPERTS - 2, 0, 48 * (EXPERTS // 2 - 1))
            expert(EXPERTS - 1, 1, splits=False)


def _interp(n_in, n_out):
    pos = (np.arange(n_out, dtype=np.float32) + np.float32(0.5)) * np.float32(n_in / n_out) - np.float32(0.5)
    pos = np.clip(pos, 0.0, n_in - 1).astype(np.float32)
    i0 = np.floor(pos).astype(np.int64)
    i1 = np.minimum(i0 + 1, n_in - 1)
    w = (pos - i0).astype(np.float32)
    m = np.zeros((n_in, n_out), np.float32)
    m[i0, np.arange(n_out)] += np.float32(1.0) - w
    m[i1, np.arange(n_out)] += w
    return m


def _layout(x, W0, b0, W1, b1, W2, b2, Wf, bf, idx0, idx1, idx2, Wqkv, Wout, Wr, w1, w3, w2, s1, s3, s2):
    def patches(p):
        n = 64 // p
        return x.reshape(B, CH, n, p, n, p).transpose(2, 4, 0, 3, 5, 1).reshape(n * n, B * p * p * CH)

    a = {"x0": patches(1)}
    a["x12"] = np.concatenate([patches(2).reshape(P, 8 * B * C1), patches(4).reshape(P, 2 * B * C2)], 1)
    a["idx0"] = idx0.reshape(2, P, GP).transpose(1, 0, 2).reshape(P, 2 * GP)
    a["idx12"] = np.concatenate([idx1.reshape(64, 2, 8).transpose(2, 1, 0).reshape(1, N1),
                                 idx2.reshape(16, 8, 2).transpose(2, 1, 0).reshape(1, N2)], 1)
    place = np.arange(P, dtype=np.float32)[:, None]
    a["patch_no"] = np.concatenate([place * 8 + np.arange(8, dtype=np.float32), place * 2 + np.arange(2, dtype=np.float32)], 1)
    a["w0t"] = W0.T
    a["w1t"] = W1.T.reshape(2, 96, EMB).transpose(1, 0, 2)
    a["w2t"] = W2.T.reshape(8, 96, EMB).transpose(1, 0, 2)
    m1, m2 = _interp(64, TOK), _interp(16, TOK)
    i1 = np.zeros((2, 64, 2, 2, P), np.float32)
    for b in range(2):
        i1[b, :, :, b, :] = m1.reshape(64, 2, P)
    a["i1m"] = i1.reshape(P, 2, 2 * P)
    i2 = np.zeros((B, 16, 2, B, P), np.float32)
    for b in range(B):
        i2[b, :, :, b, :] = m2.reshape(16, 2, P)
    a["i2m"] = i2.reshape(B * 16, 2, B * P)
    bc = np.zeros((P, 2), np.float32)
    bc[0:EMB, 0], bc[EMB:, 0], bc[0:EMB, 1] = b0, b1, b2
    a["bcat"] = bc
    wf = np.zeros((P, 2, D), np.float32)
    wf[:, 0] = Wf.T[0:P]
    wf[0:EMB, 1] = Wf.T[P:D]
    wf[EMB, 1] = bf
    a["wft"] = wf
    rows = np.arange(P * INIT_ROWS).reshape(P, INIT_ROWS)
    a["trash_no"] = (TRASH + rows % CAP).astype(np.int32)
    a["token_no"] = np.arange(N, dtype=np.int32).reshape(NT, P).T
    a["ident"] = np.eye(P, dtype=np.float32)
    a["tri"] = np.tril(np.ones((P, P), np.float32), -1)
    a["iota8"] = np.broadcast_to(np.arange(EXPERTS, dtype=np.float32), (P, NT, EXPERTS))

    def chunks(w):
        tail = np.concatenate([w[..., P:, :], w[..., P:, :]], -2)
        return np.stack([w[..., 0:P, :], tail], -2)

    a["wqkv"] = chunks(Wqkv.T).reshape(P, KC * 3 * INNER)
    a["wo"] = Wout.T.reshape(PAIRS, P, D).transpose(1, 0, 2)
    a["wr"] = chunks(Wr)
    up = np.concatenate([np.concatenate([w1, s1[None]]), np.concatenate([w3, s3[None]])], 2)
    a["w13"] = chunks(up).reshape(EXPERTS + 1, P, KC * W13)
    down = np.concatenate([w2, s2[None]])
    a["w2"] = down.reshape(EXPERTS + 1, FM, P, D).transpose(0, 2, 1, 3)
    return {k: np.ascontiguousarray(v) for k, v in a.items()}


def kernel(x, L0_tok_W0, L0_tok_b0, L0_tok_W1, L0_tok_b1, L0_tok_W2, L0_tok_b2, L0_tok_Wf, L0_tok_bf,
           L0_tok_idx0, L0_tok_idx1, L0_tok_idx2, L0_attn_W_qkv, L0_attn_W_out, L0_ffn_Wr, L0_ffn_w1, L0_ffn_w3,
           L0_ffn_w2, L0_ffn_s1, L0_ffn_s3, L0_ffn_s2):
    import concourse.bacc as _bacc
    from concourse.bass_utils import run_bass_kernel_spmd as _run

    given = (x, L0_tok_W0, L0_tok_b0, L0_tok_W1, L0_tok_b1, L0_tok_W2, L0_tok_b2, L0_tok_Wf, L0_tok_bf,
             L0_tok_idx0, L0_tok_idx1, L0_tok_idx2, L0_attn_W_qkv, L0_attn_W_out, L0_ffn_Wr, L0_ffn_w1, L0_ffn_w3,
             L0_ffn_w2, L0_ffn_s1, L0_ffn_s3, L0_ffn_s2)
    arrays = _layout(*[np.asarray(g) for g in given])
    nc = _bacc.Bacc("TRN2", target_bir_lowering=False, num_devices=1)
    ins = {k: nc.dram_tensor(f"in_{k}", a.shape, mybir.dt.from_np(a.dtype), kind="ExternalInput").ap() for k, a in arrays.items()}
    out = nc.dram_tensor("out_tokens", (N + CAP, D), F32, kind="ExternalOutput").ap()
    vit_tower(nc, ins, out)
    r = _run(nc, [{f"in_{k}": a for k, a in arrays.items()}], core_ids=[0])
    return r.results[0]["out_tokens"][0:N].reshape(B, TOK, D)
```

```python
from contextlib import ExitStack

import numpy as np

import concourse.bass as bass
from concourse import mybir

ALU = mybir.AluOpType
ACT = mybir.ActivationFunctionType
AX = mybir.AxisListType
F32 = mybir.dt.float32
F32R = mybir.dt.float32r
I32 = mybir.dt.int32

P = 128
B = 4
CH = 3
GP = 16
EMB = 64
N1, C1 = 1024, 12
N2, C2 = 256, 48
X12 = 8 * B * C1 + 2 * B * C2
TOK = 256
N = B * TOK
NT = N // P
D = 192
KC = 2
TAIL = D - P
DW = P + 2 * TAIL
PLANES = 3
HEADS = 12
DH = 64
INNER = HEADS * DH
PAIRS = HEADS // 2
AHEAD = PAIRS // 2
LOGIT_GAIN = 8.0
EXPERTS = 8
FF = 768
FM = FF // P
CAP = 320
CT = (P, P, CAP - 2 * P)
SLOTS = EXPERTS * CAP
DROPPED = 8192.0
SHARED_CHUNK = 512
EW = 32 + EXPERTS
RSQRT_START = float(0x5F3759DF)
RW = DW + 2
INIT_ROWS = 5
TRASH = N
LN_EPS = 1e-5
W13 = 2 * FF


def vit_tower(nc, ins, out):
    with ExitStack() as ctx:
        def sem(name):
            return ctx.enter_context(nc.semaphore(name))

        def sb(name, shape, dt=F32, where=ctx):
            return where.enter_context(nc.sbuf_tensor(name, shape, dt))

        slots_in = nc.dram_tensor("slots_in", [SLOTS, RW], F32, kind="Internal").ap()

        bank = ctx.enter_context(nc.psum_tensor("bank", [P, 8, 512], F32))

        ident = sb("ident", [P, P])
        tri = sb("tri", [P, P])
        iota8 = sb("iota8", [P, NT, EXPERTS])
        h = sb("h", [P, NT, D])
        x2_lo = sb("x2_lo", [P, KC, N], F32R)
        raw = sb("raw", [P, 2, KC * W13])
        ws = sb("ws", [P, PLANES, W13], F32R)
        we = sb("we", [P, 2, PLANES, W13], F32R)
        w2s = sb("w2s", [P, FM, D])
        w2e = sb("w2e", [P, 2, FM, D])
        empty = sb("empty", [P, INIT_ROWS, RW])
        token_no = sb("token_no", [P, NT], I32)
        trash_no = sb("trash_no", [P, INIT_ROWS], I32)
        wr_raw = sb("wr_raw", [P, KC, EXPERTS])
        wr = sb("wr", [P, PLANES, EXPERTS], F32R)
        stats = sb("stats", [P, NT, 6])
        mv = sb("mv", [P, NT, 2])
        ve = sb("ve", [P, NT])
        hv = sb("hv", [P, NT])
        rstd = sb("rstd", [P, NT])
        nt1 = sb("nt1", [P, NT])
        stats2 = sb("stats2", [P, NT, 6])
        mv2 = sb("mv2", [P, NT, 2])

        early = ExitStack()
        wq = sb("wq", [P, PLANES, 3 * INNER], F32R, early)
        wo = sb("wo", [P, PAIRS, D], F32, early)
        negmax = sb("negmax", [P, 3, 2], F32, early)
        rowsum = sb("rowsum", [P, 3, 2], F32, early)
        rinv = sb("rinv", [P, 3, 2], F32, early)
        tok = ExitStack()
        idx0 = sb("idx0_s", [P, 2 * GP], I32, tok)
        idx12 = sb("idx12_s", [P, N1 + N2], I32, tok)
        patch_no = sb("patch_no", [P, 8 + 2], F32, tok)
        x12 = sb("x12", [P, X12], F32, tok)
        x12_hi = sb("x12_hi", [P, X12], F32R, tok)
        x12_lo = sb("x12_lo", [P, X12], F32R, tok)
        x2p = sb("x2p", [2 * C2, 2, N2], F32, tok)
        x1p = sb("x1p", [B * C1, N1], F32, tok)
        g0 = sb("g0", [P, 2, GP, B * CH], F32, tok)
        s0 = sb("s0", [P, 2, B, GP * CH], F32, tok)
        s1g = sb("s1g", [P, B, 96], F32, tok)
        s2g = sb("s2g", [P, B, 96], F32, tok)
        w0t = sb("w0t", [GP * CH, EMB], F32, tok)
        w1t = sb("w1t", [96, 2, EMB], F32, tok)
        w2t = sb("w2t", [96, 8, EMB], F32, tok)
        i1m = sb("i1m", [P, 2, 2 * P], F32, tok)
        i2m = sb("i2m", [B * 16, 2, B * P], F32, tok)
        bcat = sb("bcat", [P, 2], F32, tok)
        wft = sb("wft", [P, 2, D], F32, tok)
        x0t = sb("x0t", [GP * CH, 2, B, P], F32, tok)
        x1t = sb("x1t", [96, 2, B, 64], F32, tok)
        x2t = sb("x2t", [96, 8, B, 16], F32, tok)
        o1s = sb("o1s", [P, 2, EMB], F32, tok)
        o2s = sb("o2s", [EMB, EMB], F32, tok)
        cat_a = sb("cat_a", [P, 2, B, P], F32, tok)
        cat_b = sb("cat_b", [EMB + 1, 2, B, P], F32, tok)
        tok.close()
        xn = sb("xn", [P, 2, DW], F32, early)
        xt_hi = sb("xt_hi", [P, KC, TOK], F32R, early)
        xt_lo = sb("xt_lo", [P, KC, TOK], F32R, early)
        qs = sb("qs", [P, AHEAD, 2, TOK], F32R, early)
        ks = sb("ks", [P, AHEAD, 2, 2, TOK], F32R, early)
        q_lo = sb("q_lo", [P, AHEAD, TOK], F32R, early)
        v = sb("v", [P, 2, INNER], F32, early)
        prob = sb("prob", [P, 3, 2, TOK], F32, early)
        prob_t = sb("prob_t", [P, 2, 2, TOK], F32, early)
        ot = sb("ot", [P, PAIRS, TOK], F32, early)
        early.close()

        late = ctx.enter_context(ExitStack())
        xs = sb("xs", [P, 2, NT, RW], F32, late)
        x2_hi = sb("x2_hi", [P, KC, N], F32R, late)
        hs = sb("hs", [P, FM, N], F32, late)
        gate = sb("gate", [P, 2, 512], F32, late)
        rk = sb("rk", [P, 2, NT, 4], F32, late)
        slot = sb("slot", [P, 2, NT], I32, late)
        base = sb("base", [P, 2, NT], F32, late)
        oh = sb("oh", [P, 2, NT, EW], F32, late)
        score = sb("score", [P, NT, EW], F32, late)
        big = [sb(f"rt{i}", [P, NT, EXPERTS], F32, late) for i in range(5)]
        sml = [sb(f"rs{i}", [P, NT], F32, late) for i in range(8)]
        ranking = ExitStack()
        oh_t = sb("oh_t", [P, 2, N], F32R, ranking)
        sc_t = sb("sc_t", [P, N], F32R, ranking)
        cmp = sb("cmp", [P, 2, N + P], F32, ranking)
        ranking.close()
        he = sb("he", [P, FM, CAP], F32, late)
        xd = sb("xd", [P, 2, 3, RW], F32, late)
        wn = sb("wn", [P, 2, 3, 2], F32, late)
        xd_hi = sb("xd_hi", [P, KC, CAP], F32R, late)
        xd_lo = sb("xd_lo", [P, KC, CAP], F32R, late)
        ye = sb("ye", [P, 2, 3, D], F32, late)

        consts_in = sem("consts_in")
        idx_in = sem("idx_in")
        wqkv_in = sem("wqkv_in")
        wo_in = sem("wo_in")
        wr_in = sem("wr_in")
        w2s_in = sem("w2s_in")
        idx12_in, x12_in = sem("idx12_in"), sem("x12_in")
        g0_in = [sem("g0_in_half0"), sem("g0_in_half1")]
        first_raw_in = [sem("first_raw_in_0"), sem("first_raw_in_1")]
        raw_in = [sem("raw_in_0"), sem("raw_in_1")]
        first_w2e_in = sem("first_w2e_in")
        w2e_in = [sem("w2e_in_0"), sem("w2e_in_1")]
        xd_in = [sem("xd_in_0"), sem("xd_in_1")]
        empty_ready = sem("empty_ready")
        slots_empty = sem("slots_empty")
        scattered = sem("scattered")
        out_base = sem("out_base")
        trash_zeroed = sem("trash_zeroed")
        added = [sem("added_0"), sem("added_1")]
        x12_split = sem("x12_split")
        picks = sem("picks")
        picked = sem("picked")
        picked_copied = sem("picked_copied")
        turned = sem("turned")
        grouped = sem("grouped")
        grouped_0 = sem("grouped_0")
        dve = sem("dve_step")
        pe_tok = sem("pe_tok")
        tok_copied = sem("tok_copied")
        fused = sem("fused")
        h_in = sem("h_in")
        wq_split = sem("wq_split")
        xn_ready = sem("xn_ready")
        xt_done = sem("xt_done")
        xt_hi_ready = sem("xt_hi_ready")
        xt_lo_ready = sem("xt_lo_ready")
        proj_done = sem("proj_done")
        q_hi_ready = sem("q_hi_ready")
        k_hi_ready = sem("k_hi_ready")
        q_ready = sem("q_ready")
        k_ready = sem("k_ready")
        q_moved = [sem(f"q_moved_{i}") for i in range(AHEAD)]
        k_moved = [sem(f"k_moved_{i}") for i in range(AHEAD)]
        vproj_done = sem("vproj_done")
        v_ready = sem("v_ready")
        scores_done = sem("scores_done")
        max_ready = sem("max_ready")
        exp_done = sem("exp_done")
        norm_done = sem("norm_done")
        pt_done = sem("pt_done")
        pt_ready = sem("pt_ready")
        pv_done = sem("pv_done")
        o_ready = sem("o_ready")
        oproj_done = sem("oproj_done")
        resid_done = sem("resid_done")
        pool_hi = sem("pool_hi")
        pool_lo = sem("pool_lo")
        reg_waited = sem("reg_waited")
        raw_split = sem("raw_split")
        xn2_ready = sem("xn2_ready")
        xs1_ready = sem("xs1_ready")
        x2t_done = sem("x2t_done")
        x2_hi_ready = sem("x2_hi_ready")
        x2_lo_ready = sem("x2_lo_ready")
        wr_split = sem("wr_split")
        logits_done = sem("logits_done")
        lsh_ready = sem("lsh_ready")
        ex_ready = sem("ex_ready")
        topk_ready = sem("topk_ready")
        late_zeroed = sem("late_zeroed")
        sct_done = sem("sct_done")
        sct_copied = sem("sct_copied")
        sc_lo_ready = sem("sc_lo_ready")
        rank_rows = sem("rank_rows")
        rank_read = sem("rank_read")
        slot_ready = sem("slot_ready")
        gu_done = sem("gu_done")
        gate_ready = sem("gate_ready")
        hid_ready = sem("hid_ready")
        xdt_done = sem("xdt_done")
        xd_hi_ready = sem("xd_hi_ready")
        xd_lo_ready = sem("xd_lo_ready")
        ye_done = sem("ye_done")
        ye_copied = sem("ye_copied")
        ys_done = sem("ys_done")
        ys_read = sem("ys_read")

        onehot = we[:].rearrange("p a c n -> p (a c n)")

        STEPS = ["t2", "o2", "i2_0", "i2_1", "t1", "o1", "t0_0", "a_0", "t0_1a", "a_1a", "t0_1b", "a_1b"]
        STEP = {s: i + 1 for i, s in enumerate(STEPS)}

        FUSED_AT = (((2, 0), (2, 1), (3, 0), (3, 1)), ((6, 0), (1, 0), (3, 0), (3, 1)))

        NPRE = 6
        X2_BANK = (6, 7, 6, 1)
        MSTEPS = [(c, m) for c in range(N // SHARED_CHUNK) for m in range(FM)]
        GROUPS = [(k, g) for k in range(2) for g in range(NT // 4)]

        block = ctx.enter_context(nc.Block())

        @block.sync
        def _(sp):
            sp.dma_start(idx0[:], ins["idx0"]).then_inc(idx_in, 16)
            sp.dma_start(idx12[:], ins["idx12"].broadcast_to((P, N1 + N2))).then_inc(idx12_in, 16)
            sp.dma_start(patch_no[:], ins["patch_no"]).then_inc(idx12_in, 16)
            sp.dma_start(x12[:], ins["x12"]).then_inc(x12_in, 16)
            raw_qkv = raw[:].rearrange("p a c -> p (a c)")[:, 0:KC * 3 * INNER]
            for dst, src in ((ident, "ident"), (w2t, "w2t"), (w1t, "w1t"), (w0t, "w0t"), (i1m, "i1m"), (i2m, "i2m"),
                             (bcat, "bcat"), (wft, "wft"), (tri, "tri"), (iota8, "iota8"), (token_no, "token_no"),
                             (trash_no, "trash_no")):
                sp.dma_start(dst[:], ins[src]).then_inc(consts_in, 16)
            sp.dma_start(wr_raw[:], ins["wr"]).then_inc(wr_in, 16)
            sp.dma_start(raw_qkv, ins["wqkv"]).then_inc(wqkv_in, 16)
            sp.dma_start(wo[:], ins["wo"]).then_inc(wo_in, 16)

            def move_q(b, p):
                at = p % AHEAD
                sp.wait_ge(q_ready, PAIRS * b + p + 1)
                sp.dma_start(qs[DH:P, at, 0].bitcast(F32), q_lo[0:DH, at].bitcast(F32)).then_inc(q_moved[at], 16)
                sp.dma_start(qs[0:DH, at, 1].bitcast(F32), q_lo[DH:P, at].bitcast(F32)).then_inc(q_moved[at], 16)

            def move_k(b, p):
                at = p % AHEAD
                sp.wait_ge(k_ready, PAIRS * b + p + 1)
                sp.dma_start(ks[DH:P, at, 0].bitcast(F32), ks[0:DH, at, 0].bitcast(F32)).then_inc(k_moved[at], 16)
                sp.dma_start(ks[0:DH, at, 1].bitcast(F32), ks[DH:P, at, 1].bitcast(F32)).then_inc(k_moved[at], 16)

            def move(b, pairs):
                for p in pairs:
                    move_q(b, p)
                    move_k(b, p)

            move(0, range(AHEAD))
            with sp.Fori(0, B - 1) as b:
                move(b, range(AHEAD, PAIRS))
                move(b + 1, range(AHEAD))
            move(B - 1, range(AHEAD, PAIRS))

            sp.wait_ge(scattered, 16 * 2 * NT)

            def load_slots(e, par):
                full = slots_in[bass.ds(e * CAP, 2 * P), :].rearrange("(t p) d -> p t d", p=P)
                sp.dma_start(xd[:, par, 0:2, :], full).then_inc(xd_in[par], 16)
                sp.dma_start(xd[0:CT[2], par, 2, :], slots_in[bass.ds(e * CAP + 2 * P, CT[2]), :]).then_inc(xd_in[par], 16)

            def load_up(e, par):
                sp.wait_ge(raw_split, e + 2)
                sp.dma_start(raw[:, 1 - par], ins["w13"][bass.ds(e + 2, 1)].rearrange("o p c -> (o p) c")).then_inc(raw_in[1 - par], 16)

            def load_down(e, par):
                sp.wait_ge(ye_done, 3 * e + 3)
                sp.dma_start(w2e[:, par], ins["w2"][bass.ds(e + 2, 1)].rearrange("o p m d -> (o p) m d")).then_inc(w2e_in[par], 16)

            load_slots(0, 0)
            load_slots(1, 1)
            for t in range(NT):
                sp.wait_ge(ys_read, t + 1)
                sp.dma_start(out[t * P:(t + 1) * P], h[:, t]).then_inc(out_base, 16)
            load_up(0, 0)
            sp.wait_ge(xd_lo_ready, 1)
            load_slots(2, 0)
            load_up(1, 1)
            load_down(0, 0)
            sp.wait_ge(xd_lo_ready, 2)
            load_slots(3, 1)
            with sp.Fori(1, EXPERTS // 2 - 1) as ee:
                for par in range(2):
                    e = 2 * ee + par
                    load_up(e, par)
                    load_down(e - 1, 1 - par)
                    sp.wait_ge(xd_lo_ready, e + 1)
                    load_slots(e + 2, par)
            load_down(EXPERTS - 3, 1)

        @block.gpsimd
        def _(pool):
            nc.gpsimd.memset(empty[:], 0.0).then_inc(empty_ready, 1)
            pool.wait_ge(idx_in, 16)
            for half in range(2):
                for g in range(GP):
                    c = half * GP + g
                    nc.gpsimd.indirect_dma_start(out=g0[:, half, g, :], out_offset=None, in_=ins["x0"],
                                                 in_offset=bass.IndirectOffsetOnAxis(ap=idx0[:, c:c + 1], axis=0)).then_inc(g0_in[half], 16)

            def split(n, dst):
                src = raw[:, n % 2]
                pool.wait_ge(first_raw_in[n % 2], 16 if n < 2 else 16 * (1 + 2 * KC))
                nc.gpsimd.tensor_scalar(dst[:, 0:2].rearrange("p c n -> p (c n)"), src, 1.0, 0.0, ALU.mult, ALU.add).then_inc(pool_hi, 1)
                pool.wait_ge(pool_hi, n + 1)
                nc.gpsimd.tensor_tensor(dst[:, 2], src[:, 0:W13], dst[:, 0].bitcast(F32), ALU.subtract).then_inc(pool_lo, 1)
                pool.wait_ge(pool_lo, n + 1)
                nc.gpsimd.tensor_tensor(dst[TAIL:P, 1], src[TAIL:P, W13:2 * W13], dst[TAIL:P, 1].bitcast(F32), ALU.subtract).then_inc(raw_split, 1)
                pool.wait_ge(raw_split, n + 1)

            pool.wait_ge(g0_in[0], 16 * GP)
            pool.wait_ge(g0_in[1], 16 * GP)
            pool.wait_ge(wq_split, 2)
            nc.gpsimd.dma_start(raw[:, 0], ins["w13"][EXPERTS]).then_inc(first_raw_in[0], 16)
            nc.gpsimd.dma_start(raw[:, 1], ins["w13"][0]).then_inc(first_raw_in[1], 16)
            split(0, ws[:])
            pool.wait_ge(picked, 3)
            split(1, we[:, 0])
            pieces = [(raw[:, 0, q * W13 // 2:(q + 1) * W13 // 2], ins["w13"][1][:, q * W13 // 2:(q + 1) * W13 // 2], first_raw_in[0])
                      for q in range(2 * KC)]
            pieces += [(w2s[:], ins["w2"][EXPERTS], w2s_in)] + [(w2e[:, e], ins["w2"][e], first_w2e_in) for e in range(2)]
            rows = slots_in.rearrange("(q p r) d -> q p (r d)", p=P, r=INIT_ROWS)
            zeros = empty[:].rearrange("p r d -> p (r d)")
            pieces += [(rows[q], zeros, slots_empty) for q in range(SLOTS // (P * INIT_ROWS))]
            pieces += [(out[TRASH:TRASH + CAP].rearrange("(p r) d -> p r d", r=INIT_ROWS), empty[0:CAP // INIT_ROWS, :, 0:D], trash_zeroed)]
            pool.wait_ge(empty_ready, 2)
            for i, (dst, src, landed) in enumerate(pieces):
                pool.wait_ge(norm_done, HEADS + 2 * i)
                nc.gpsimd.dma_start(dst, src).then_inc(landed, 16)
            split(2, we[:, 1])
            pool.wait_ge(resid_done, NT)
            nc.gpsimd.memset(oh[:], 0.0).then_inc(late_zeroed, 1)
            nc.gpsimd.memset(score[:], 0.0).then_inc(late_zeroed, 1)
            nc.gpsimd.memset(sc_t[:].bitcast(F32), 0.0).then_inc(late_zeroed, 1)
            nc.gpsimd.memset(oh_t[:].bitcast(F32), 0.0).then_inc(late_zeroed, 1)
            pool.wait_ge(slots_empty, 16 * SLOTS // (P * INIT_ROWS))
            for i, (k, g) in enumerate(GROUPS):
                pool.wait_ge(slot_ready, i + 1)
                if k == 1 and g == 0:
                    pool.wait_ge(xs1_ready, 1)
                for t in range(4 * g, 4 * g + 4):
                    nc.gpsimd.indirect_dma_start(out=slots_in, out_offset=bass.IndirectOffsetOnAxis(ap=slot[:, k, t:t + 1], axis=0),
                                                 in_=xs[:, k, t, :], in_offset=None, bounds_check=SLOTS - 1,
                                                 oob_is_err=False).then_inc(scattered, 16)

            def add_rows(e, par, before=None):
                if before is not None:
                    pool.wait_ge(added[1 - par], before)
                for s, rows in enumerate(CT):
                    pool.wait_ge(ye_copied, 3 * e + s + 1)
                    pool.sem_inc(reg_waited, 1)
                    nc.gpsimd.indirect_dma_start(out=out, out_offset=bass.IndirectOffsetOnAxis(ap=wn[0:rows, par, s, 1:2].bitcast(I32), axis=0),
                                                 in_=ye[0:rows, par, s, :], in_offset=None,
                                                 compute_op=ALU.add).then_inc(added[par], 16)

            def next_hi(e, par, landed):
                pool.wait_ge(raw_in[1 - par], 16 * landed)
                pool.wait_ge(gu_done, len(MSTEPS) + FM * e + FM)
                pool.sem_inc(reg_waited, 1)
                nc.gpsimd.tensor_scalar(we[:, par, 0:2].rearrange("p c n -> p (c n)"), raw[:, 1 - par], 1.0, 0.0, ALU.mult, ALU.add).then_inc(pool_hi, 1)

            next_hi(0, 0, 1)
            pool.wait_ge(trash_zeroed, 16)
            pool.wait_ge(out_base, 16 * NT)
            add_rows(0, 0)
            next_hi(1, 1, 1)
            add_rows(1, 1, 48)
            with pool.Fori(1, EXPERTS // 2 - 1) as ee:
                next_hi(2 * ee, 0, ee + 1)
                add_rows(2 * ee, 0, 48 * ee)
                next_hi(2 * ee + 1, 1, ee + 1)
                add_rows(2 * ee + 1, 1, 48 * (ee + 1))
            add_rows(EXPERTS - 2, 0, 48 * (EXPERTS // 2 - 1))
            add_rows(EXPERTS - 1, 1, 48 * EXPERTS // 2)
            pool.wait_ge(added[1], 48 * EXPERTS // 2)

        @block.tensor
        def _(pe):
            mm = nc.tensor.matmul

            def product(dst, w, x_hi, x_lo):
                mm(dst, w[:, 2], x_hi[:, 0], start=True, stop=False)
                mm(dst, w[:, 0], x_lo[:, 0], start=False, stop=False)
                mm(dst, w[:, 1], x_lo[:, 1], start=False, stop=False)
                mm(dst, w[:, 1], x_hi[:, 1], start=False, stop=False)
                return mm(dst, w[:, 0], x_hi[:, 0], start=False, stop=True)

            def product_by_token(dst, x_hi, x_lo, w):
                mm(dst, x_hi[:, 0], w[:, 2], start=True, stop=False)
                mm(dst, x_lo[:, 0], w[:, 0], start=False, stop=False)
                mm(dst, x_lo[:, 1], w[:, 1], start=False, stop=False)
                mm(dst, x_hi[:, 1], w[:, 1], start=False, stop=False)
                return mm(dst, x_hi[:, 0], w[:, 0], start=False, stop=True)

            pe.wait_ge(x12_split, 2)
            pe.wait_ge(picks, 1)
            for q in range(2):
                for i, part in enumerate((x12_lo, x12_hi)):
                    for k in range(2):
                        at = 8 * B * C1 + (k * B + 2 * q) * C2
                        t = mm(bank[0:2 * C2, 6, q * N2:(q + 1) * N2], part[:, at:at + 2 * C2], onehot[:, 8 * N1 + k * N2:8 * N1 + (k + 1) * N2],
                               start=(i == 0 and k == 0), stop=(i == 1 and k == 1))
            t.then_inc(picked, 1)
            pe.wait_ge(consts_in, 16 * 12)
            pe.wait_ge(picked_copied, 1)
            for q in range(2):
                for j in range(2):
                    t = nc.tensor.transpose(bank[:, 7, (2 * q + j) * 2 * C2:(2 * q + j + 1) * 2 * C2], x2p[:, q, j * P:(j + 1) * P],
                                            ident[0:2 * C2, 0:2 * C2])
            t.then_inc(turned, 1)
            pe.wait_ge(grouped, 1)
            for b in range(B):
                t = nc.tensor.transpose(bank[0:96, 0, b * P:(b + 1) * P], s2g[:, b], ident[:])
            t.then_inc(pe_tok, 1)
            pe.wait_ge(tok_copied, STEP["t2"])
            for g in range(8):
                t = mm(bank[0:EMB, 2, 0:EMB], x2t[:, g].rearrange("p b t -> p (b t)"), w2t[:, g], start=(g == 0), stop=(g == 7))
            t.then_inc(pe_tok, 1)
            pe.wait_ge(tok_copied, STEP["o2"])
            for half in range(2):
                mm(bank[0:EMB, 6 + half, :], o2s[:], i2m[:, half], start=True, stop=True).then_inc(pe_tok, 1)
            pe.wait_ge(picks, 2)
            for half in range(2):
                for i, part in enumerate((x12_lo, x12_hi)):
                    for k in range(8):
                        t = mm(bank[0:B * C1, 4 + half, :], part[:, k * B * C1:(k + 1) * B * C1],
                               onehot[:, k * N1 + half * 512:k * N1 + (half + 1) * 512], start=(i == 0 and k == 0), stop=(i == 1 and k == 7))
                t.then_inc(picked, 1)
            for half in range(2):
                pe.wait_ge(picked_copied, 2 + half)
                for j in range(4 * half, 4 * half + 4):
                    t = nc.tensor.transpose(bank[:, 0, j * B * C1:(j + 1) * B * C1], x1p[:, j * P:(j + 1) * P], ident[0:B * C1, 0:B * C1])
            t.then_inc(turned, 1)
            pe.wait_ge(grouped, 2)
            for b in range(B):
                t = nc.tensor.transpose(bank[0:96, 1, b * P:(b + 1) * P], s1g[:, b], ident[:])
            t.then_inc(pe_tok, 1)
            pe.wait_ge(tok_copied, STEP["t1"])
            for q in range(2):
                for c in range(2):
                    t = mm(bank[:, 3, q * EMB:(q + 1) * EMB], x1t[:, c, 2 * q:2 * q + 2].rearrange("p b t -> p (b t)"), w1t[:, c],
                           start=(c == 0), stop=(c == 1))
            t.then_inc(pe_tok, 1)
            pe.wait_ge(tok_copied, STEP["o1"])
            for half in range(2):
                for q in range(2):
                    mm(bank[EMB:P, 4 + half, q * TOK:(q + 1) * TOK], o1s[:, q], i1m[:, half], start=True, stop=True)

            def turn_half(half, first, end):
                for b in range(first, end):
                    t = nc.tensor.transpose(bank[0:GP * CH, half, b * P:(b + 1) * P], s0[:, half, b], ident[:])
                t.then_inc(pe_tok, 1)

            def level_0(half, first, end, turned_half):
                pe.wait_ge(tok_copied, STEP[turned_half])
                mm(bank[0:EMB, 4 + half, first * P:end * P], w0t[:], x0t[:, half, first:end].rearrange("p b t -> p (b t)"),
                   start=True, stop=True).then_inc(pe_tok, 1)

            def fuse(half, images):
                for b in images:
                    bk, place = FUSED_AT[half][b]
                    dst = bank[:, bk, place * D:(place + 1) * D]
                    mm(dst, cat_a[:, half, b], wft[:, 0], start=True, stop=False)
                    t = mm(dst, cat_b[:, half, b], wft[0:EMB + 1, 1], start=False, stop=True)
                t.then_inc(fused, 1)

            pe.wait_ge(grouped_0, 1)
            turn_half(0, 0, B)
            level_0(0, 0, B, "t0_0")
            pe.wait_ge(tok_copied, STEP["a_0"])
            fuse(0, (0, 1))
            pe.wait_ge(grouped_0, 2)
            turn_half(1, 0, 1)
            level_0(1, 0, 1, "t0_1a")
            pe.wait_ge(tok_copied, STEP["a_1a"])
            fuse(1, (0,))
            turn_half(1, 1, B)
            fuse(0, (2, 3))
            level_0(1, 1, B, "t0_1b")

            def turn_x(b):
                pe.wait_ge(xn_ready, b + 1)
                for c in range(KC):
                    for half in range(2):
                        t = nc.tensor.transpose(bank[:, 6, c * TOK + half * P:c * TOK + (half + 1) * P],
                                                xn[:, half, c * P:(c + 1) * P], ident[:])
                t.then_inc(xt_done, 1)

            def project(col):
                product(bank[:, 4, 0:TOK], wq[:, :, col:col + P], xt_hi, xt_lo).then_inc(proj_done, 1)

            def project_q(b, p, first=False):
                if not first:
                    pe.wait_ge(k_ready, PAIRS * b + p)
                if p == 0:
                    pe.wait_ge(xt_lo_ready, b + 1)
                project(p * P)

            def project_k(b, p):
                pe.wait_ge(q_ready, PAIRS * b + p + 1)
                project(INNER + p * P)

            def project_v(side, sh, bk):
                cols = slice(2 * INNER + side * (INNER // 2), 2 * INNER + (side + 1) * (INNER // 2))
                rows = slice(sh * P, (sh + 1) * P)
                product_by_token(bank[:, bk, 0:INNER // 2], xt_hi[:, :, rows], xt_lo[:, :, rows], wq[:, :, cols]).then_inc(vproj_done, 1)

            def scores(b, hd):
                u = HEADS * b + hd
                p, at, side = hd // 2, hd // 2 % AHEAD, hd % 2
                if side == 0:
                    pe.wait_ge(q_moved[at], 32 * (2 * b + p // AHEAD + 1))
                    pe.wait_ge(k_moved[at], 32 * (2 * b + p // AHEAD + 1))
                if hd >= 3:
                    pe.wait_ge(exp_done, u - 2)
                for half in range(2):
                    dst = bank[:, hd % 3, half * TOK:(half + 1) * TOK]
                    rows = qs[:, at, side, half * P:(half + 1) * P]
                    mm(dst, rows, ks[:, at, side, 1], start=True, stop=False)
                    t = mm(dst, rows, ks[:, at, side, 0], start=False, stop=True)
                t.then_inc(scores_done, 1)

            def turn_probs(b, hd):
                u = HEADS * b + hd
                pe.wait_ge(norm_done, u + 1)
                if hd:
                    pe.wait_ge(pt_ready, u)
                for sh in range(2):
                    for half in range(2):
                        t = nc.tensor.transpose(bank[:, 3, sh * TOK + half * P:sh * TOK + (half + 1) * P],
                                                prob[:, hd % 3, half, sh * P:(sh + 1) * P], ident[:])
                t.then_inc(pt_done, 1)

            def values(b, hd):
                u = HEADS * b + hd
                pe.wait_ge(pt_ready, u + 1)
                if hd == 0:
                    pe.wait_ge(v_ready, 4 * b + 2)
                if hd == HEADS // 2:
                    pe.wait_ge(v_ready, 4 * b + 4)
                if hd % 2 == 0 and hd:
                    pe.wait_ge(o_ready, PAIRS * b + hd // 2)
                rows = slice(hd % 2 * DH, (hd % 2 + 1) * DH)
                for sh in range(2):
                    t = mm(bank[rows, 5, 0:TOK], v[:, sh, hd * DH:(hd + 1) * DH], prob_t[:, hd % 2, sh],
                           start=(sh == 0), stop=(sh == 1))
                t.then_inc(pv_done, 1)

            def project_out(b, half, bk):
                pe.wait_ge(o_ready, PAIRS * b + PAIRS)
                project_out_part(half, bk, range(PAIRS)).then_inc(oproj_done, 1)

            turn_x(0)
            pe.wait_ge(tok_copied, STEP["a_1b"])
            fuse(1, (1,))
            pe.wait_ge(wq_split, 2)
            project_q(0, 0, first=True)
            project_v(0, 0, 7)
            project_k(0, 0)
            pe.wait_ge(xt_lo_ready, 1)
            project_v(0, 1, 6)
            project_q(0, 1)
            pe.wait_ge(h_in, 3)
            fuse(1, (2, 3))
            project_k(0, 1)
            scores(0, 0)
            project_q(0, 2)
            pe.wait_ge(h_in, 5)
            scores(0, 1)
            pe.wait_ge(wo_in, 16)
            project_k(0, 2)
            scores(0, 2)
            turn_probs(0, 0)

            def image(b, last, first=False):
                for hd in range(HEADS):
                    if 0 < hd < HEADS - 2:
                        scores(b, hd + 2)
                    elif hd and not last:
                        scores(b + 1, hd + 2 - HEADS)
                    if hd < 2 * AHEAD:
                        (project_k if hd % 2 else project_q)(b, AHEAD + hd // 2)
                    elif hd > 2 * AHEAD and not last:
                        (project_q if hd % 2 else project_k)(b + 1, (hd - 2 * AHEAD - 1) // 2)
                    elif hd > HEADS - 4 and last:
                        turn_x2(hd - (HEADS - 3))
                    if hd == 2 * AHEAD - 1 and not last:
                        pe.wait_ge(v_ready, 4 * b + 4)
                        turn_x(b + 1)
                    if hd:
                        turn_probs(b, hd)
                    if hd == 3:
                        pe.wait_ge(v_ready, 4 * b + 1)
                        project_v(1, 0, 7)
                    if hd == 4:
                        pe.wait_ge(v_ready, 4 * b + 2)
                        project_v(1, 1, 6)
                    if hd > 0:
                        values(b, hd - 1)
                    if hd < 2 and not first:
                        pe.wait_ge(v_ready, 4 * b + 1 + hd)
                        project_out(b - 1, hd, 7 - hd)
                    if hd == 9 and not last:
                        project_v(0, 0, 7)
                    if hd == 10 and not last:
                        project_v(0, 1, 6)
                if not last:
                    project_k(b + 1, AHEAD - 1)
                    scores(b + 1, 2)
                    values(b, HEADS - 1)
                    turn_probs(b + 1, 0)
                else:
                    pe.wait_ge(o_ready, PAIRS * B - 1)
                    project_out_part(0, 4, range(PAIRS - 1))
                    values(b, HEADS - 1)
                    pe.wait_ge(x2_lo_ready, 2)
                    project_out_part(1, 7, range(PAIRS - 1))
                    pe.wait_ge(o_ready, PAIRS * B)
                    project_out_part(0, 4, (PAIRS - 1,)).then_inc(oproj_done, 1)
                    project_out_part(1, 7, (PAIRS - 1,)).then_inc(oproj_done, 1)

            def project_out_part(half, bk, pairs):
                for p in pairs:
                    t = mm(bank[:, bk, 0:D], ot[:, p, half * P:(half + 1) * P], wo[:, p], start=(p == 0), stop=(p == PAIRS - 1))
                return t

            def turn_x2(q):
                pe.wait_ge(xn2_ready, 2 * q + 2)
                if q == 0:
                    pe.wait_ge(v_ready, 4 * B)
                if q == 2:
                    pe.wait_ge(x2_lo_ready, 1)
                for c in range(KC):
                    for i in range(2):
                        t = nc.tensor.transpose(bank[:, X2_BANK[q], c * TOK + i * P:c * TOK + (i + 1) * P],
                                                xs[:, 0, 2 * q + i, c * P:(c + 1) * P], ident[:])
                t.then_inc(x2t_done, 1)

            image(0, False, first=True)
            with pe.Fori(1, B - 1) as b:
                image(b, False)
            image(B - 1, True)

            def logits(tiles):
                for t in tiles:
                    rows = slice(t * P, (t + 1) * P)
                    x = product_by_token(bank[:, 0, t * EXPERTS:(t + 1) * EXPERTS], x2_hi[:, :, rows], x2_lo[:, :, rows], wr)
                return x

            def hidden(n, weights, m, x_hi, x_lo, cols, w):
                pair = 4 + 2 * (m % 2)
                if not (isinstance(n, int) and n < 2):
                    pe.wait_ge(hid_ready, n - 1)
                for half in range(2):
                    at = half * FF + m * P
                    t = product(bank[:, pair + half, 0:w], weights[:, :, at:at + P], x_hi[:, :, cols], x_lo[:, :, cols])
                t.then_inc(gu_done, 1)

            def shared_hidden(n):
                c, m = MSTEPS[n]
                hidden(n, ws, m, x2_hi, x2_lo, slice(c * SHARED_CHUNK, (c + 1) * SHARED_CHUNK), SHARED_CHUNK)

            pe.wait_ge(raw_split, 1)
            pe.wait_ge(wr_split, 2)
            pe.wait_ge(x2_lo_ready, 3)
            logits(range(NT - 2))
            pe.wait_ge(resid_done, NT - 1)
            shared_hidden(0)
            pe.wait_ge(resid_done, NT)
            shared_hidden(1)
            turn_x2(3)
            shared_hidden(2)
            pe.wait_ge(x2_lo_ready, 4)
            logits(range(NT - 2, NT)).then_inc(logits_done, 1)
            for n in range(3, NPRE):
                shared_hidden(n)
            pe.wait_ge(topk_ready, 1)
            for src, b0 in ((score, 0), (oh[:, 0], 2)):
                for t in range(NT):
                    x = nc.tensor.transpose(bank[0:EW, b0 + t // 4, t % 4 * P:(t % 4 + 1) * P], src[:, t, :], ident[:])
                x.then_inc(sct_done, 1)
            pe.wait_ge(sc_lo_ready, 1)
            for t in range(NT):
                x = nc.tensor.transpose(bank[0:EW, t // 4, t % 4 * P:(t % 4 + 1) * P], oh[:, 1, t, :], ident[:])
            x.then_inc(sct_done, 1)

            def shared_out(t, bk):
                for m in range(FM):
                    x = mm(bank[:, bk, 0:D], hs[:, m, t * P:(t + 1) * P], w2s[:, m], start=(m == 0), stop=(m == FM - 1))
                x.then_inc(ys_done, 1)

            n = NPRE
            pe.wait_ge(late_zeroed, 4)
            pe.wait_ge(w2s_in, 16)
            for i in range(2 * NT):
                k, t = divmod(i, NT)
                b0 = 2 - 2 * (i % 2)
                if i < 2:
                    pe.wait_ge(sct_copied, 2 + i)
                else:
                    pe.wait_ge(rank_read, i - 1)
                for half in range(2):
                    x = mm(bank[:, b0 + half, :], oh_t[:, k, t * P:(t + 1) * P], sc_t[:, half * 512:(half + 1) * 512],
                           start=True, stop=True)
                x.then_inc(rank_rows, 1)
                if i % 2 == 1 and n < len(MSTEPS):
                    shared_hidden(n)
                    n += 1
                if i >= 2 * NT - NT // 2:
                    q = i - (2 * NT - NT // 2)
                    if q < 2:
                        pe.wait_ge(hid_ready, len(MSTEPS) - 1 + q)
                    else:
                        pe.wait_ge(ys_read, q - 1)
                    shared_out(q, 4 + 2 * (q % 2))
            assert n == len(MSTEPS)

            pe.wait_ge(hid_ready, len(MSTEPS))
            pe.wait_ge(rank_read, 2 * NT)
            for t in range(NT // 2, NT):
                shared_out(t, t % 4)

            def turn_slots(e, par, first=False):
                if first:
                    pe.wait_ge(ys_read, NT)
                else:
                    pe.wait_ge(xd_lo_ready, e)
                pe.wait_ge(xd_in[par], 32 * (e // 2 + 1) if isinstance(e, int) else 32 * (e_pair[0] + 1))
                for c in range(KC):
                    for s, rows in enumerate(CT):
                        t = nc.tensor.transpose(bank[:, c, s * P:s * P + rows], xd[0:rows, par, s, c * P:(c + 1) * P],
                                                ident[0:rows, 0:rows])
                t.then_inc(xdt_done, 1)

            e_pair = [0]

            def expert(e, par, last):
                pe.wait_ge(xd_lo_ready, e + 1)
                pe.wait_ge(raw_split, e + 2)
                for m in range(FM):
                    hidden(len(MSTEPS) + FM * e + m, we[:, par], m, xd_hi, xd_lo, slice(0, CAP), CAP)
                if not last:
                    if par == 1:
                        e_pair[0] = e_pair[0] + 1
                    turn_slots(e + 1, 1 - par)
                if isinstance(e, int) and e < 2:
                    pe.wait_ge(first_w2e_in, 32)
                else:
                    pe.wait_ge(w2e_in[par], 16 * e_pair_now[0])
                pe.wait_ge(hid_ready, len(MSTEPS) + FM * e + FM)
                for s, rows in enumerate(CT):
                    if not (isinstance(e, int) and 3 * e + s < 2):
                        pe.wait_ge(ye_copied, 3 * e + s - 1)
                    for m in range(FM):
                        t = mm(bank[0:rows, 2 + (3 * par + s) % 2, 0:D], he[:, m, s * P:s * P + rows], w2e[:, par, m],
                               start=(m == 0), stop=(m == FM - 1))
                    t.then_inc(ye_done, 1)

            turn_slots(0, 0, first=True)
            e_pair_now = [0]
            expert(0, 0, False)
            expert(1, 1, False)
            with pe.Fori(1, EXPERTS // 2 - 1) as ee:
                e_pair[0] = ee
                e_pair_now[0] = ee
                expert(2 * ee, 0, False)
                expert(2 * ee + 1, 1, False)
            e_pair[0] = e_pair_now[0] = EXPERTS // 2 - 1
            expert(EXPERTS - 2, 0, False)
            expert(EXPERTS - 1, 1, True)

        @block.scalar
        def _(sc):
            fn = nc.scalar.activation

            def copied(step, *ops):
                sc.wait_ge(pe_tok, STEP[step])
                for x in ops:
                    last = x()
                last.then_inc(tok_copied, 1)

            def grouped_rows(dst, src, g):
                return fn(dst.rearrange("p b (g c) -> p g b c", g=g), src.rearrange("p (g b c) -> p g b c", g=g, b=dst.shape[1]), ACT.Copy)

            sc.wait_ge(picked, 1)
            fn(x2p[:].rearrange("p q n -> p (q n)"), bank[0:2 * C2, 6, :], ACT.Copy).then_inc(picked_copied, 1)
            sc.wait_ge(turned, 1)
            for q in range(2):
                x = grouped_rows(s2g[:, 2 * q:2 * q + 2], bank[:, 7, q * 4 * C2:(q + 1) * 4 * C2], 2)
            x.then_inc(grouped, 1)
            copied("t2", lambda: fn(x2t[:].rearrange("p g b t -> p b g t"), bank[0:96, 0, :].rearrange("p (b g t) -> p b g t", b=B, g=8), ACT.Copy))
            copied("o2", lambda: fn(o2s[:], bank[0:EMB, 2, 0:EMB], ACT.Copy))
            sc.wait_ge(consts_in, 16 * 12)
            for half in range(2):
                copied(f"i2_{half}", lambda: fn(cat_b[0:EMB, half].rearrange("p b t -> p (b t)"), bank[0:EMB, 6 + half, :],
                                                ACT.Identity, bias=bcat[0:EMB, 1:2]))
            for half in range(2):
                sc.wait_ge(picked, 2 + half)
                fn(x1p[:, half * 512:(half + 1) * 512], bank[0:B * C1, 4 + half, :], ACT.Copy).then_inc(picked_copied, 1)
            sc.wait_ge(turned, 2)
            grouped_rows(s1g[:], bank[:, 0, 0:8 * B * C1], 8).then_inc(grouped, 1)
            copied("t1", lambda: fn(x1t[:].rearrange("p c b t -> p b c t"), bank[0:96, 1, :].rearrange("p (b c t) -> p b c t", b=B, c=2), ACT.Copy))
            copied("o1", lambda: fn(o1s[:].rearrange("p q e -> p (q e)"), bank[:, 3, 0:2 * EMB], ACT.Copy))

            def copy_half(step, half, first, end):
                copied(step, lambda: fn(x0t[:, half, first:end].rearrange("p b t -> p (b t)"), bank[0:GP * CH, half, first * P:end * P], ACT.Copy))

            def copy_level_0(step, half, first, end):
                copied(step, lambda: fn(cat_a[:, half, first:end].rearrange("p b t -> p (b t)"), bank[:, 4 + half, first * P:end * P],
                                        ACT.Identity, bias=bcat[:, 0:1]))

            def copy_h(n, half, b, images):
                bk, place = FUSED_AT[half][b]
                sc.wait_ge(fused, n)
                fn(h[:].rearrange("p (b i) d -> p i b d", i=2)[:, half, b:b + images],
                   bank[:, bk, place * D:(place + images) * D].rearrange("p (b d) -> p b d", b=images), ACT.Copy).then_inc(h_in, 1)

            copy_half("t0_0", 0, 0, B)
            copy_level_0("a_0", 0, 0, B)
            copy_h(1, 0, 0, 2)
            copy_half("t0_1a", 1, 0, 1)
            copy_level_0("a_1a", 1, 0, 1)
            copy_h(2, 1, 0, 1)
            copy_half("t0_1b", 1, 1, B)
            copy_h(3, 0, 2, 2)
            copy_level_0("a_1b", 1, 1, B)

            def copy_x(b):
                sc.wait_ge(xt_done, b + 1)
                fn(xt_hi[:].rearrange("p c t -> p (c t)"), bank[:, 6, :], ACT.Copy).then_inc(xt_hi_ready, 1)

            def hi_parts(b, p, n, dst, scale, done):
                sc.wait_ge(proj_done, HEADS * b + n)
                if not (isinstance(b, int) and b == 0 and p < AHEAD):
                    sc.wait_ge(scores_done, HEADS * b + 2 * (p - AHEAD) + 2)
                fn(dst[0], bank[0:DH, 4, 0:TOK], ACT.Copy, scale=scale)
                fn(dst[1], bank[DH:P, 4, 0:TOK], ACT.Copy, scale=scale).then_inc(done, 1)

            def copy_q(b, p):
                at = p % AHEAD
                hi_parts(b, p, 2 * p + 1, (qs[0:DH, at, 0], qs[DH:P, at, 1]), LOGIT_GAIN, q_hi_ready)

            def copy_k(b, p):
                at = p % AHEAD
                hi_parts(b, p, 2 * p + 2, (ks[0:DH, at, 0, 0], ks[DH:P, at, 1, 0]), 1.0, k_hi_ready)

            def copy_v(n, side, sh, bk):
                sc.wait_ge(vproj_done, n)
                fn(v[:, sh, side * (INNER // 2):(side + 1) * (INNER // 2)], bank[:, bk, 0:INNER // 2], ACT.Copy).then_inc(v_ready, 1)

            def exps(b, hd):
                sc.wait_ge(max_ready, HEADS * b + hd + 1)
                at = hd % 3
                for half in range(2):
                    last = fn(prob[:, at, half], bank[:, at, half * TOK:(half + 1) * TOK], ACT.Exp,
                              bias=negmax[:, at, half:half + 1], accum_out=rowsum[:, at, half:half + 1])
                last.then_inc(exp_done, 1)

            def copy_probs(b, hd):
                u = HEADS * b + hd
                sc.wait_ge(pt_done, u + 1)
                if hd >= 2:
                    sc.wait_ge(pv_done, u - 1)
                fn(prob_t[:, hd % 2].rearrange("p s t -> p (s t)"), bank[:, 3, :], ACT.Copy).then_inc(pt_ready, 1)

            def copy_o(b, p):
                sc.wait_ge(pv_done, HEADS * b + 2 * p + 2)
                fn(ot[:, p], bank[:, 5, 0:TOK], ACT.Copy).then_inc(o_ready, 1)

            copy_x(0)
            copy_h(4, 1, 1, 1)
            copy_q(0, 0)
            copy_v(1, 0, 0, 7)
            copy_k(0, 0)
            copy_v(2, 0, 1, 6)
            copy_q(0, 1)
            copy_h(5, 1, 2, 2)
            copy_k(0, 1)
            exps(0, 0)
            copy_q(0, 2)
            exps(0, 1)
            copy_k(0, 2)
            exps(0, 2)
            copy_probs(0, 0)

            def image(b, last):
                for hd in range(HEADS):
                    if hd < 2 * AHEAD:
                        (copy_k if hd % 2 else copy_q)(b, AHEAD + hd // 2)
                    elif hd > 2 * AHEAD and not last:
                        (copy_q if hd % 2 else copy_k)(b + 1, (hd - 2 * AHEAD - 1) // 2)
                    if 0 < hd < HEADS - 2:
                        exps(b, hd + 2)
                    elif hd and not last:
                        exps(b + 1, hd + 2 - HEADS)
                    if hd > HEADS - 4 and last:
                        copy_x2(hd - (HEADS - 3))
                    if hd == 2 * AHEAD - 1 and not last:
                        sc.wait_ge(proj_done, HEADS * (b + 1))
                        copy_x(b + 1)
                    if hd:
                        copy_probs(b, hd)
                    if hd == 3:
                        copy_v(4 * b + 3, 1, 0, 7)
                    if hd == 4:
                        copy_v(4 * b + 4, 1, 1, 6)
                    if hd >= 2 and hd % 2 == 0:
                        copy_o(b, hd // 2 - 1)
                    if hd == 9 and not last:
                        sc.wait_ge(pv_done, HEADS * b + HEADS // 2)
                        copy_v(4 * b + 5, 0, 0, 7)
                    if hd == 10 and not last:
                        copy_v(4 * b + 6, 0, 1, 6)
                if not last:
                    copy_k(b + 1, AHEAD - 1)
                copy_o(b, PAIRS - 1)
                if not last:
                    exps(b + 1, 2)
                    copy_probs(b + 1, 0)

            def copy_x2(q):
                sc.wait_ge(x2t_done, q + 1)
                fn(x2_hi[:, :, q * TOK:(q + 1) * TOK], bank[:, X2_BANK[q], :].rearrange("p (c t) -> p c t", c=KC), ACT.Copy).then_inc(x2_hi_ready, 1)

            with sc.Fori(0, B - 1) as b:
                image(b, False)
            image(B - 1, True)

            def silu(n, m, w):
                sc.wait_ge(gu_done, n + 1)
                if not (isinstance(n, int) and n < 2):
                    sc.wait_ge(hid_ready, n - 1)
                fn(gate[:, m % 2, 0:w], bank[:, 4 + 2 * (m % 2), 0:w], ACT.Silu).then_inc(gate_ready, 1)

            for n in range(NPRE):
                silu(n, MSTEPS[n][1], SHARED_CHUNK)
                if n == 1:
                    copy_x2(3)
                    sc.wait_ge(xn2_ready, NT)
                    fn(xs[:, 1, :, 0:DW], xs[:, 0, :, 0:DW], ACT.Copy).then_inc(xs1_ready, 1)
                if n == 2:
                    sc.wait_ge(lsh_ready, 1)
                    fn(big[1][:], big[0][:], ACT.Exp).then_inc(ex_ready, 1)
            sc.wait_ge(late_zeroed, 4)
            sc.wait_ge(sct_done, 1)
            fn(sc_t[0:EW], bank[0:EW, 0:2, :].rearrange("p a c -> p (a c)"), ACT.Copy).then_inc(sct_copied, 1)
            sc.wait_ge(sct_done, 2)
            fn(oh_t[0:EW, 0], bank[0:EW, 2:4, :].rearrange("p a c -> p (a c)"), ACT.Copy).then_inc(sct_copied, 1)
            sc.wait_ge(sct_done, 3)
            fn(oh_t[0:EW, 1], bank[0:EW, 0:2, :].rearrange("p a c -> p (a c)"), ACT.Copy).then_inc(sct_copied, 1)
            for n in range(NPRE, len(MSTEPS)):
                silu(n, MSTEPS[n][1], SHARED_CHUNK)

            def split_slots(e):
                sc.wait_ge(xdt_done, e + 1)
                fn(xd_hi[:], bank[:, 0:KC, 0:CAP], ACT.Copy).then_inc(xd_hi_ready, 1)

            def copy_out(e, par, stored=None):
                if stored is not None:
                    sc.wait_ge(added[par], stored)
                for s, rows in enumerate(CT):
                    sc.wait_ge(ye_done, 3 * e + s + 1)
                    fn(ye[0:rows, par, s], bank[0:rows, 2 + (3 * par + s) % 2, 0:D], ACT.Copy,
                       scale=wn[0:rows, par, s, 0:1]).then_inc(ye_copied, 1)

            def expert(e, par, last, stored=None):
                for m in range(FM):
                    silu(len(MSTEPS) + FM * e + m, m, CAP)
                if not last:
                    split_slots(e + 1)
                copy_out(e, par, stored)

            split_slots(0)
            expert(0, 0, False)
            expert(1, 1, False)
            with sc.Fori(1, EXPERTS // 2 - 1) as ee:
                expert(2 * ee, 0, False, 48 * ee)
                expert(2 * ee + 1, 1, False, 48 * ee)
            expert(EXPERTS - 2, 0, False, 48 * (EXPERTS // 2 - 1))
            expert(EXPERTS - 1, 1, True, 48 * (EXPERTS // 2 - 1))

        @block.vector
        def _(vec):
            ts, tt, stt = nc.vector.tensor_scalar, nc.vector.tensor_tensor, nc.vector.scalar_tensor_tensor
            steps = [0]
            offset = [0]
            chain = []

            def step(x):
                x.then_inc(dve, 1)
                steps[0] += 1
                vec.wait_ge(dve, offset[0] + steps[0])

            vec.wait_ge(x12_in, 16)
            nc.vector.tensor_copy(x12_hi[:], x12[:]).then_inc(x12_split, 1)
            vec.wait_ge(x12_split, 1)
            tt(x12_lo[:], x12[:], x12_hi[:].bitcast(F32), ALU.subtract).then_inc(x12_split, 1)
            vec.wait_ge(idx12_in, 32)
            for k in range(2):
                x = ts(onehot[:, N1 * 8 + k * N2:N1 * 8 + (k + 1) * N2], idx12[:, N1:], patch_no[:, 8 + k:9 + k], None, ALU.is_equal)
            x.then_inc(picks, 1)
            for k in range(8):
                x = ts(onehot[:, k * N1:(k + 1) * N1], idx12[:, 0:N1], patch_no[:, k:k + 1], None, ALU.is_equal)
            x.then_inc(picks, 1)

            nc.vector.memset(cat_b[EMB:EMB + 1].rearrange("p h b t -> p (h b t)"), 1.0)

            def split_lo(src, dst, cols, signal):
                tt(dst[:, 2, cols], src[:, 0, cols], dst[:, 0, cols].bitcast(F32), ALU.subtract)
                tt(dst[TAIL:P, 1, cols], src[TAIL:P, 1, cols], dst[TAIL:P, 1, cols].bitcast(F32), ALU.subtract).then_inc(signal, 1)

            vec.wait_ge(wr_in, 16)
            nc.vector.tensor_copy(wr[:, 0:KC], wr_raw[:]).then_inc(wr_split, 1)
            vec.wait_ge(wr_split, 1)
            split_lo(wr_raw, wr, slice(0, EXPERTS), wr_split)
            vec.wait_ge(empty_ready, 1)
            vec.wait_ge(consts_in, 16 * 12)
            nc.vector.tensor_copy(empty[:, :, DW + 1].bitcast(I32), trash_no[:]).then_inc(empty_ready, 1)
            raw_qkv = raw[:].rearrange("p a c -> p (a c)")[:, 0:KC * 3 * INNER].rearrange("p (c n) -> p c n", c=KC)
            vec.wait_ge(wqkv_in, 16)
            nc.vector.tensor_copy(wq[:, 0:KC], raw_qkv).then_inc(wq_split, 1)
            vec.wait_ge(wq_split, 1)
            split_lo(raw_qkv, wq, slice(0, 3 * INNER), wq_split)

            def regroup(half):
                vec.wait_ge(g0_in[half], 16 * GP)
                nc.vector.tensor_copy(s0[:, half].rearrange("p b (g c) -> p b g c", g=GP),
                                      g0[:, half].rearrange("p g (b c) -> p b g c", b=B)).then_inc(grouped_0, 1)

            def inv_std(m, a, n):
                cols = slice(a, a + n)
                var, y, t, half_v = ve[:, cols], rstd[:, cols], nt1[:, cols], hv[:, cols]
                newton = [lambda: tt(t, y, y, ALU.mult), lambda: tt(t, t, half_v, ALU.mult), lambda: stt(y, t, 1.5, y, ALU.add, ALU.mult)]
                return [lambda: ts(var, m[:, cols, 1], LN_EPS, None, ALU.add),
                        lambda: ts(y.bitcast(I32), var.bitcast(I32), 1, None, ALU.arith_shift_right),
                        lambda: ts(y.bitcast(I32), y.bitcast(I32), -1.0, RSQRT_START, ALU.mult, ALU.add),
                        lambda: ts(half_v, var, -0.5, None, ALU.mult)] + 3 * newton

            def moments_of(t):
                return [lambda: nc.vector.bn_stats(stats[:, t], h[:, t]),
                        lambda: nc.vector.bn_aggr(mv[:, t], stats[:, t])]

            def aggregate(t):
                return lambda: nc.vector.bn_aggr(mv2[:, t], stats2[:, t])

            def settle():
                vec.wait_ge(dve, offset[0] + steps[0])

            def tick(n=1):
                for _ in range(n):
                    if chain:
                        settle()
                        chain.pop(0)().then_inc(dve, 1)
                        steps[0] += 1

            def run(fs):
                for f in fs:
                    step(f())

            regroup(0)
            regroup(1)
            for half in range(2):
                vec.wait_ge(h_in, half + 1)
                run(moments_of(half))
            run(inv_std(mv, 0, 2))

            def normalize(b):
                for half in range(2):
                    t = 2 * b + half
                    m = mv[:, bass.ds(t, 1), 0]
                    r = rstd[:, bass.ds(t, 1)]
                    for to, cols in ((slice(0, D), slice(0, D)), (slice(D, DW), slice(P, D))):
                        x = ts(xn[:, half, to], h[:, bass.ds(t, 1), cols].rearrange("p o d -> p (o d)"), m, r, ALU.subtract, ALU.mult)
                x.then_inc(xn_ready, 1)

            def rest_x(b):
                vec.wait_ge(xt_hi_ready, b + 1)
                tt(xt_lo[:].rearrange("p c t -> p (c t)"), bank[:, 6, :], xt_hi[:].rearrange("p c t -> p (c t)").bitcast(F32),
                   ALU.subtract).then_inc(xt_lo_ready, 1)

            def rest_q(b, p):
                at = p % AHEAD
                vec.wait_ge(q_hi_ready, PAIRS * b + p + 1)
                for side, rows in enumerate((slice(0, DH), slice(DH, P))):
                    x = stt(q_lo[rows, at], bank[rows, 4, 0:TOK], LOGIT_GAIN, qs[rows, at, side].bitcast(F32), ALU.mult, ALU.subtract)
                x.then_inc(q_ready, 1)

            def rest_k(b, p):
                at = p % AHEAD
                vec.wait_ge(k_hi_ready, PAIRS * b + p + 1)
                for side, rows in enumerate((slice(0, DH), slice(DH, P))):
                    x = tt(ks[rows, at, side, 1], bank[rows, 4, 0:TOK], ks[rows, at, side, 0].bitcast(F32), ALU.subtract)
                x.then_inc(k_ready, 1)

            def head_max(b, hd):
                vec.wait_ge(scores_done, HEADS * b + hd + 1)
                nc.vector.tensor_reduce(negmax[:, hd % 3], bank[:, hd % 3, :].rearrange("p (h s) -> p h s", h=2), AX.X, ALU.max,
                                        negate=True).then_inc(max_ready, 1)

            def head_norm(b, hd):
                vec.wait_ge(exp_done, HEADS * b + hd + 1)
                at = hd % 3
                step(nc.vector.reciprocal(rinv[:, at], rowsum[:, at]))
                for half in range(2):
                    x = ts(prob[:, at, half], prob[:, at, half], rinv[:, at, half:half + 1], None, ALU.mult)
                x.then_inc(norm_done, 1)

            normalize(0)
            rest_x(0)
            rest_q(0, 0)
            rest_k(0, 0)
            rest_q(0, 1)
            rest_k(0, 1)
            head_max(0, 0)
            rest_q(0, 2)
            head_max(0, 1)
            head_norm(0, 0)
            rest_k(0, 2)
            head_max(0, 2)
            head_norm(0, 1)

            def add_heads(b, half, bk):
                vec.wait_ge(oproj_done, 2 * b + half + 1)
                ht = h[:, bass.ds(2 * b + half, 1)].rearrange("p o d -> p (o d)")
                st = stats2[:, bass.ds(2 * b + half, 1)].rearrange("p o d -> p (o d)")
                tt(ht, bank[:, bk, 0:D], ht, ALU.add).then_inc(resid_done, 1)
                vec.wait_ge(resid_done, 2 * b + half + 1)
                step(nc.vector.bn_stats(st, ht))

            def image(b, last, first=False):
                if first:
                    vec.wait_ge(h_in, 5)
                    for t in (2, 3):
                        chain.extend(moments_of(t))
                    chain.extend(inv_std(mv, 2, 2))
                    others = [f for t in range(4, NT) for f in moments_of(t)] + inv_std(mv, 4, NT - 4)
                for hd in range(HEADS):
                    if 0 < hd < HEADS - 2:
                        head_max(b, hd + 2)
                    elif hd and not last:
                        head_max(b + 1, hd + 2 - HEADS)
                    tick(2)
                    if 0 < hd < HEADS - 1:
                        head_norm(b, hd + 1)
                    elif hd and not last:
                        head_norm(b + 1, 0)
                    tick(1)
                    if hd < 2 * AHEAD:
                        (rest_k if hd % 2 else rest_q)(b, AHEAD + hd // 2)
                    elif hd > 2 * AHEAD and not last:
                        (rest_q if hd % 2 else rest_k)(b + 1, (hd - 2 * AHEAD - 1) // 2)
                    tick(3 if hd < 3 else last)
                    if hd in (1, 2) and not first:
                        add_heads(b - 1, hd - 1, 8 - hd)
                    if hd == 2 and last:
                        chain.extend(aggregate(t) for t in range(NT - 2))
                        chain.extend(inv_std(mv2, 0, NT - 2))
                    if hd == 3 and not last:
                        if first:
                            assert not chain
                            settle()
                            chain.extend(others)
                        vec.wait_ge(xt_done, b + 1)
                        normalize(b + 1)
                    if hd == 2 * AHEAD - 1 and not last:
                        rest_x(b + 1)
                    if hd == 8 and last:
                        assert not chain
                        settle()
                        vec.wait_ge(proj_done, HEADS * B)
                    if HEADS - 4 <= hd < HEADS - 1 and last:
                        for t in range(2):
                            normalize_2(2 * (hd - (HEADS - 4)) + t)
                    if hd > HEADS - 4 and last:
                        rest_x2(hd - (HEADS - 3))
                if first:
                    assert not chain
                    settle()
                if not last:
                    rest_k(b + 1, AHEAD - 1)
                    head_max(b + 1, 2)
                    head_norm(b + 1, 1)
                else:
                    add_heads(b, 0, 4)
                    add_heads(b, 1, 7)

            def normalize_2(t):
                ts(xs[:, 0, t, 0:D], h[:, t], mv2[:, t, 0:1], rstd[:, t:t + 1], ALU.subtract, ALU.mult)
                ts(xs[:, 0, t, D:DW], h[:, t, P:D], mv2[:, t, 0:1], rstd[:, t:t + 1], ALU.subtract, ALU.mult).then_inc(xn2_ready, 1)

            def rest_x2(q):
                vec.wait_ge(x2_hi_ready, q + 1)
                cols = slice(q * TOK, (q + 1) * TOK)
                tt(x2_lo[:, :, cols], bank[:, X2_BANK[q], :].rearrange("p (c t) -> p c t", c=KC), x2_hi[:, :, cols].bitcast(F32),
                   ALU.subtract).then_inc(x2_lo_ready, 1)

            image(0, False, first=True)
            before = steps[0]
            per_image = HEADS + 2
            with vec.Fori(1, B - 1) as b:
                offset[0] = per_image * (b - 1)
                image(b, False)
            assert steps[0] - before == per_image
            offset[0] = per_image * (B - 3)
            image(B - 1, True)

            for t in (NT - 2, NT - 1):
                step(nc.vector.bn_aggr(mv2[:, t], stats2[:, t]))
            run(inv_std(mv2, NT - 2, 2))
            normalize_2(NT - 2)
            normalize_2(NT - 1)

            def wide(x):
                return x.unsqueeze(2).to_broadcast([P, NT, EXPERTS])

            def mul_hidden(n, m, dst, w):
                vec.wait_ge(gate_ready, n + 1)
                tt(dst, gate[:, m % 2, 0:w], bank[:, 5 + 2 * (m % 2), 0:w], ALU.mult).then_inc(hid_ready, 1)

            done = [0]

            def shared_mul():
                n = done[0]
                if n < len(MSTEPS):
                    c, m = MSTEPS[n]
                    mul_hidden(n, m, hs[:, m, c * SHARED_CHUNK:(c + 1) * SHARED_CHUNK], SHARED_CHUNK)
                    done[0] += 1

            shared_mul()
            shared_mul()
            rest_x2(3)
            nc.vector.tensor_copy(xs[:, 0, :, DW + 1].bitcast(I32), token_no[:])
            nc.vector.tensor_copy(xs[:, 1, :, DW + 1].bitcast(I32), token_no[:])
            step(nc.vector.memset(rk[:], 0.0))
            shared_mul()
            m1, s1, r1, i1, p1, p2, i2, tmp = [x[:] for x in sml]
            ls, pr, key, tmp8 = big[0][:], big[2][:], big[3][:], big[4][:]
            chosen = [oh[:, k, :, 0:EXPERTS] for k in range(2)]
            vec.wait_ge(logits_done, 1)
            lg = bank[:, 0, 0:NT * EXPERTS].rearrange("p (t e) -> p t e", t=NT)
            step(nc.vector.tensor_reduce(m1, lg, AX.X, ALU.max))
            tt(ls, lg, wide(m1), ALU.subtract).then_inc(lsh_ready, 1)
            vec.wait_ge(ex_ready, 1)
            ex = big[1][:]
            step(nc.vector.tensor_reduce(s1, ex, AX.X, ALU.add))
            step(nc.vector.reciprocal(r1, s1))
            step(tt(pr, ex, wide(r1), ALU.mult))

            def choose(k, vals, top, idx):
                step(nc.vector.tensor_reduce(top, vals, AX.X, ALU.max))
                step(tt(key, vals, wide(top), ALU.is_lt))
                step(stt(key, key, float(EXPERTS), iota8[:], ALU.mult, ALU.add))
                step(nc.vector.tensor_reduce(idx, key, AX.X, ALU.min))
                tt(oh[:, k, :, 32:EW], iota8[:], wide(idx), ALU.is_equal)
                step(tt(chosen[k], iota8[:], wide(idx), ALU.is_equal))

            vec.wait_ge(late_zeroed, 2)
            choose(0, pr, p1, i1)
            shared_mul()
            step(stt(pr, chosen[0], -2.0, pr, ALU.mult, ALU.add))
            choose(1, pr, p2, i2)
            shared_mul()
            step(tt(tmp, p1, p2, ALU.add))
            step(ts(tmp, tmp, 1e-9, None, ALU.max))
            step(nc.vector.reciprocal(r1, tmp))
            step(tt(xs[:, 0, :, DW], p1, r1, ALU.mult))
            step(tt(xs[:, 1, :, DW], p2, r1, ALU.mult))
            step(tt(ls, chosen[0], wide(xs[:, 0, :, DW]), ALU.mult))
            step(tt(key, chosen[1], wide(xs[:, 1, :, DW]), ALU.mult))
            step(tt(ls, ls, key, ALU.add))
            step(tt(tmp8, chosen[0], chosen[1], ALU.add))
            stt(score[:, :, 32:EW], tmp8, -1.0, ls, ALU.add, ALU.add)
            stt(score[:, :, 0:EXPERTS], tmp8, -1.0, ls, ALU.add, ALU.add).then_inc(topk_ready, 1)
            vec.wait_ge(topk_ready, 1)
            step(ts(base[:, 0], i1, float(CAP), None, ALU.mult))
            step(ts(base[:, 1], i2, float(CAP), None, ALU.mult))
            shared_mul()
            vec.wait_ge(sct_copied, 1)
            tt(sc_t[32:EW], bank[32:EW, 0:2, :].rearrange("p a c -> p (a c)"), sc_t[32:EW].bitcast(F32),
               ALU.subtract).then_inc(sc_lo_ready, 1)

            def add_shared(t, bk):
                vec.wait_ge(ys_done, t + 1)
                tt(h[:, t], bank[:, bk, 0:D], h[:, t], ALU.add).then_inc(ys_read, 1)

            n_group = 0
            for i in range(2 * NT):
                k, t = divmod(i, NT)
                b0 = 2 - 2 * (i % 2)
                rows = bank[:, b0:b0 + 2, :].rearrange("p a c -> p (a c)")
                own = xs[:, k, t, DW:DW + 1]
                vec.wait_ge(rank_rows, i + 1)
                if i > 1:
                    vec.wait_ge(rank_read, i - 1)
                junk = cmp[:, i % 2]
                if t:
                    ts(junk[:, 0:t * P], rows[:, 0:t * P], own, None, ALU.is_ge, ALU.add, rk[:, k, t, 0:1])
                ts(junk[:, t * P:N], rows[:, t * P:N], own, None, ALU.is_gt, ALU.add, rk[:, k, t, 1:2])
                stt(junk[:, N:N + P], rows[:, t * P:(t + 1) * P], own, tri[:], ALU.is_equal, ALU.mult,
                    accum_out=rk[:, k, t, 2:3]).then_inc(rank_read, 1)
                if i % 2 == 1:
                    shared_mul()
                if i >= 2 * NT - NT // 2:
                    q = i - (2 * NT - NT // 2)
                    add_shared(q, 4 + 2 * (q % 2))
                if t % 4 == 3:
                    g = slice(t - 3, t + 1)
                    r, s = s1[:, g], m1[:, g]
                    vec.wait_ge(rank_read, i + 1)
                    step(nc.vector.tensor_reduce(r, rk[:, k, g], AX.X, ALU.add))
                    step(ts(s, r, float(CAP), DROPPED, ALU.is_ge, ALU.mult))
                    step(tt(s, s, r, ALU.add))
                    tt(slot[:, k, g], s, base[:, k, g], ALU.add).then_inc(slot_ready, 1)
                    n_group += 1
                    vec.wait_ge(slot_ready, n_group)
            assert done[0] == len(MSTEPS)
            for t in range(NT // 2, NT):
                add_shared(t, t % 4)

            def rest_slots(e, par, added_before=None):
                vec.wait_ge(xd_hi_ready, e + 1)
                if added_before is not None:
                    vec.wait_ge(added[par], added_before)
                nc.vector.tensor_copy(wn[:, par, 0:2], xd[:, par, 0:2, DW:RW])
                nc.vector.tensor_copy(wn[0:CT[2], par, 2], xd[0:CT[2], par, 2, DW:RW])
                tt(xd_lo[:], bank[:, 0:KC, 0:CAP], xd_hi[:].bitcast(F32), ALU.subtract).then_inc(xd_lo_ready, 1)

            def next_lo(e, par, m):
                w = W13 // (FM // 2)
                cols = slice(m // 2 * w, (m // 2 + 1) * w)
                src, dst = raw[:, par].rearrange("p (c n) -> p c n", c=KC), we[:, 1 - par]
                if m == 0:
                    vec.wait_ge(pool_hi, e + 3)
                if m % 2 == 0:
                    tt(dst[:, 2, cols], src[:, 0, cols], dst[:, 0, cols].bitcast(F32), ALU.subtract)
                else:
                    x = tt(dst[TAIL:P, 1, cols], src[TAIL:P, 1, cols], dst[TAIL:P, 1, cols].bitcast(F32), ALU.subtract)
                    if m == FM - 1:
                        x.then_inc(raw_split, 1)

            def expert(e, par, added_before=None, splits=True):
                if not (isinstance(e, int) and e == 0):
                    vec.wait_ge(ye_done, 3 * e)
                for m in range(FM):
                    mul_hidden(len(MSTEPS) + FM * e + m, m, he[:, m], CAP)
                    if splits:
                        next_lo(e, par, m)
                if not (isinstance(e, int) and e == EXPERTS - 1):
                    rest_slots(e + 1, 1 - par, added_before)

            rest_slots(0, 0)
            expert(0, 0, splits=False)
            expert(1, 1, 48)
            with vec.Fori(1, EXPERTS // 2 - 1) as ee:
                expert(2 * ee, 0, 48 * ee)
                expert(2 * ee + 1, 1, 48 * (ee + 1))
            expert(EXPERTS - 2, 0, 48 * (EXPERTS // 2 - 1))
            expert(EXPERTS - 1, 1, splits=False)


def _interp(n_in, n_out):
    pos = (np.arange(n_out, dtype=np.float32) + np.float32(0.5)) * np.float32(n_in / n_out) - np.float32(0.5)
    pos = np.clip(pos, 0.0, n_in - 1).astype(np.float32)
    i0 = np.floor(pos).astype(np.int64)
    i1 = np.minimum(i0 + 1, n_in - 1)
    w = (pos - i0).astype(np.float32)
    m = np.zeros((n_in, n_out), np.float32)
    m[i0, np.arange(n_out)] += np.float32(1.0) - w
    m[i1, np.arange(n_out)] += w
    return m


def _layout(x, W0, b0, W1, b1, W2, b2, Wf, bf, idx0, idx1, idx2, Wqkv, Wout, Wr, w1, w3, w2, s1, s3, s2):
    def patches(p):
        n = 64 // p
        return x.reshape(B, CH, n, p, n, p).transpose(2, 4, 0, 3, 5, 1).reshape(n * n, B * p * p * CH)

    a = {"x0": patches(1)}
    a["x12"] = np.concatenate([patches(2).reshape(P, 8 * B * C1), patches(4).reshape(P, 2 * B * C2)], 1)
    a["idx0"] = idx0.reshape(2, P, GP).transpose(1, 0, 2).reshape(P, 2 * GP)
    a["idx12"] = np.concatenate([idx1.reshape(64, 2, 8).transpose(2, 1, 0).reshape(1, N1),
                                 idx2.reshape(16, 8, 2).transpose(2, 1, 0).reshape(1, N2)], 1)
    place = np.arange(P, dtype=np.float32)[:, None]
    a["patch_no"] = np.concatenate([place * 8 + np.arange(8, dtype=np.float32), place * 2 + np.arange(2, dtype=np.float32)], 1)
    a["w0t"] = W0.T
    a["w1t"] = W1.T.reshape(2, 96, EMB).transpose(1, 0, 2)
    a["w2t"] = W2.T.reshape(8, 96, EMB).transpose(1, 0, 2)
    m1, m2 = _interp(64, TOK), _interp(16, TOK)
    i1 = np.zeros((2, 64, 2, 2, P), np.float32)
    for b in range(2):
        i1[b, :, :, b, :] = m1.reshape(64, 2, P)
    a["i1m"] = i1.reshape(P, 2, 2 * P)
    i2 = np.zeros((B, 16, 2, B, P), np.float32)
    for b in range(B):
        i2[b, :, :, b, :] = m2.reshape(16, 2, P)
    a["i2m"] = i2.reshape(B * 16, 2, B * P)
    bc = np.zeros((P, 2), np.float32)
    bc[0:EMB, 0], bc[EMB:, 0], bc[0:EMB, 1] = b0, b1, b2
    a["bcat"] = bc
    wf = np.zeros((P, 2, D), np.float32)
    wf[:, 0] = Wf.T[0:P]
    wf[0:EMB, 1] = Wf.T[P:D]
    wf[EMB, 1] = bf
    a["wft"] = wf
    rows = np.arange(P * INIT_ROWS).reshape(P, INIT_ROWS)
    a["trash_no"] = (TRASH + rows % CAP).astype(np.int32)
    a["token_no"] = np.arange(N, dtype=np.int32).reshape(NT, P).T
    a["ident"] = np.eye(P, dtype=np.float32)
    a["tri"] = np.tril(np.ones((P, P), np.float32), -1)
    a["iota8"] = np.broadcast_to(np.arange(EXPERTS, dtype=np.float32), (P, NT, EXPERTS))

    def chunks(w):
        tail = np.concatenate([w[..., P:, :], w[..., P:, :]], -2)
        return np.stack([w[..., 0:P, :], tail], -2)

    a["wqkv"] = chunks(Wqkv.T).reshape(P, KC * 3 * INNER)
    a["wo"] = Wout.T.reshape(PAIRS, P, D).transpose(1, 0, 2)
    a["wr"] = chunks(Wr)
    up = np.concatenate([np.concatenate([w1, s1[None]]), np.concatenate([w3, s3[None]])], 2)
    a["w13"] = chunks(up).reshape(EXPERTS + 1, P, KC * W13)
    down = np.concatenate([w2, s2[None]])
    a["w2"] = down.reshape(EXPERTS + 1, FM, P, D).transpose(0, 2, 1, 3)
    return {k: np.ascontiguousarray(v) for k, v in a.items()}


def kernel(x, L0_tok_W0, L0_tok_b0, L0_tok_W1, L0_tok_b1, L0_tok_W2, L0_tok_b2, L0_tok_Wf, L0_tok_bf,
           L0_tok_idx0, L0_tok_idx1, L0_tok_idx2, L0_attn_W_qkv, L0_attn_W_out, L0_ffn_Wr, L0_ffn_w1, L0_ffn_w3,
           L0_ffn_w2, L0_ffn_s1, L0_ffn_s3, L0_ffn_s2):
    import concourse.bacc as _bacc
    from concourse.bass_utils import run_bass_kernel_spmd as _run

    given = (x, L0_tok_W0, L0_tok_b0, L0_tok_W1, L0_tok_b1, L0_tok_W2, L0_tok_b2, L0_tok_Wf, L0_tok_bf,
             L0_tok_idx0, L0_tok_idx1, L0_tok_idx2, L0_attn_W_qkv, L0_attn_W_out, L0_ffn_Wr, L0_ffn_w1, L0_ffn_w3,
             L0_ffn_w2, L0_ffn_s1, L0_ffn_s3, L0_ffn_s2)
    arrays = _layout(*[np.asarray(g) for g in given])
    nc = _bacc.Bacc("TRN2", target_bir_lowering=False, num_devices=1)
    ins = {k: nc.dram_tensor(f"in_{k}", a.shape, mybir.dt.from_np(a.dtype), kind="ExternalInput").ap() for k, a in arrays.items()}
    out = nc.dram_tensor("out_tokens", (N + CAP, D), F32, kind="ExternalOutput").ap()
    vit_tower(nc, ins, out)
    r = _run(nc, [{f"in_{k}": a for k, a in arrays.items()}], core_ids=[0])
    return r.results[0]["out_tokens"][0:N].reshape(B, TOK, D)
```
